# Optimizing a Trainium2 kernel written in Bass

```python
import numpy as np
import jax
import jax.numpy as jnp

def _softmax(x, axis=-1):
    return jax.nn.softmax(x, axis=axis)

def _gelu(x):
    return jax.nn.gelu(x, approximate=True)

def _silu(x):
    return jax.nn.silu(x)

def _sigmoid(x):
    return jax.nn.sigmoid(x)

def _layernorm(x, axis=-1, eps=1e-05):
    m = jnp.mean(x, axis=axis, keepdims=True)
    v = jnp.var(x, axis=axis, keepdims=True)
    return (x - m) / jnp.sqrt(v + eps)

def _scatter_add(tgt, idx, src, axis=0):
    return tgt.at[idx].add(src)

def _segment_sum(src, seg, n):
    return jax.ops.segment_sum(src, seg, n)
kernel_name = 'mk_gps_d1_gnn_r32_9f9d51'

def setup_inputs(seed: int=0):
    np.random.seed(seed)
    _w = jnp.asarray

    def _rec_inputs():
        import jax
        import jax.numpy as jnp
        _gk = jax.random.key(seed)
        x = -6.415e-05 + 1 * jax.random.normal(jax.random.fold_in(_gk, 1), (625, 512), jnp.float32)
        src = jax.random.randint(jax.random.fold_in(_gk, 2), (10000,), 0, 625, jnp.int32)
        dst = jax.random.randint(jax.random.fold_in(_gk, 3), (10000,), 0, 625, jnp.int32)
        _o = jnp.argsort(dst, stable=True)
        src = src[_o]
        dst = dst[_o]
        edge_attr_8 = -0.000521468 + 0.999954 * jax.random.normal(jax.random.fold_in(_gk, 12), (10000, 8), jnp.float32)
        edge_attr_8_n2 = -0.000521468 + 0.999954 * jax.random.normal(jax.random.fold_in(_gk, 13), (10000, 8), jnp.float32)
        return (x, src, dst, edge_attr_8, edge_attr_8_n2)
    x, src, dst, edge_attr_8, edge_attr_8_n2 = _rec_inputs()

    def _L0_gnn_setup():
        import jax, jax.numpy as jnp
        import numpy as np
        N = 625
        E = 20000
        D = 512
        H = 8
        DH = D // H
        EPS = 1e-05

        def layer_norm(x, g, b):
            mu = x.mean(-1, keepdims=True)
            var = ((x - mu) ** 2).mean(-1, keepdims=True)
            return (x - mu) * jax.lax.rsqrt(var + EPS) * g + b
        key = jax.random.key(seed)
        ks = jax.random.split(key, 12)
        return dict(node_feature=jax.random.normal(ks[0], (N, D), jnp.float32), src=jax.random.randint(ks[1], (E,), 0, N, dtype=jnp.int32), dst=jax.random.randint(ks[2], (E,), 0, N, dtype=jnp.int32), dist_attn=jax.random.normal(ks[3], (E, H), jnp.float32), path_attn=jax.random.normal(ks[4], (E, H), jnp.float32), Wqkv=jax.random.normal(ks[5], (D, 3 * D), jnp.float32) / np.float32(np.sqrt(D)), bqkv=jnp.zeros((3 * D,), jnp.float32), Wo=jax.random.normal(ks[6], (D, D), jnp.float32) / np.float32(np.sqrt(D)), bo=jnp.zeros((D,), jnp.float32), ln1_g=jnp.ones((D,), jnp.float32), ln1_b=jnp.zeros((D,), jnp.float32), W1=jax.random.normal(ks[7], (D, 4 * D), jnp.float32) / np.float32(np.sqrt(D)), b1=jnp.zeros((4 * D,), jnp.float32), W2=jax.random.normal(ks[8], (4 * D, D), jnp.float32) / np.float32(np.sqrt(4 * D)), b2=jnp.zeros((D,), jnp.float32), ln2_g=jnp.ones((D,), jnp.float32), ln2_b=jnp.zeros((D,), jnp.float32))
    _L0_gnn_all = _L0_gnn_setup()
    _L0_gnn_in = {k: v for k, v in _L0_gnn_all.items() if k in ('Wqkv', 'bqkv', 'Wo', 'bo', 'ln1_g', 'ln1_b', 'W1', 'b1', 'W2', 'b2', 'ln2_g', 'ln2_b')}
    del _L0_gnn_all

    def _L0_mix_setup():
        import jax, jax.numpy as jnp
        import numpy as np
        DEPTH, DIM, HEADS, DIM_HEAD, NBF, MULT = (2, 512, 8, 64, 256, 4)
        INNER = HEADS * DIM_HEAD

        def layernorm(x, g, b, eps=1e-05):
            mu = jnp.mean(x, axis=-1, keepdims=True)
            var = jnp.mean((x - mu) ** 2, axis=-1, keepdims=True)
            return (x - mu) * jax.lax.rsqrt(var + eps) * g + b

        def softmax_kernel(data, proj, is_query, eps=0.0001):
            d = data.shape[-1]
            normalizer = d ** (-0.25)
            ratio = proj.shape[0] ** (-0.5)
            data_dash = jnp.einsum('bhnd,md->bhnm', data * normalizer, proj)
            diag = jnp.sum(data ** 2, axis=-1, keepdims=True) * 0.5 * normalizer ** 2
            if is_query:
                m = jnp.max(data_dash, axis=-1, keepdims=True)
            else:
                m = jnp.max(data_dash, axis=(-2, -1), keepdims=True)
            m = jax.lax.stop_gradient(m)
            return ratio * (jnp.exp(data_dash - diag - m) + eps)
        key = jax.random.key(seed)
        ks = jax.random.split(key, 16)
        s = 0.02
        B, N = (4, 256)
        inp = {'x': jax.random.normal(ks[0], (B, N, DIM), jnp.float32), 'ln1_g': jnp.ones((DEPTH, DIM), jnp.float32), 'ln1_b': jnp.zeros((DEPTH, DIM), jnp.float32), 'ln2_g': jnp.ones((DEPTH, DIM), jnp.float32), 'ln2_b': jnp.zeros((DEPTH, DIM), jnp.float32), 'Wq': jax.random.normal(ks[1], (DEPTH, DIM, INNER), jnp.float32) * s, 'bq': jnp.zeros((DEPTH, INNER), jnp.float32), 'Wk': jax.random.normal(ks[2], (DEPTH, DIM, INNER), jnp.float32) * s, 'bk': jnp.zeros((DEPTH, INNER), jnp.float32), 'Wv': jax.random.normal(ks[3], (DEPTH, DIM, INNER), jnp.float32) * s, 'bv': jnp.zeros((DEPTH, INNER), jnp.float32), 'Wo': jax.random.normal(ks[4], (DEPTH, INNER, DIM), jnp.float32) * s, 'bo': jnp.zeros((DEPTH, DIM), jnp.float32), 'proj': jax.random.normal(ks[5], (DEPTH, NBF, DIM_HEAD), jnp.float32), 'W1': jax.random.normal(ks[6], (DEPTH, DIM, DIM * MULT), jnp.float32) * s, 'b1': jnp.zeros((DEPTH, DIM * MULT), jnp.float32), 'W2': jax.random.normal(ks[7], (DEPTH, DIM * MULT, DIM), jnp.float32) * s, 'b2': jnp.zeros((DEPTH, DIM), jnp.float32)}
        return inp
    _L0_mix_all = _L0_mix_setup()
    _L0_mix_in = {k: v for k, v in _L0_mix_all.items() if k in ('ln1_g', 'ln1_b', 'ln2_g', 'ln2_b', 'Wq', 'bq', 'Wk', 'bk', 'Wv', 'bv', 'Wo', 'bo', 'proj', 'W1', 'b1', 'W2', 'b2')}
    del _L0_mix_all

    def _L0_ffn_setup():
        import jax, jax.numpy as jnp
        import numpy as np
        B, S, D = (4, 64, 512)
        I = 384
        E = 16
        K = 2

        def _inv_softplus(v):
            return float(np.log(np.expm1(v)))

        def swiglu5(h, alpha, gate_scale, up_shift, gate_clamp_raw, up_clamp_raw):
            gate_clamp = jax.nn.softplus(gate_clamp_raw)
            up_clamp = jax.nn.softplus(up_clamp_raw)
            g = jnp.clip(h[..., ::2], -gate_clamp, gate_clamp)
            u = jnp.clip(h[..., 1::2], -up_clamp, up_clamp)
            return g * jax.nn.sigmoid(g * alpha) * gate_scale * (u + up_shift)
        key = jax.random.key(seed)
        ks = jax.random.split(key, 10)
        std = 0.02
        raw = _inv_softplus(7.0)
        act = jnp.array([1.702, 1.0, 1.0, raw, raw], dtype=jnp.float32)
        return {'x': jax.random.normal(ks[0], (B, S, D), dtype=jnp.float32), 'gate_w': jax.random.normal(ks[1], (D, E), dtype=jnp.float32) * 0.01, 'gate_b': jnp.zeros((E,), dtype=jnp.float32), 'shared_w1': jax.random.normal(ks[2], (D, 2 * I), dtype=jnp.float32) * std, 'shared_b1': jnp.zeros((2 * I,), dtype=jnp.float32), 'shared_w2': jax.random.normal(ks[3], (I, D), dtype=jnp.float32) * std, 'shared_b2': jnp.zeros((D,), dtype=jnp.float32), 'shared_act': act, 'expert_w1': jax.random.normal(ks[4], (E, D, 2 * I), dtype=jnp.float32) * std, 'expert_b1': jnp.zeros((E, 2 * I), dtype=jnp.float32), 'expert_w2': jax.random.normal(ks[5], (E, I, D), dtype=jnp.float32) * std, 'expert_b2': jnp.zeros((E, D), dtype=jnp.float32), 'expert_act': jnp.tile(act[None, :], (E, 1))}
    _L0_ffn_all = _L0_ffn_setup()
    _L0_ffn_in = {k: v for k, v in _L0_ffn_all.items() if k in ('gate_w', 'gate_b', 'shared_w1', 'shared_b1', 'shared_w2', 'shared_b2', 'shared_act', 'expert_w1', 'expert_b1', 'expert_w2', 'expert_b2', 'expert_act')}
    del _L0_ffn_all
    return {'x': x, 'src': src, 'dst': dst, 'edge_attr_8': edge_attr_8, 'edge_attr_8_n2': edge_attr_8_n2, 'L0_gnn_Wqkv': _L0_gnn_in['Wqkv'], 'L0_gnn_bqkv': _L0_gnn_in['bqkv'], 'L0_gnn_Wo': _L0_gnn_in['Wo'], 'L0_gnn_bo': _L0_gnn_in['bo'], 'L0_gnn_ln1_g': _L0_gnn_in['ln1_g'], 'L0_gnn_ln1_b': _L0_gnn_in['ln1_b'], 'L0_gnn_W1': _L0_gnn_in['W1'], 'L0_gnn_b1': _L0_gnn_in['b1'], 'L0_gnn_W2': _L0_gnn_in['W2'], 'L0_gnn_b2': _L0_gnn_in['b2'], 'L0_gnn_ln2_g': _L0_gnn_in['ln2_g'], 'L0_gnn_ln2_b': _L0_gnn_in['ln2_b'], 'L0_mix_ln1_g': _L0_mix_in['ln1_g'], 'L0_mix_ln1_b': _L0_mix_in['ln1_b'], 'L0_mix_ln2_g': _L0_mix_in['ln2_g'], 'L0_mix_ln2_b': _L0_mix_in['ln2_b'], 'L0_mix_Wq': _L0_mix_in['Wq'], 'L0_mix_bq': _L0_mix_in['bq'], 'L0_mix_Wk': _L0_mix_in['Wk'], 'L0_mix_bk': _L0_mix_in['bk'], 'L0_mix_Wv': _L0_mix_in['Wv'], 'L0_mix_bv': _L0_mix_in['bv'], 'L0_mix_Wo': _L0_mix_in['Wo'], 'L0_mix_bo': _L0_mix_in['bo'], 'L0_mix_proj': _L0_mix_in['proj'], 'L0_mix_W1': _L0_mix_in['W1'], 'L0_mix_b1': _L0_mix_in['b1'], 'L0_mix_W2': _L0_mix_in['W2'], 'L0_mix_b2': _L0_mix_in['b2'], 'L0_ffn_gate_w': _L0_ffn_in['gate_w'], 'L0_ffn_gate_b': _L0_ffn_in['gate_b'], 'L0_ffn_shared_w1': _L0_ffn_in['shared_w1'], 'L0_ffn_shared_b1': _L0_ffn_in['shared_b1'], 'L0_ffn_shared_w2': _L0_ffn_in['shared_w2'], 'L0_ffn_shared_b2': _L0_ffn_in['shared_b2'], 'L0_ffn_shared_act': _L0_ffn_in['shared_act'], 'L0_ffn_expert_w1': _L0_ffn_in['expert_w1'], 'L0_ffn_expert_b1': _L0_ffn_in['expert_b1'], 'L0_ffn_expert_w2': _L0_ffn_in['expert_w2'], 'L0_ffn_expert_b2': _L0_ffn_in['expert_b2'], 'L0_ffn_expert_act': _L0_ffn_in['expert_act']}

def reference(x, src, dst, edge_attr_8, edge_attr_8_n2, L0_gnn_Wqkv, L0_gnn_bqkv, L0_gnn_Wo, L0_gnn_bo, L0_gnn_ln1_g, L0_gnn_ln1_b, L0_gnn_W1, L0_gnn_b1, L0_gnn_W2, L0_gnn_b2, L0_gnn_ln2_g, L0_gnn_ln2_b, L0_mix_ln1_g, L0_mix_ln1_b, L0_mix_ln2_g, L0_mix_ln2_b, L0_mix_Wq, L0_mix_bq, L0_mix_Wk, L0_mix_bk, L0_mix_Wv, L0_mix_bv, L0_mix_Wo, L0_mix_bo, L0_mix_proj, L0_mix_W1, L0_mix_b1, L0_mix_W2, L0_mix_b2, L0_ffn_gate_w, L0_ffn_gate_b, L0_ffn_shared_w1, L0_ffn_shared_b1, L0_ffn_shared_w2, L0_ffn_shared_b2, L0_ffn_shared_act, L0_ffn_expert_w1, L0_ffn_expert_b1, L0_ffn_expert_w2, L0_ffn_expert_b2, L0_ffn_expert_act):
    import jax
    import jax.numpy as jnp

    def _L0_gnn_ref(node_feature, src, dst, dist_attn, path_attn, Wqkv, bqkv, Wo, bo, ln1_g, ln1_b, W1, b1, W2, b2, ln2_g, ln2_b):
        import jax, jax.numpy as jnp
        import numpy as np
        N = 625
        E = 20000
        D = 512
        H = 8
        DH = D // H
        EPS = 1e-05

        def layer_norm(x, g, b):
            mu = x.mean(-1, keepdims=True)
            var = ((x - mu) ** 2).mean(-1, keepdims=True)
            return (x - mu) * jax.lax.rsqrt(var + EPS) * g + b
        h = layer_norm(node_feature, ln1_g, ln1_b)
        qkv = (h @ Wqkv + bqkv).reshape(N, 3, H, DH)
        q = qkv[:, 0] * D ** (-0.5)
        k = qkv[:, 1]
        v = qkv[:, 2]
        logits = jnp.einsum('ehd,ehd->eh', q[src], k[dst])
        a = logits + dist_attn + path_attn
        mx = jax.ops.segment_max(a, dst, num_segments=N)
        e = jnp.exp(a - mx[dst])
        s = jax.ops.segment_sum(e, dst, num_segments=N)
        sa = e / s[dst]
        msg = v[src] * sa[:, :, None]
        agg = jax.ops.segment_sum(msg, dst, num_segments=N).reshape(N, D)
        x = agg @ Wo + bo
        h1 = node_feature + x
        h2 = layer_norm(h1, ln2_g, ln2_b)
        h2 = jax.nn.gelu(h2 @ W1 + b1, approximate=False) @ W2 + b2
        return h1 + h2

    def _L0_mix_ref(x, ln1_g, ln1_b, ln2_g, ln2_b, Wq, bq, Wk, bk, Wv, bv, Wo, bo, proj, W1, b1, W2, b2):
        import jax, jax.numpy as jnp
        import numpy as np
        DEPTH, DIM, HEADS, DIM_HEAD, NBF, MULT = (2, 512, 8, 64, 256, 4)
        INNER = HEADS * DIM_HEAD

        def layernorm(x, g, b, eps=1e-05):
            mu = jnp.mean(x, axis=-1, keepdims=True)
            var = jnp.mean((x - mu) ** 2, axis=-1, keepdims=True)
            return (x - mu) * jax.lax.rsqrt(var + eps) * g + b

        def softmax_kernel(data, proj, is_query, eps=0.0001):
            d = data.shape[-1]
            normalizer = d ** (-0.25)
            ratio = proj.shape[0] ** (-0.5)
            data_dash = jnp.einsum('bhnd,md->bhnm', data * normalizer, proj)
            diag = jnp.sum(data ** 2, axis=-1, keepdims=True) * 0.5 * normalizer ** 2
            if is_query:
                m = jnp.max(data_dash, axis=-1, keepdims=True)
            else:
                m = jnp.max(data_dash, axis=(-2, -1), keepdims=True)
            m = jax.lax.stop_gradient(m)
            return ratio * (jnp.exp(data_dash - diag - m) + eps)
        B, N, D = x.shape
        for i in range(DEPTH):
            y = layernorm(x, ln1_g[i], ln1_b[i])
            q = (y @ Wq[i] + bq[i]).reshape(B, N, HEADS, DIM_HEAD).transpose(0, 2, 1, 3)
            k = (y @ Wk[i] + bk[i]).reshape(B, N, HEADS, DIM_HEAD).transpose(0, 2, 1, 3)
            v = (y @ Wv[i] + bv[i]).reshape(B, N, HEADS, DIM_HEAD).transpose(0, 2, 1, 3)
            qp = softmax_kernel(q, proj[i], True)
            kp = softmax_kernel(k, proj[i], False)
            k_sum = kp.sum(axis=2)
            d_inv = 1.0 / jnp.einsum('bhnm,bhm->bhn', qp, k_sum)
            ctx = jnp.einsum('bhnm,bhnd->bhmd', kp, v)
            o = jnp.einsum('bhmd,bhnm,bhn->bhnd', ctx, qp, d_inv)
            o = o.transpose(0, 2, 1, 3).reshape(B, N, INNER)
            x = x + o @ Wo[i] + bo[i]
            y = layernorm(x, ln2_g[i], ln2_b[i])
            h = jax.nn.gelu(y @ W1[i] + b1[i], approximate=False)
            x = x + h @ W2[i] + b2[i]
        return x

    def _L0_ffn_ref(x, gate_w, gate_b, shared_w1, shared_b1, shared_w2, shared_b2, shared_act, expert_w1, expert_b1, expert_w2, expert_b2, expert_act):
        import jax, jax.numpy as jnp
        import numpy as np
        B, S, D = (4, 64, 512)
        I = 384
        E = 16
        K = 2

        def _inv_softplus(v):
            return float(np.log(np.expm1(v)))

        def swiglu5(h, alpha, gate_scale, up_shift, gate_clamp_raw, up_clamp_raw):
            gate_clamp = jax.nn.softplus(gate_clamp_raw)
            up_clamp = jax.nn.softplus(up_clamp_raw)
            g = jnp.clip(h[..., ::2], -gate_clamp, gate_clamp)
            u = jnp.clip(h[..., 1::2], -up_clamp, up_clamp)
            return g * jax.nn.sigmoid(g * alpha) * gate_scale * (u + up_shift)
        shape = x.shape
        xf = x.reshape(-1, shape[-1])
        h = xf @ shared_w1 + shared_b1
        t = swiglu5(h, shared_act[0], shared_act[1], shared_act[2], shared_act[3], shared_act[4])
        z = t @ shared_w2 + shared_b2
        gate_logits = xf @ gate_w + gate_b
        gate_probs = jax.nn.softmax(gate_logits, -1)
        w, idx = jax.lax.top_k(gate_probs, K)
        w = w / jnp.sum(w, axis=-1, keepdims=True)
        cw = jnp.sum(jax.nn.one_hot(idx, E, dtype=xf.dtype) * w[..., None], axis=1)
        he = jnp.einsum('nd,edh->enh', xf, expert_w1) + expert_b1[:, None, :]
        a = expert_act
        te = swiglu5(he, a[:, 0, None, None], a[:, 1, None, None], a[:, 2, None, None], a[:, 3, None, None], a[:, 4, None, None])
        oe = jnp.einsum('enh,ehd->end', te, expert_w2) + expert_b2[:, None, :]
        y = jnp.einsum('ne,end->nd', cw, oe)
        return (y + z).reshape(shape)
    xn = _layernorm(x, axis=-1)
    x = x + _L0_gnn_ref(xn, src, dst, edge_attr_8, edge_attr_8_n2, L0_gnn_Wqkv, L0_gnn_bqkv, L0_gnn_Wo, L0_gnn_bo, L0_gnn_ln1_g, L0_gnn_ln1_b, L0_gnn_W1, L0_gnn_b1, L0_gnn_W2, L0_gnn_b2, L0_gnn_ln2_g, L0_gnn_ln2_b) + _L0_mix_ref(xn[None], L0_mix_ln1_g, L0_mix_ln1_b, L0_mix_ln2_g, L0_mix_ln2_b, L0_mix_Wq, L0_mix_bq, L0_mix_Wk, L0_mix_bk, L0_mix_Wv, L0_mix_bv, L0_mix_Wo, L0_mix_bo, L0_mix_proj, L0_mix_W1, L0_mix_b1, L0_mix_W2, L0_mix_b2)[0]
    x = x + _L0_ffn_ref(_layernorm(x, axis=-1)[None], L0_ffn_gate_w, L0_ffn_gate_b, L0_ffn_shared_w1, L0_ffn_shared_b1, L0_ffn_shared_w2, L0_ffn_shared_b2, L0_ffn_shared_act, L0_ffn_expert_w1, L0_ffn_expert_b1, L0_ffn_expert_w2, L0_ffn_expert_b2, L0_ffn_expert_act)[0]
    return x

_drawn_inputs = setup_inputs


def setup_inputs(seed=0):
    import zlib

    import numpy as np

    out = dict(_drawn_inputs(seed))
    spreads = {'L0_gnn_bqkv': (0.0, 0.1),
     'L0_gnn_bo': (0.0, 0.1),
     'L0_gnn_ln1_g': (1.0, 0.2),
     'L0_gnn_ln1_b': (0.0, 0.1),
     'L0_gnn_b1': (0.0, 0.36),
     'L0_gnn_b2': (0.0, 0.1),
     'L0_gnn_ln2_g': (1.0, 0.2),
     'L0_gnn_ln2_b': (0.0, 0.359),
     'L0_mix_ln1_g': (1.0, 0.6),
     'L0_mix_ln1_b': (0.0, 0.8),
     'L0_mix_ln2_g': (1.0, 0.6),
     'L0_mix_ln2_b': (0.0, 0.67),
     'L0_mix_bq': (0.0, 0.8),
     'L0_mix_bk': (0.0, 0.8),
     'L0_mix_bv': (0.0, 0.372),
     'L0_mix_bo': (0.0, 0.1),
     'L0_mix_b1': (0.0, 0.324),
     'L0_mix_b2': (0.0, 0.1),
     'L0_ffn_gate_b': (0.0, 0.307),
     'L0_ffn_shared_b1': (0.0, 0.8),
     'L0_ffn_shared_b2': (0.0, 0.272),
     'L0_ffn_expert_b1': (0.0, 0.8),
     'L0_ffn_expert_b2': (0.0, 0.352)}
    factors = {'L0_mix_Wq': 8.0, 'L0_mix_Wk': 8.0, 'L0_mix_Wv': 3.626, 'L0_mix_proj': 8.0}
    for name, (base, spread) in spreads.items():
        noise = np.random.default_rng([zlib.crc32(name.encode()), seed]).standard_normal(out[name].shape)
        drawn = base * np.exp(spread * noise) if base else spread * noise
        out[name] = jnp.asarray(drawn.astype(out[name].dtype))
    for name, factor in factors.items():
        out[name] = (out[name] * factor).astype(out[name].dtype)
    return out
```

```python
from contextlib import ExitStack

import concourse.bass as bass
from concourse import mybir

ALU = mybir.AluOpType
ACT = mybir.ActivationFunctionType
F32 = mybir.dt.float32
I32 = mybir.dt.int32
U32 = mybir.dt.uint32
AX_X = mybir.AxisListType.X
RMAX = bass.bass_isa.ReduceOp.max

P, T = 125, 5
N = P * T
D, KD = 512, 4
H, DH = 8, 64
FF, FM = 2048, 16
NF = 256
NE, NI, KI = 16, 384, 3
LAYERS = 3
GNN = 2
EDGES = 10000
EB = EDGES // P
EG = 4
PAIRS = N * N
BLOCK = 128
BLOCKS = (2 * N + NE * (BLOCK - 1)) // BLOCK
CHUNKS = [(0, 3), (3, 5)]
QK_NORM = float(DH) ** -0.25
GNN_SCALE = float(D) ** -0.5
EPS_LN = 1e-5
EPS_RF = 1e-4
MASK = -1e30
WSLOTS = 6
WPER = 12


class Ring:

    def __init__(self, banks, filled, drained):
        self.banks, self.filled, self.drained, self.at = banks, filled, drained, {}

    def add(self, job):
        assert job not in self.at, job
        self.at[job] = len(self.at)
        return self.at[job]

    def bank(self, job):
        return self.banks[self.at[job] % len(self.banks)]

    def count(self, job):
        return self.at[job] + 1


def columns(c):
    t0, t1 = CHUNKS[c]
    return t0 * P, t1 * P


def gps_layer(nc, A, out):
    ctx = ExitStack()
    with ctx:
        def sb(name, shape, dt=F32):
            return ctx.enter_context(nc.sbuf_tensor(name, shape, dt))

        def sem(name):
            return ctx.enter_context(nc.semaphore(name))

        pair_table = nc.dram_tensor("pair_table", (PAIRS + 128, H), F32, kind="Internal").ap()
        slot_in = nc.dram_tensor("slot_in", (BLOCKS * BLOCK, D), F32, kind="Internal").ap()
        slot_out = nc.dram_tensor("slot_out", (BLOCKS * BLOCK, D), F32, kind="Internal").ap()
        act_table = nc.dram_tensor("act_table", (NE + 1, 8), F32, kind="Internal").ap()

        XN = sb("XN", [P, T, D])
        MX = sb("MX", [P, T, D])
        ZB = sb("ZB", [128, T * D])
        Z = ZB[0:P, :].rearrange("p (t d) -> p t d", t=T)
        YT = sb("YT", [128, KD, N])
        QK = sb("QK", [128, 2, KD, N])
        V1 = sb("V1", [P, T, H, DH + 1])
        ARENA = sb("ARENA", [128, 10240])
        W = sb("W", [128, WSLOTS, KD * 512])
        ROWB = sb("ROWB", [P, 2, 3, D])
        EXPB = sb("EXPB", [128, 2560])
        TRB = sb("TRB", [128, 2 * 1250])
        PROJ = sb("PROJ", [128, 2, NF])
        KMA = sb("KMA", [P, H])
        spare_i = sb("spare_i", [P, 1], I32)
        spare = sb("spare", [P, 1])
        CTX = sb("CTX", [128, 2, 2, DH + 1])
        ident = sb("ident", [128, 128])
        lower = sb("lower", [P, P])
        zero = sb("zero", [128, 625])
        halves = sb("halves", [128, 2])
        COLS = sb("COLS", [128, 120])
        st = sb("st", [P, T, 6])
        mv = sb("mv", [P, T, 2])
        sd = sb("sd", [P, T])
        rstd = sb("rstd", [P, T])
        eps_ln = sb("eps_ln", [128, 1])
        DG = sb("DG", [P, T, 2, H])
        KM = sb("KM", [P, H])
        KMH = sb("KMH", [H, 1])
        KDIAG = sb("KDIAG", [H, H])
        ones = sb("ones", [H, 128])
        NK = sb("NK", [P, T, H])
        QM = sb("QM", [P, H, T])
        NQ = sb("NQ", [P, H, T])
        REC = sb("REC", [P, 2, T])
        src_i = sb("src_i", [P, EB], I32)
        dst_i = sb("dst_i", [P, EB], I32)
        key = sb("key", [P, EB])
        srcf = sb("srcf", [P, EB])
        EA = sb("EA", [P, EB, H])
        EA2 = sb("EA2", [P, EB, H])
        VC = EA2
        before = sb("before", [P, EB])
        idx = sb("idx", [P, EB], U32)
        emax = sb("emax", [P, H])
        emaxa = sb("emaxa", [P, H])
        pairmax = sb("pairmax", [P, 4, 2])
        negmax = sb("negmax", [P, 4])
        den = sb("den", [P, 4])
        rden = sb("rden", [P, 4])
        neg1 = sb("neg1", [P, 1])

        PROJR = EXPB[:, 0:512].rearrange("p (l a c d) -> p l a c d", l=2, a=2, c=2)
        VROWS = EXPB[:, 512:640]
        KP = ARENA[0:P, :].rearrange("p (h t m) -> p h t m", h=H, t=T)
        HT = ARENA[:, 0:FM * N].rearrange("p (f n) -> p f n", f=FM)
        SQQ = ZB[:, 0:KD * N].rearrange("p (k n) -> p k n", k=KD)
        SQK = ARENA[:, 0:KD * N].rearrange("p (k n) -> p k n", k=KD)
        QP = [EXPB[0:P, s * 1280:(s + 1) * 1280].rearrange("p (t m) -> p t m", t=T) for s in range(2)]
        QPT = [TRB[:, s * 1250:(s + 1) * 1250] for s in range(2)]
        O = Z
        XAGAIN = QK[0:P].rearrange("p a k n -> p (a k n)")[:, 0:T * D].rearrange("p (t d) -> p t d", t=T)
        QT, KT = QK[:, 0], QK[:, 1]
        PAIRW = [ARENA[0:P, s * 5000:(s + 1) * 5000].rearrange("p (s h) -> p s h", h=H) for s in range(2)]
        TS = [EXPB[0:P, s * 625:(s + 1) * 625] for s in range(4)]
        PT = [TRB[0:P, s * 625:(s + 1) * 625].rearrange("p (s d) -> p s d", s=T) for s in range(2)]
        NEG = [TRB[0:P, 1250 + s * 625:1250 + (s + 1) * 625] for s in range(2)]
        SAME = [EXPB[0:P, s * 500:(s + 1) * 500].rearrange("p (j q) -> p j q", j=EG) for s in range(2)]
        SAMEL = [EXPB[0:P, 1000 + s * 500:1500 + s * 500].rearrange("p (j q) -> p j q", j=EG) for s in range(2)]

        banks = [ctx.enter_context(nc.psum_tensor(f"bank{i}", [128, 512], F32)) for i in range(8)]

        act_filled, act_drained = sem("act_filled"), sem("act_drained")
        vec_filled, vec_drained = sem("vec_filled"), sem("vec_drained")
        RA = Ring(banks[0:4], act_filled, act_drained)
        RV = Ring(banks[4:8], vec_filled, vec_drained)

        vec_step, act_step, pool_step = sem("vec_step"), sem("act_step"), sem("pool_step")
        x_loaded, rows_loaded, rowb_loaded, rowb_again = sem("x_loaded"), sem("rows_loaded"), sem("rowb_loaded"), sem("rowb_again")
        edges_loaded, attrs_loaded = sem("edges_loaded"), sem("attrs_loaded")
        proj_loaded = sem("proj_loaded")
        consts_ready, zero_ready = sem("consts_ready"), sem("zero_ready")
        table_zeroed, slots_zeroed = sem("table_zeroed"), sem("slots_zeroed")
        w_loaded = [sem(f"w_loaded{i}") for i in range(WSLOTS)]
        var_ready, std_ready, xn_ready, z_ready = sem("var_ready"), sem("std_ready"), sem("xn_ready"), sem("z_ready")
        resid_ready = sem("resid_ready")
        squares_ready = sem("squares_ready")
        kmax_part, kdiag_ready, kbias_ready, qbias_ready = sem("kmax_part"), sem("kdiag_ready"), sem("kbias_ready"), sem("qbias_ready")
        kexp_done, kcol_ready, kp_ready = sem("kexp_done"), sem("kcol_ready"), sem("kp_ready")
        edge_attr_ready, edge_max_part, edge_max_all = sem("edge_attr_ready"), sem("edge_max_part"), sem("edge_max_all")
        edge_sub_ready, edge_exp_ready, idx_ready = sem("edge_sub_ready"), sem("edge_exp_ready"), sem("idx_ready")
        scattered = sem("scattered")
        pairw_loaded = [sem(f"pairw_loaded{i}") for i in range(2)]
        smax_ready, sexp_done, p_ready = sem("smax_ready"), sem("sexp_done"), sem("p_ready")
        x_again = sem("x_again")

        WFREE = W[:, :, :].rearrange("p s n -> p (s n)")
        SW1 = WFREE[:, 0:KD * 2 * NI].rearrange("p (k n) -> p k n", k=KD)
        GATEW = WFREE[:, 3072:3136].rearrange("p (k e) -> p k e", k=KD)
        SB1 = WFREE[0:P, 3136:3904]
        QKFREE = QK[:, :, :, :].rearrange("p a k n -> p (a k n)")
        SW2 = QKFREE[:, 2560:4096].rearrange("p (k n) -> p k n", k=KI)
        SB2 = QKFREE[0:P, 4096:4608]
        GATEB = QKFREE[0:P, 4608:4624]
        SACT = QKFREE[0:P, 4624:4632]
        EW1 = [ARENA[:, s * 4608:s * 4608 + 3072].rearrange("p (k n) -> p k n", k=KD) for s in range(2)]
        EW2 = [ARENA[:, s * 4608 + 3072:(s + 1) * 4608].rearrange("p (k n) -> p k n", k=KI) for s in range(2)]

        def pair_of(base, size):
            return [WFREE[:, base + s * size:base + (s + 1) * size] for s in range(2)]

        XG, XGT = pair_of(4096, 512), pair_of(5120, 512)
        HB, GC, TE, TET = pair_of(6144, 768), pair_of(7680, 384), pair_of(8448, 384), pair_of(9216, 384)
        UC = pair_of(11520, 384)
        ROW1 = [QKFREE[0:1, s * 1288:(s + 1) * 1288] for s in range(2)]
        ROWS = [WFREE[:, 9984:9984 + 1288], QKFREE[:, 2576:2576 + 1288]]
        EB1, EB2, EACT = [r[:, 0:768] for r in ROWS], [r[:, 768:1280] for r in ROWS], [r[:, 1280:1288] for r in ROWS]
        OG = [EXPB[:, s * 512:(s + 1) * 512] for s in range(2)]
        SIG = [EXPB[:, 1024 + s * 384:1408 + s * 384] for s in range(2)]
        UPPER, ONESP = ROWB[:, 1, 0, 0:P], ROWB[:, 1, 1, 0:P]
        COUNT_I = ROWB[:, 1, 2, 0:BLOCKS].bitcast(I32)
        COUNT = ROWB[:, 1, 2, 32:32 + BLOCKS]
        THRESH = ROWB[:, 1, 2, 64:69]
        UPTO = ROWB[:, 1, 2, 128:384].rearrange("p (a b) -> p a b", a=NE)
        TR = TRB[0:P, :]
        LOGIT = TR[:, 0:80].rearrange("p (t e) -> p t e", t=T)
        LMAX, LSUM = TR[:, 80:85], TR[:, 85:90]
        TOP = TR[:, 96:136].rearrange("p (t e) -> p t e", t=T)
        TOPI = TR[:, 136:176].bitcast(U32).rearrange("p (t e) -> p t e", t=T)
        TOPF = TR[:, 176:186].rearrange("p (t c) -> p t c", t=T)
        CW = TR[:, 186:196].rearrange("p (t c) -> p t c", t=T)
        PICK = TR[:, 256:416].rearrange("p (t c e) -> p t c e", t=T, c=2)
        PICKED = TR[:, 416:496].rearrange("p (t e) -> p t e", t=T)
        RANK = TR[:, 512:608].rearrange("p (t e) -> p t e", t=T + 1)
        NBLK, UPBLK, BASE = TR[:, 608:624], TR[:, 624:640], TR[:, 640:656]
        CMP = TR[:, 1024:1024 + 400]
        SLOTF = TR[:, 656:666]
        SLOT = TR[:, 672:682].bitcast(U32)
        BLKF = TR[:, 704:729]
        BLKE = TR[:, 736:761].bitcast(I32)
        GOT = ARENA[0:P, 0:T * 2 * D].rearrange("p (t c d) -> p t c d", t=T, c=2)
        PRM = sb("PRM", [NE + 1, 8])
        PRMT = sb("PRMT", [NE + 1, 4])

        prm_in, prm_step_a, prm_step_d, prm_done, prm_stored = sem("prm_in"), sem("prm_step_a"), sem("prm_step_d"), sem("prm_done"), sem("prm_stored")
        ffn_w_loaded, ffn_b_loaded, count_ready, tiles_ready = sem("ffn_w_loaded"), sem("ffn_b_loaded"), sem("count_ready"), sem("tiles_ready")
        logits_ready, gate_exp, picked_ready, routed, slots_filled = sem("logits_ready"), sem("gate_exp"), sem("picked_ready"), sem("routed"), sem("slots_filled")
        sgate_ready, ssig_ready, ste_ready = sem("sgate_ready"), sem("ssig_ready"), sem("ste_ready")
        w1_loaded, w2_loaded = [sem(f"w1_loaded{s}") for s in range(2)], [sem(f"w2_loaded{s}") for s in range(2)]
        row_loaded, xg_loaded = [sem(f"row_loaded{s}") for s in range(2)], [sem(f"xg_loaded{s}") for s in range(2)]
        stored = [sem(f"stored{s}") for s in range(2)]
        rows_spread = sem("rows_spread")
        xt_filled, xgt_ready, h_filled, h_drained = sem("xt_filled"), sem("xgt_ready"), sem("h_filled"), sem("h_drained")
        g_ready, u_ready, gu_ready, sig_ready, te_ready, tt_filled, tet_ready = sem("g_ready"), sem("u_ready"), sem("gu_ready"), sem("sig_ready"), sem("te_ready"), sem("tt_filled"), sem("tet_ready")
        o_filled, o_drained, gathered, y_ready, y_stored = sem("o_filled"), sem("o_drained"), sem("gathered"), sem("y_ready"), sem("y_stored")
        XT_BANK, H_BANK, TT_BANK, O_BANK = [banks[0], banks[1]], [banks[2:4], banks[4:6]], banks[6], banks[7]

        def run_blocks(engine, step):
            for b in range(3):
                step(b, b // 2, b % 2)
            with engine.Fori(1, (BLOCKS - 3) // 2) as i:
                step(2 * i + 1, i, 1)
                step(2 * i + 2, i + 1, 0)
            for b in range(2 * ((BLOCKS - 3) // 2) + 1, BLOCKS + 1):
                step(b, b // 2, b % 2)

        chunk_last = {}
        col_at, n = {}, 0
        for group in ("mix", "gnn"):
            layers = 2 if group == "mix" else 1
            for name, k in (("ln1_g", 4), ("ln1_b", 4), ("bq", 4), ("bk", 4), ("ln2_g", 4), ("ln2_b", 4), ("b1", 16)):
                for l in range(layers):
                    col_at[name, l if group == "mix" else GNN] = n
                    n += k
        n_cols = n

        def col(name, L, k):
            c = col_at[name, L] + k
            return COLS[:, c:c + 1]

        def weight(chunk):
            return W[:, chunk % WSLOTS, :].rearrange("p (k n) -> p k n", k=KD)

        def pair_columns(L, t):
            return t * P, (t + 1) * P

        block = ctx.enter_context(nc.Block())

        @block.tensor
        def _(pe):
            seen = {}

            def wait(s, n):
                if seen.get(s.name, 0) < n:
                    pe.wait_ge(s, n)
                    seen[s.name] = n

            def bank_for(ring, job):
                n = ring.add(job)
                if n >= 4:
                    wait(ring.drained, n - 3)
                return ring.bank(job)

            def ready(ring, job):
                wait(ring.drained, ring.count(job))

            def chunk_loaded(c):
                wait(w_loaded[c % WSLOTS], 16 * (c // WSLOTS + 1))

            def transposes(tag, L, src):
                for c, (t0, t1) in enumerate(CHUNKS):
                    for k in range(KD):
                        ring = RV if k % 2 == 0 else RA
                        b = bank_for(ring, (tag, L, c, k))
                        for t in range(t0, t1):
                            ins = pe.transpose(b[:, (t - t0) * P:(t - t0 + 1) * P],
                                               src[:, t, k * 128:(k + 1) * 128], ident[0:P, 0:P])
                        ins.then_inc(ring.filled, 1)

            def column_form_ready(tag, L):
                ready(RV, (tag, L, 1, 2))
                ready(RA, (tag, L, 1, 3))

            def rows_product(ring, job, chunk, t):
                b = bank_for(ring, job)
                for k in range(KD):
                    ins = pe.matmul(b[0:P, :], YT[:, k, t * P:(t + 1) * P], weight(chunk)[:, k, :],
                                    start=(k == 0), stop=(k == KD - 1))
                ins.then_inc(ring.filled, 1)

            wait(consts_ready, 1)
            wait(rows_loaded, 16 * 14)
            b = bank_for(RV, ("cols",))
            pe.transpose(b[:, 0:n_cols], VROWS[0:n_cols, :], ident[0:n_cols, 0:n_cols]).then_inc(vec_filled, 1)

            wait(proj_loaded, 32)
            b = bank_for(RV, ("proj",))
            for i in range(4):
                ins = pe.transpose(b[:, i * 128:(i + 1) * 128], PROJR[:, i // 2, i % 2].rearrange("p c d -> p (c d)"), ident[:, :])
            ins.then_inc(vec_filled, 1)

            def edge_group(g):
                b = bank_for(RV, ("keys", g))
                wait(edge_exp_ready, 1)
                for j in range(EG):
                    ins = pe.transpose(b[0:P, j * P:(j + 1) * P], key[:, g * EG + j:g * EG + j + 1].to_broadcast([P, P]),
                                       ident[0:P, 0:P])
                ins.then_inc(vec_filled, 1)

            def edge_sums(g):
                b = bank_for(RV, ("sums", g))
                ready(RV, ("keys", g))
                for j in range(EG):
                    ins = pe.matmul(b[0:P, j * H:(j + 1) * H], SAME[g % 2][:, j, :], EA[:, g * EG + j, :],
                                    start=True, stop=True)
                ins.then_inc(vec_filled, 1)

            for L in range(LAYERS):
                c0 = WPER * L
                wait(z_ready, 10 * L + 5)
                transposes("y1", L, Z)
                column_form_ready("y1", L)
                chunk_loaded(c0)
                chunk_loaded(c0 + 1)
                for m in range(KD):
                    for c in range(2):
                        n0, n1 = columns(c)
                        for ring, job, ch in ((RV, ("q", L, m, c), c0), (RA, ("k", L, m, c), c0 + 1)):
                            b = bank_for(ring, job)
                            for k in range(KD):
                                ins = pe.matmul(b[:, 0:n1 - n0], weight(ch)[:, k, m * 128:(m + 1) * 128],
                                                YT[:, k, n0:n1], start=(k == 0), stop=(k == KD - 1))
                            ins.then_inc(ring.filled, 1)
                chunk_last[c0] = (RV, ("q", L, KD - 1, 1))
                chunk_last[c0 + 1] = (RA, ("k", L, KD - 1, 1))
                chunk_loaded(c0 + 2)
                for t in range(T):
                    rows_product(RV, ("v", L, t), c0 + 2, t)
                chunk_last[c0 + 2] = (RV, ("v", L, T - 1))

                if L != GNN:
                    b = bank_for(RV, ("diag", L))
                    dg = b[0:P, 0:T * 2 * H].rearrange("p (t q h) -> p t q h", t=T, q=2)
                    wait(squares_ready, 2 * L + 2)
                    for t in range(T):
                        for q in range(2):
                            for k in range(KD):
                                s = (SQQ if q == 0 else SQK)[:, k, t * P:(t + 1) * P]
                                ins = pe.matmul(dg[:, t, q, 2 * k:2 * k + 2], s, halves[:, :], start=True, stop=True)
                    ins.then_inc(vec_filled, 1)
                    ready(RA, ("k", L, KD - 1, 1))
                    ready(RV, ("q", L, KD - 1, 1))

                    def features(tag, x, h, tp):
                        b = bank_for(RA, (tag, L, h, tp))
                        r0 = 64 * (h % 2)
                        for t in range(2 * tp, min(2 * tp + 2, T)):
                            ins = pe.matmul(b[0:P, (t - 2 * tp) * NF:(t - 2 * tp + 1) * NF],
                                            x[r0:r0 + DH, h // 2, t * P:(t + 1) * P],
                                            PROJ[r0:r0 + DH, L % 2, :], start=True, stop=True)
                        ins.then_inc(act_filled, 1)

                    def q_features(h):
                        for tp in range(3):
                            features("qd", QT, h, tp)

                    def attend(h):
                        ready(RV, ("qt", L, h, 2))
                        ready(RV, ("ctx", L, h))
                        b = bank_for(RV, ("o", L, h))
                        for t in range(T):
                            for mh in range(2):
                                blk = mh * T + t
                                ins = pe.matmul(b[0:P, t * (DH + 1):(t + 1) * (DH + 1)],
                                                QPT[h % 2][:, blk * P:(blk + 1) * P], CTX[:, h % 2, mh, :],
                                                start=(mh == 0), stop=(mh == 1))
                        ins.then_inc(vec_filled, 1)

                    for hp in range(H // 2):
                        for tp in range(3):
                            for hh in range(2):
                                features("kd", KT, 2 * hp + hh, tp)
                    q_features(0)
                    q_features(1)
                    b = bank_for(RV, ("kmax", L))
                    wait(kmax_part, H * L + H)
                    pe.transpose(b[0:H, 0:P], KM[:, :], ident[0:P, 0:P]).then_inc(vec_filled, 1)
                    b = bank_for(RV, ("kmax_all", L))
                    wait(kdiag_ready, L + 1)
                    pe.matmul(b[0:P, 0:H], ones[0:H, 0:P], KDIAG[:, :], start=True, stop=True).then_inc(vec_filled, 1)
                    for h in range(H):
                        ready(RA, ("qd", L, h, 2))
                        for i in range(3):
                            b = bank_for(RV, ("qt", L, h, i))
                            for blk in range(4 * i, min(4 * i + 4, 2 * T)):
                                mh, t = blk // T, blk % T
                                ins = pe.transpose(b[:, (blk - 4 * i) * P:(blk - 4 * i + 1) * P],
                                                   QP[h % 2][:, t, mh * 128:(mh + 1) * 128], ident[0:P, 0:P])
                            ins.then_inc(vec_filled, 1)
                        if h + 2 < H:
                            q_features(h + 2)
                        wait(kp_ready, H * L + h + 1)
                        b = bank_for(RV, ("ctx", L, h))
                        for mh in range(2):
                            for t in range(T):
                                ins = pe.matmul(b[:, mh * (DH + 1):(mh + 1) * (DH + 1)],
                                                KP[:, h, t, mh * 128:(mh + 1) * 128], V1[:, t, h, :],
                                                start=(t == 0), stop=(t == T - 1))
                        ins.then_inc(vec_filled, 1)
                        if h:
                            attend(h - 1)
                    attend(H - 1)
                    ready(RV, ("o", L, H - 1))
                else:
                    ready(RA, ("k", L, KD - 1, 1))
                    ready(RV, ("v", L, T - 1))

                    def scores(i):
                        dt, h = divmod(i, H)
                        r0 = 64 * (h % 2)
                        for c in range(2):
                            n0, n1 = columns(c)
                            b = bank_for(RV, ("s", i, c))
                            pe.matmul(b[0:P, 0:n1 - n0], KT[r0:r0 + DH, h // 2, dt * P:(dt + 1) * P],
                                      QT[r0:r0 + DH, h // 2, n0:n1], start=True, stop=True).then_inc(vec_filled, 1)

                    def probs_turned(i):
                        wait(p_ready, i + 1)
                        for j in range(2):
                            b = bank_for(RA, ("pt", i, j))
                            for s in range(4 * j, min(4 * j + 4, T)):
                                ins = pe.transpose(b[0:P, (s - 4 * j) * P:(s - 4 * j + 1) * P],
                                                   TS[i % 4][:, s * P:(s + 1) * P], ident[0:P, 0:P])
                            ins.then_inc(act_filled, 1)

                    def gather_messages(i):
                        ready(RA, ("pt", i, 1))
                        b = bank_for(RV, ("agg", i))
                        for s in range(T):
                            ins = pe.matmul(b[0:P, 0:DH], PT[i % 2][:, s, :], V1[:, s, i % H, 0:DH],
                                            start=(s == 0), stop=(s == T - 1))
                        ins.then_inc(vec_filled, 1)

                    for i in range(T * H + 3):
                        if i < T * H:
                            scores(i)
                        if 0 <= i - 2 < T * H:
                            probs_turned(i - 2)
                        if 0 <= i - 3 < T * H:
                            gather_messages(i - 3)
                    ready(RV, ("agg", T * H - 1))

                transposes("oT", L, O)
                column_form_ready("oT", L)
                chunk_loaded(c0 + 3)
                for t in range(T):
                    rows_product(RV, ("x1", L, t), c0 + 3, t)
                chunk_last[c0 + 3] = (RV, ("x1", L, T - 1))

                wait(z_ready, 10 * L + 10)
                transposes("y2", L, Z)
                column_form_ready("y2", L)
                for f in range(FM):
                    ch = c0 + 4 + f // 4
                    chunk_loaded(ch)
                    for c in range(2):
                        n0, n1 = columns(c)
                        b = bank_for(RA, ("h", L, f, c))
                        for k in range(KD):
                            ins = pe.matmul(b[:, 0:n1 - n0], weight(ch)[:, k, (f % 4) * 128:(f % 4 + 1) * 128],
                                            YT[:, k, n0:n1], start=(k == 0), stop=(k == KD - 1))
                        ins.then_inc(act_filled, 1)
                    chunk_last[ch] = (RA, ("h", L, f, 1))
                    if L == 0:
                        for g in range(5 * f // 4, 5 * (f + 1) // 4):
                            edge_group(g)
                            if g:
                                edge_sums(g - 1)
                if L == 0:
                    edge_sums(EB // EG - 1)
                for g in range(4):
                    chunk_loaded(c0 + 8 + g)
                for t in range(T):
                    b = bank_for(RV, ("x2", L, t))
                    ready(RA, ("h", L, FM - 1, 1))
                    for f in range(FM):
                        ins = pe.matmul(b[0:P, :], HT[:, f, t * P:(t + 1) * P], weight(c0 + 8 + f // 4)[:, f % 4, :],
                                        start=(f == 0), stop=(f == FM - 1))
                    ins.then_inc(vec_filled, 1)
                for g in range(4):
                    chunk_last[c0 + 8 + g] = (RV, ("x2", L, T - 1))

            wait(z_ready, 5 * (2 * LAYERS + 1))
            transposes("yf", 0, Z)
            column_form_ready("yf", 0)
            wait(ffn_w_loaded, 16 * 3)
            b = bank_for(RV, ("gate",))
            for t in range(T):
                for k in range(KD):
                    ins = pe.matmul(b[0:P, t * NE:(t + 1) * NE], YT[:, k, t * P:(t + 1) * P], GATEW[:, k, :],
                                    start=(k == 0), stop=(k == KD - 1))
            ins.then_inc(vec_filled, 1)

            def shared_hidden(t):
                for half in range(2):
                    b = bank_for(RV, ("sh", t, half))
                    for k in range(KD):
                        ins = pe.matmul(b[0:P, 0:NI], YT[:, k, t * P:(t + 1) * P], SW1[:, k, half * NI:(half + 1) * NI],
                                        start=(k == 0), stop=(k == KD - 1))
                    ins.then_inc(vec_filled, 1)

            shared_hidden(0)
            b = bank_for(RV, ("rank",))
            wait(picked_ready, 1)
            wait(tiles_ready, 1)
            for t in range(T + 1):
                for u in range(min(t, T)):
                    ins = pe.matmul(b[0:P, t * NE:(t + 1) * NE], ONESP, PICKED[:, u, :], start=(u == 0), stop=(t == T and u == T - 1))
                if t < T:
                    ins = pe.matmul(b[0:P, t * NE:(t + 1) * NE], UPPER, PICKED[:, t, :], start=(t == 0), stop=True)
            ins.then_inc(vec_filled, 1)
            for t in range(T):
                if t + 1 < T:
                    shared_hidden(t + 1)
                wait(ste_ready, t + 1)
                b = bank_for(RA, ("st", t))
                for k in range(KI):
                    ins = pe.transpose(b[:, k * P:(k + 1) * P], TE[t % 2][0:P, k * 128:(k + 1) * 128], ident[0:P, 0:P])
                ins.then_inc(act_filled, 1)
                ready(RA, ("st", t))
                b = bank_for(RV, ("so", t))
                for k in range(KI):
                    ins = pe.matmul(b[0:P, :], TET[t % 2][:, k * 128:k * 128 + P], SW2[:, k, :], start=(k == 0), stop=(k == KI - 1))
                ins.then_inc(vec_filled, 1)
            ready(RV, ("so", T - 1))

            def turn_tokens(b, j, s):
                pe.wait_ge(xg_loaded[s], 16 * (j + 1))
                if not (isinstance(b, int) and b < 2):
                    pe.wait_ge(xgt_ready, b - 1)
                for k in range(KD):
                    ins = pe.transpose(XT_BANK[s][:, k * 128:(k + 1) * 128], XG[s][:, k * 128:(k + 1) * 128], ident[:, :])
                ins.then_inc(xt_filled, 1)

            def hidden(b, j, s):
                pe.wait_ge(w1_loaded[s], 16 * (j + 1))
                pe.wait_ge(xgt_ready, b + 1)
                if not (isinstance(b, int) and b < 2):
                    pe.wait_ge(h_drained, b - 1)
                for half in range(2):
                    for k in range(KD):
                        ins = pe.matmul(H_BANK[s][half][:, 0:NI], XGT[s][:, k * 128:(k + 1) * 128],
                                        EW1[s][:, k, half * NI:(half + 1) * NI], start=(k == 0), stop=(k == KD - 1))
                ins.then_inc(h_filled, 1)

            def output(b, j, s):
                pe.wait_ge(te_ready, b + 1)
                if not (isinstance(b, int) and b < 1):
                    pe.wait_ge(tet_ready, b)
                for k in range(KI):
                    ins = pe.transpose(TT_BANK[:, k * 128:(k + 1) * 128], TE[s][:, k * 128:(k + 1) * 128], ident[:, :])
                ins.then_inc(tt_filled, 1)
                pe.wait_ge(tet_ready, b + 1)
                pe.wait_ge(w2_loaded[s], 16 * (j + 1))
                if not (isinstance(b, int) and b < 1):
                    pe.wait_ge(o_drained, b)
                for k in range(KI):
                    ins = pe.matmul(O_BANK[:, :], TET[s][:, k * 128:(k + 1) * 128], EW2[s][:, k, :], start=(k == 0), stop=(k == KI - 1))
                ins.then_inc(o_filled, 1)

            def step(b, j, s):
                last = isinstance(b, int) and b >= BLOCKS
                if isinstance(b, int) and b == 0:
                    turn_tokens(0, 0, 0)
                if not last:
                    hidden(b, j, s)
                    if not (isinstance(b, int) and b == BLOCKS - 1):
                        turn_tokens(b + 1, j + s, 1 - s)
                if not (isinstance(b, int) and b == 0):
                    output(b - 1, j - 1 + s, 1 - s)

            run_blocks(pe, step)


        @block.sync
        def _(sp):
            x_rows = A["x"].rearrange("(t p) d -> p t d", p=P)
            sp.dma_start(Z, x_rows).then_inc(x_loaded, 16)
            for group, prefix, names in (("mix", "L0_mix_", ("ln1_g", "ln1_b", "bq", "bk", "ln2_g", "ln2_b", "b1")),
                                         ("gnn", "L0_gnn_", ("ln1_g", "ln1_b", "bq", "bk", "ln2_g", "ln2_b", "b1"))):
                for name in names:
                    if group == "mix":
                        v = A[prefix + name].rearrange("l (k p) -> (l k) p", p=128)
                        r0 = col_at[name, 0]
                    elif name in ("bq", "bk"):
                        j = ("bq", "bk").index(name)
                        v = A[prefix + "bqkv"][j * D:(j + 1) * D].rearrange("(k p) -> k p", p=128)
                        r0 = col_at[name, GNN]
                    else:
                        v = A[prefix + name].rearrange("(k p) -> k p", p=128)
                        r0 = col_at[name, GNN]
                    sp.dma_start(VROWS[r0:r0 + v.shape[0], :], v).then_inc(rows_loaded, 16)

            for c in range(2):
                sp.dma_start(PROJR[:, :, :, c, :], A["L0_mix_proj"].rearrange("l (a p) d -> p l a d", p=128)).then_inc(proj_loaded, 16)

            for row0, v in ((0, A["L0_ffn_expert_act"]), (NE, A["L0_ffn_shared_act"].unsqueeze(0))):
                sp.dma_start(PRM[row0:row0 + v.shape[0], 0:5], v).then_inc(prm_in, 16)

            def load_chunk(c):
                L, j = divmod(c, WPER)
                mixed = L != GNN
                if j < 3:
                    src = (A["L0_mix_" + ("Wq", "Wk", "Wv")[j]][L] if mixed
                           else A["L0_gnn_Wqkv"][:, j * D:(j + 1) * D])
                elif j == 3:
                    src = A["L0_mix_Wo"][L] if mixed else A["L0_gnn_Wo"]
                elif j < 8:
                    src = (A["L0_mix_W1"][L] if mixed else A["L0_gnn_W1"])[:, (j - 4) * 512:(j - 3) * 512]
                else:
                    src = (A["L0_mix_W2"][L] if mixed else A["L0_gnn_W2"])[(j - 8) * 512:(j - 7) * 512, :]
                if c >= WSLOTS:
                    ring, job = chunk_last[c - WSLOTS]
                    sp.wait_ge(ring.filled, ring.count(job))
                sp.dma_start(weight(c), src.rearrange("(k p) n -> p k n", p=128)).then_inc(w_loaded[c % WSLOTS], 16)

            for c in range(WPER * LAYERS):
                load_chunk(c)
                if c == WPER + 5:
                    sp.wait_ge(vec_drained, RV.count(("x2", 0, T - 1)))
                    for j, v in enumerate((A["L0_gnn_bqkv"][2 * D:3 * D], A["L0_gnn_bo"], A["L0_gnn_b2"])):
                        sp.dma_start(ROWB[:, 0, j, :], v.partition_broadcast(P)).then_inc(rowb_again, 16)
                if c == WPER * GNN + 8:
                    sp.wait_ge(vec_filled, RV.count(("s", T * H - 1, 1)))
                    sp.dma_start(XAGAIN, x_rows).then_inc(x_again, 16)

            ring, job = chunk_last[WPER * GNN + 7]
            sp.wait_ge(ring.filled, ring.count(job))
            sp.dma_start(SW1, A["L0_ffn_shared_w1"].rearrange("(k p) n -> p k n", p=128)).then_inc(ffn_w_loaded, 16)
            sp.dma_start(GATEW, A["L0_ffn_gate_w"].rearrange("(k p) n -> p k n", p=128)).then_inc(ffn_w_loaded, 16)
            sp.dma_start(SW2, A["L0_ffn_shared_w2"].rearrange("(k p) n -> p k n", p=128)).then_inc(ffn_w_loaded, 16)
            sp.dma_start(SB1, A["L0_ffn_shared_b1"].partition_broadcast(P)).then_inc(ffn_b_loaded, 16)
            sp.dma_start(SB2, A["L0_ffn_shared_b2"].partition_broadcast(P)).then_inc(ffn_b_loaded, 16)
            sp.dma_start(GATEB, A["L0_ffn_gate_b"].partition_broadcast(P)).then_inc(ffn_b_loaded, 16)
            sp.wait_ge(prm_stored, 16)
            sp.dma_start(SACT, act_table[NE].partition_broadcast(P)).then_inc(ffn_b_loaded, 16)

            def step(b, j, s):
                if isinstance(b, int) and b >= BLOCKS:
                    return
                first = isinstance(b, int) and b < 2
                e = sp.value_load(BLKE[0:1, bass.ds(b, 1)], min_val=0, max_val=NE - 1)
                if not first:
                    sp.wait_ge(xt_filled, b - 1)
                sp.dma_start(XG[s], slot_in[bass.ds(b * BLOCK, BLOCK), :]).then_inc(xg_loaded[s], 16)
                if not first:
                    sp.wait_ge(h_filled, b - 1)
                sp.dma_start(EW1[s], A["L0_ffn_expert_w1"][bass.ds(e, 1)].rearrange("o (k p) n -> p (o k) n", p=128)).then_inc(w1_loaded[s], 16)
                if not first:
                    sp.wait_ge(rows_spread, b - 1)
                sp.dma_start(ROW1[s][:, 0:2 * NI], A["L0_ffn_expert_b1"][bass.ds(e, 1)]).then_inc(row_loaded[s], 16)
                sp.dma_start(ROW1[s][:, 2 * NI:2 * NI + D], A["L0_ffn_expert_b2"][bass.ds(e, 1)]).then_inc(row_loaded[s], 16)
                sp.dma_start(ROW1[s][:, 2 * NI + D:], act_table[bass.ds(e, 1)]).then_inc(row_loaded[s], 16)

            sp.wait_ge(routed, 1)
            sp.wait_ge(slots_filled, 16 * 2 * T)
            sp.wait_ge(vec_drained, RV.count(("so", T - 1)))
            run_blocks(sp, step)
            for t in range(T):
                sp.wait_ge(y_ready, t + 1)
                sp.dma_start(out.rearrange("(t p) d -> p t d", p=P)[:, t, :], MX[:, t, :]).then_inc(y_stored, 16)
            sp.wait_ge(y_stored, 16 * T)

        @block.gpsimd
        def _(pool):
            nc.gpsimd.memset(ident[:, :], 0.0).then_inc(pool_step, 1)
            nc.gpsimd.memset(lower[:, :], 1.0).then_inc(pool_step, 1)
            nc.gpsimd.memset(ones[:, :], 1.0).then_inc(pool_step, 1)
            pool.wait_ge(pool_step, 3)
            nc.gpsimd.affine_select(out=ident[:, :], in_=ident[:, :], compare_op=ALU.not_equal, fill=1.0, base=0,
                                    pattern=[[-1, 128]], channel_multiplier=1).then_inc(pool_step, 1)
            nc.gpsimd.affine_select(out=lower[:, :], in_=lower[:, :], compare_op=ALU.is_gt, fill=0.0, base=0,
                                    pattern=[[-1, P]], channel_multiplier=1).then_inc(pool_step, 1)
            pool.wait_ge(pool_step, 5)
            nc.gpsimd.iota(spare_i[:, :], pattern=[[0, 1]], base=PAIRS, channel_multiplier=1).then_inc(pool_step, 1)
            pool.wait_ge(pool_step, 6)
            nc.gpsimd.memset(zero[:, :], 0.0).then_inc(consts_ready, 1)
            pool.wait_ge(consts_ready, 1)
            for L in range(2):
                for j, name in enumerate(("bv", "bo", "b2")):
                    pool.dma_start(ROWB[:, L, j, :], A["L0_mix_" + name][L].partition_broadcast(P)).then_inc(rowb_loaded, 16)
            pool.dma_start(src_i[:, :], A["src"].rearrange("(p j) -> p j", p=P)).then_inc(edges_loaded, 16)
            pool.dma_start(dst_i[:, :], A["dst"].rearrange("(p j) -> p j", p=P)).then_inc(edges_loaded, 16)
            pool.dma_start(EA[:, :, :], A["edge_attr_8"].rearrange("(p j) h -> p j h", p=P)).then_inc(attrs_loaded, 16)
            pool.dma_start(EA2[:, :, :], A["edge_attr_8_n2"].rearrange("(p j) h -> p j h", p=P)).then_inc(attrs_loaded, 16)
            for t in range(T):
                pool.dma_start(pair_table[t * P * N:(t + 1) * P * N, :].rearrange("(p s) h -> p (s h)", p=P)
                               .rearrange("p (r c) -> p r c", r=H),
                               zero[0:P, :].unsqueeze(1).to_broadcast([P, H, N])).then_inc(table_zeroed, 16)
            pool.dma_start(pair_table[PAIRS:PAIRS + 128, :], zero[:, 0:H]).then_inc(table_zeroed, 16)
            for b in range(BLOCKS):
                pool.dma_start(slot_in[b * BLOCK:(b + 1) * BLOCK, :], zero[:, 0:D]).then_inc(slots_zeroed, 16)
            pool.wait_ge(edge_max_part, 1)
            nc.gpsimd.partition_all_reduce(emaxa[:, :], emax[:, :], P, RMAX).then_inc(edge_max_all, 1)
            pool.wait_ge(table_zeroed, 16 * (T + 1))
            pool.wait_ge(idx_ready, 1)
            for j in range(EB):
                pool.indirect_dma_start(out=pair_table[:, :], out_offset=bass.IndirectOffsetOnAxis(ap=idx[:, j:j + 1], axis=0),
                                        in_=VC[:, j, :], in_offset=None, compute_op=ALU.add).then_inc(scattered, 16)
                pool.wait_ge(scattered, 16 * (j + 1))
            for dt in range(T):
                if dt == 0:
                    pool.wait_ge(vec_filled, RV.count(("x2", 1, T - 1)))
                if dt >= 2:
                    pool.wait_ge(p_ready, H * (dt - 1))
                pool.dma_start(PAIRW[dt % 2], pair_table[dt * P * N:(dt + 1) * P * N, :].rearrange("(p s) h -> p s h", p=P))\
                    .then_inc(pairw_loaded[dt % 2], 16)

            pool.wait_ge(vec_drained, RV.count(("x2", 1, T - 1)))
            nc.gpsimd.iota(COUNT_I, pattern=[[1, BLOCKS]], base=0, channel_multiplier=0).then_inc(count_ready, 1)
            nc.gpsimd.memset(UPPER, 1.0).then_inc(pool_step, 1)
            nc.gpsimd.memset(ONESP, 1.0).then_inc(pool_step, 1)
            pool.wait_ge(pool_step, 8)
            nc.gpsimd.affine_select(out=UPPER, in_=UPPER, compare_op=ALU.is_gt, fill=0.0, base=0,
                                    pattern=[[1, P]], channel_multiplier=-1).then_inc(tiles_ready, 1)
            pool.wait_ge(slots_zeroed, 16 * BLOCKS)
            pool.wait_ge(routed, 1)
            for t in range(T):
                for c in range(2):
                    pool.indirect_dma_start(out=slot_in[:, :], out_offset=bass.IndirectOffsetOnAxis(ap=SLOT[:, 2 * t + c:2 * t + c + 1], axis=0),
                                            in_=Z[:, t, :], in_offset=None).then_inc(slots_filled, 16)

            def step(b, j, s):
                if not (isinstance(b, int) and b >= BLOCKS):
                    pool.wait_ge(row_loaded[s], 48 * (j + 1))
                    if not (isinstance(b, int) and b < 2):
                        pool.wait_ge(o_drained, b - 1)
                    nc.gpsimd.tensor_tensor(zero[0:1, s:s + 1], zero[0:1, 2:3], zero[0:1, 3:4], ALU.add)
                    nc.gpsimd.partition_broadcast(ROWS[s], ROW1[s], 128).then_inc(rows_spread, 1)
                if not (isinstance(b, int) and b < 2):
                    pool.wait_ge(o_drained, b - 1)
                    pool.dma_start(slot_out[bass.ds((b - 2) * BLOCK, BLOCK), :], OG[s]).then_inc(stored[s], 16)

            pool.wait_ge(vec_drained, RV.count(("so", T - 1)))
            run_blocks(pool, step)
            pool.wait_ge(o_drained, BLOCKS)
            pool.dma_start(slot_out[(BLOCKS - 1) * BLOCK:BLOCKS * BLOCK, :], OG[(BLOCKS - 1) % 2]).then_inc(stored[(BLOCKS - 1) % 2], 16)
            pool.wait_ge(stored[0], 16 * ((BLOCKS + 1) // 2))
            pool.wait_ge(stored[1], 16 * (BLOCKS // 2))
            for t in range(T):
                for c in range(2):
                    pool.indirect_dma_start(out=GOT[:, t, c, :], out_offset=None, in_=slot_out[:, :],
                                            in_offset=bass.IndirectOffsetOnAxis(ap=SLOT[:, 2 * t + c:2 * t + c + 1], axis=0)).then_inc(gathered, 16)


        @block.scalar
        def _(act):
            seen = {}
            steps = [0]

            def wait(s, n):
                if seen.get(s.name, 0) < n:
                    act.wait_ge(s, n)
                    seen[s.name] = n

            drained = [0]

            def fill_of(job):
                assert RA.at[job] == drained[0], (job, drained[0])
                drained[0] += 1
                wait(act_filled, RA.count(job))
                return RA.bank(job)

            def std(n):
                wait(var_ready, n + 1)
                nc.scalar.activation(sd[:, :], mv[:, :, 1], ACT.Sqrt, bias=eps_ln[0:P, :]).then_inc(std_ready, 1)

            def from_column_form(tag, L):
                for c in range(2):
                    n0, n1 = columns(c)
                    for k in (1, 3):
                        b = fill_of((tag, L, c, k))
                        if tag == "y1":
                            g, bb = col("ln1_g", L, k), col("ln1_b", L, k)
                        elif tag == "y2":
                            g, bb = col("ln2_g", L, k), col("ln2_b", L, k)
                        else:
                            g, bb = 1.0, 0.0
                        nc.scalar.activation(YT[:, k, n0:n1], b[:, 0:n1 - n0], ACT.Identity, bias=bb, scale=g)\
                            .then_inc(act_drained, 1)

            std(0)
            wait(vec_drained, RV.count(("cols",)))
            for L in range(LAYERS):
                std(2 * L + 1)
                from_column_form("y1", L)
                for m in range(KD):
                    for c in range(2):
                        n0, n1 = columns(c)
                        b = fill_of(("k", L, m, c))
                        wait(kcol_ready, 1)
                        nc.scalar.activation(KT[:, m, n0:n1], b[:, 0:n1 - n0], ACT.Identity, bias=col("bk", L, m),
                                             scale=QK_NORM if L != GNN else 1.0).then_inc(act_drained, 1)
                if L != GNN:
                    wait(act_drained, RA.count(("k", L, KD - 1, 1)))
                    nc.scalar.activation(SQK, KT, ACT.Square).then_inc(squares_ready, 1)
                    wait(vec_drained, RV.count(("q", L, KD - 1, 1)))
                    nc.scalar.activation(SQQ, QT, ACT.Square).then_inc(squares_ready, 1)

                    for hp in range(H // 2):
                        for tp in range(3):
                            for hh in range(2):
                                h = 2 * hp + hh
                                n = min(2, T - 2 * tp)
                                b = fill_of(("kd", L, h, tp))
                                nc.scalar.copy(KP[:, h, 2 * tp:2 * tp + n, :],
                                               b[0:P, 0:n * NF].rearrange("p (t m) -> p t m", m=NF)).then_inc(act_drained, 1)

                    def q_exp(h):
                        wait(qbias_ready, H * L + h + 1)
                        if h >= 2:
                            wait(vec_filled, RV.count(("qt", L, h - 2, 2)))
                        for tp in range(3):
                            b = fill_of(("qd", L, h, tp))
                            for t in range(2 * tp, min(2 * tp + 2, T)):
                                ins = nc.scalar.activation(QP[h % 2][:, t, :], b[0:P, (t - 2 * tp) * NF:(t - 2 * tp + 1) * NF],
                                                           ACT.Exp, bias=NQ[:, h, t:t + 1])
                            ins.then_inc(act_drained, 1)

                    def k_exp(h):
                        wait(kbias_ready, L + 1)
                        for t in range(T):
                            ins = nc.scalar.activation(KP[:, h, t, :], KP[:, h, t, :], ACT.Exp, bias=NK[:, t, h:h + 1])
                        ins.then_inc(kexp_done, 1)

                    q_exp(0)
                    q_exp(1)
                    for h in range(H):
                        k_exp(h)
                        if h + 2 < H:
                            q_exp(h + 2)
                else:
                    for i in range(T * H + 3):
                        if 0 <= i - 1 < T * H:
                            j = i - 1
                            wait(smax_ready, j + 1)
                            nc.scalar.activation(TS[j % 4], TS[j % 4], ACT.Exp, bias=negmax[:, j % 4:j % 4 + 1])\
                                .then_inc(sexp_done, 1)
                        if 0 <= i - 2 < T * H:
                            j = i - 2
                            if j >= 2:
                                wait(vec_filled, RV.count(("agg", j - 2)))
                            for q, (s0, s1) in enumerate(((0, 4), (4, 5))):
                                b = fill_of(("pt", j, q))
                                nc.scalar.copy(PT[j % 2][:, s0:s1, :], b[0:P, 0:(s1 - s0) * P].rearrange("p (s d) -> p s d", d=P))\
                                    .then_inc(act_drained, 1)
                from_column_form("oT", L)
                std(2 * L + 2)
                from_column_form("y2", L)
                for f in range(FM):
                    if L == 0 and f == 0:
                        wait(prm_step_d, 1)
                        nc.scalar.activation(PRMT[:, 2:4], PRMT[:, 0:2], ACT.Exp).then_inc(prm_step_a, 1)
                        wait(prm_step_a, 1)
                        nc.scalar.activation(PRMT[:, 0:2], PRMT[:, 2:4], ACT.Ln, bias=1.0).then_inc(prm_step_a, 1)
                        wait(prm_done, 1)
                        act.dma_start(act_table[:, :], PRM[:, :]).then_inc(prm_stored, 16)
                        wait(edge_sub_ready, 1)
                        nc.scalar.activation(EA[:, :, :], EA[:, :, :], ACT.Exp).then_inc(edge_exp_ready, 1)
                    for c in range(2):
                        n0, n1 = columns(c)
                        b = fill_of(("h", L, f, c))
                        nc.scalar.activation(HT[:, f, n0:n1], b[:, 0:n1 - n0], ACT.Gelu, bias=col("b1", L, f))\
                            .then_inc(act_drained, 1)
            std(2 * LAYERS + 1)
            from_column_form("yf", 0)
            wait(logits_ready, 1)
            nc.scalar.activation(LOGIT, LOGIT, ACT.Exp).then_inc(gate_exp, 1)
            for t in range(T):
                s = t % 2
                wait(sgate_ready, t + 1)
                nc.scalar.activation(SIG[s][0:P], GC[s][0:P], ACT.Sigmoid, scale=SACT[:, 0:1]).then_inc(ssig_ready, 1)
                b = fill_of(("st", t))
                if t >= 2:
                    wait(vec_filled, RV.count(("so", t - 2)))
                nc.scalar.copy(TET[s].rearrange("p (k n) -> p k n", k=KI)[:, :, 0:P], b[:, 0:KI * P].rearrange("p (k n) -> p k n", k=KI))\
                    .then_inc(act_drained, 1)

            def take_tokens(b, s):
                act.wait_ge(xt_filled, b + 1)
                if not (isinstance(b, int) and b < 2):
                    act.wait_ge(h_filled, b - 1)
                nc.scalar.copy(XGT[s], XT_BANK[s][:, :]).then_inc(xgt_ready, 1)

            def step(b, j, s):
                last = isinstance(b, int) and b >= BLOCKS
                if not last:
                    e = act.value_load(BLKE[0:1, bass.ds(b, 1)], min_val=0, max_val=NE - 1)
                    if not (isinstance(b, int) and b < 2):
                        act.wait_ge(o_filled, b - 1)
                    act.dma_start(EW2[s], A["L0_ffn_expert_w2"][bass.ds(e, 1)].rearrange("o (k p) n -> p (o k) n", p=128))\
                        .then_inc(w2_loaded[s], 16)
                if isinstance(b, int) and b == 0:
                    take_tokens(0, 0)
                if not last and not (isinstance(b, int) and b == BLOCKS - 1):
                    take_tokens(b + 1, 1 - s)
                if not (isinstance(b, int) and b == 0):
                    act.wait_ge(tt_filled, b)
                    if not (isinstance(b, int) and b < 3):
                        act.wait_ge(o_filled, b - 2)
                    nc.scalar.copy(TET[1 - s], TT_BANK[:, 0:NI]).then_inc(tet_ready, 1)
                if not last:
                    act.wait_ge(g_ready, b + 1)
                    nc.scalar.activation(SIG[s], GC[s], ACT.Sigmoid, scale=EACT[s][:, 0:1]).then_inc(sig_ready, 1)

            act.wait_ge(routed, 1)
            act.wait_ge(vec_drained, RV.count(("so", T - 1)))
            run_blocks(act, step)


        @block.vector
        def _(dve):
            seen = {}
            steps = [0]
            drained = [0]
            V = nc.vector

            def wait(s, n):
                if seen.get(s.name, 0) < n:
                    dve.wait_ge(s, n)
                    seen[s.name] = n

            def then(ins):
                steps[0] += 1
                ins.then_inc(vec_step, 1)
                dve.wait_ge(vec_step, steps[0])

            def fill_of(job):
                assert RV.at[job] == drained[0], (job, drained[0])
                drained[0] += 1
                wait(vec_filled, RV.count(job))
                return RV.bank(job)

            def stats(src, t):
                then(V.bn_stats(st[:, t, :], src[:, t, :]))
                return V.bn_aggr(mv[:, t, :], st[:, t, :])

            def normalize(n, src, dst, ready):
                wait(std_ready, n + 1)
                then(V.reciprocal(rstd[:, :], sd[:, :]))
                for t in range(T):
                    V.tensor_scalar(dst[:, t, :], src[:, t, :], mv[:, t, 0:1], rstd[:, t:t + 1], ALU.subtract, ALU.mult)\
                        .then_inc(ready, 1)

            def norm(n, src, dst, ready):
                for t in range(T):
                    ins = stats(src, t)
                ins.then_inc(var_ready, 1)
                normalize(n, src, dst, ready)

            def from_column_form(tag, L):
                for c in range(2):
                    n0, n1 = columns(c)
                    for k in (0, 2):
                        b = fill_of((tag, L, c, k))
                        if tag in ("y1", "y2"):
                            name = "ln1" if tag == "y1" else "ln2"
                            V.tensor_scalar(YT[:, k, n0:n1], b[:, 0:n1 - n0], col(name + "_g", L, k), col(name + "_b", L, k),
                                            ALU.mult, ALU.add).then_inc(vec_drained, 1)
                        else:
                            V.tensor_copy(YT[:, k, n0:n1], b[:, 0:n1 - n0]).then_inc(vec_drained, 1)

            V.memset(eps_ln[:, :], EPS_LN).then_inc(vec_step, 1)
            V.memset(neg1[:, :], -1.0).then_inc(vec_step, 1)
            V.memset(halves[:, :], 0.0).then_inc(vec_step, 1)
            V.memset(V1[:, :, :, DH:DH + 1], 1.0).then_inc(vec_step, 1)
            steps[0] = 4
            dve.wait_ge(vec_step, 4)
            V.memset(halves[0:64, 0:1], 0.5).then_inc(vec_step, 1)
            steps[0] = 5
            then(V.memset(halves[64:128, 1:2], 0.5))

            wait(x_loaded, 16)
            norm(0, Z, XN, xn_ready)
            b = fill_of(("cols",))
            V.tensor_copy(COLS[:, 0:n_cols], b[:, 0:n_cols]).then_inc(vec_drained, 1)
            b = fill_of(("proj",))
            V.tensor_copy(PROJ[:, :, :].rearrange("p l m -> p (l m)"), b[:, :]).then_inc(vec_drained, 1)
            wait(vec_drained, drained[0])
            c0 = col_at["bk", 0]
            V.tensor_scalar(COLS[:, c0:c0 + 2 * KD], COLS[:, c0:c0 + 2 * KD], QK_NORM, None, ALU.mult).then_inc(kcol_ready, 1)
            wait(xn_ready, T)

            wait(consts_ready, 1)
            then(V.tensor_copy(spare[:, :], spare_i[:, :]))
            def edge_same(g):
                b = fill_of(("keys", g))
                rows = b[0:P, 0:EG * P].rearrange("p (j q) -> p j q", j=EG)
                V.tensor_tensor(SAME[g % 2], rows, key[:, g * EG:(g + 1) * EG].unsqueeze(2).to_broadcast([P, EG, P]),
                                ALU.is_equal).then_inc(vec_drained, 1)
                wait(vec_drained, drained[0])
                then(V.tensor_tensor(SAMEL[g % 2], SAME[g % 2], lower[:, :].unsqueeze(1).to_broadcast([P, EG, P]), ALU.mult))
                V.tensor_reduce(before[:, g * EG:(g + 1) * EG], SAMEL[g % 2], AX_X, ALU.add).then_inc(vec_step, 1)
                steps[0] += 1

            def edge_take(g):
                b = fill_of(("sums", g))
                V.tensor_copy(VC[:, g * EG:(g + 1) * EG, :], b[0:P, 0:EG * H].rearrange("p (j h) -> p j h", j=EG))\
                    .then_inc(vec_drained, 1)

            for L in range(LAYERS):
                src = MX if L == 1 else XN
                if L != 1:
                    norm(2 * L + 1, src, Z, z_ready)
                else:
                    normalize(2 * L + 1, src, Z, z_ready)
                wait(z_ready, 10 * L + 5)
                dst = XN if L == GNN else MX
                if L == GNN:
                    wait(rowb_again, 16 * 3)
                else:
                    wait(rowb_loaded, 16 * 6)
                resid = V.tensor_tensor(dst[:, :, :], src[:, :, :], ROWB[:, L % 2, 1, :].unsqueeze(1).to_broadcast([P, T, D]), ALU.add)
                resid.then_inc(vec_step, 1)
                steps[0] += 1
                resid_step = steps[0]
                from_column_form("y1", L)
                for m in range(KD):
                    for c in range(2):
                        n0, n1 = columns(c)
                        b = fill_of(("q", L, m, c))
                        V.tensor_scalar(QT[:, m, n0:n1], b[:, 0:n1 - n0], col("bq", L, m), QK_NORM if L != GNN else GNN_SCALE,
                                        ALU.add, ALU.mult).then_inc(vec_drained, 1)
                for t in range(T):
                    b = fill_of(("v", L, t))
                    V.tensor_tensor(V1[:, t, :, 0:DH], b[0:P, :].rearrange("p (h d) -> p h d", h=H),
                                    ROWB[:, L % 2, 0, :].rearrange("p (h d) -> p h d", h=H), ALU.add).then_inc(vec_drained, 1)
                if L == 0:
                    wait(edges_loaded, 32)
                    V.tensor_copy(key[:, :], dst_i[:, :]).then_inc(vec_step, 1)
                    steps[0] += 1
                    then(V.tensor_copy(srcf[:, :], src_i[:, :]))
                    then(V.scalar_tensor_tensor(out=key[:, :], in0=key[:, :], scalar=float(N), in1=srcf[:, :], op0=ALU.mult, op1=ALU.add))
                    wait(attrs_loaded, 32)
                    then(V.tensor_tensor(EA[:, :, :], EA[:, :, :], EA2[:, :, :], ALU.add))
                    V.tensor_reduce(emax[:, :], EA[:, :, :].rearrange("p j h -> p h j"), AX_X, ALU.max).then_inc(edge_max_part, 1)
                if L != GNN:
                    b = fill_of(("diag", L))
                    V.tensor_copy(DG[:, :, :, :], b[0:P, 0:T * 2 * H].rearrange("p (t q h) -> p t q h", t=T, q=2)).then_inc(vec_drained, 1)
                    for h in range(H):
                        wait(act_drained, RA.count(("kd", L, h, 2)))
                        V.tensor_reduce(KM[:, h:h + 1], KP[:, h, :, :], mybir.AxisListType.XY, ALU.max).then_inc(kmax_part, 1)

                    def q_max(h):
                        for tp in range(3):
                            job = ("qd", L, h, tp)
                            wait(act_filled, RA.count(job))
                            n = min(2, T - 2 * tp)
                            V.tensor_reduce(QM[:, h, 2 * tp:2 * tp + n],
                                            RA.bank(job)[0:P, 0:n * NF].rearrange("p (t m) -> p t m", m=NF), AX_X, ALU.max)\
                                .then_inc(vec_step, 1)
                            steps[0] += 1
                        dve.wait_ge(vec_step, steps[0])
                        V.scalar_tensor_tensor(out=NQ[:, h, :], in0=QM[:, h, :], scalar=-1.0, in1=DG[:, :, 0, h],
                                               op0=ALU.mult, op1=ALU.subtract).then_inc(qbias_ready, 1)

                    wait(vec_drained, drained[0])
                    q_max(0)
                    q_max(1)
                    b = fill_of(("kmax", L))
                    V.tensor_reduce(KMH[:, :], b[0:H, 0:P], AX_X, ALU.max).then_inc(vec_drained, 1)
                    wait(vec_drained, drained[0])
                    V.tensor_scalar(KDIAG[:, :], ident[0:H, 0:H], KMH[:, 0:1], None, ALU.mult).then_inc(kdiag_ready, 1)
                    b = fill_of(("kmax_all", L))
                    V.tensor_copy(KMA[:, :], b[0:P, 0:H]).then_inc(vec_drained, 1)
                    wait(vec_drained, drained[0])
                    V.scalar_tensor_tensor(out=NK[:, :, :], in0=DG[:, :, 1, :], scalar=-1.0,
                                           in1=KMA[:, :].unsqueeze(1).to_broadcast([P, T, H]),
                                           op0=ALU.mult, op1=ALU.subtract).then_inc(kbias_ready, 1)

                    def take_o(h):
                        b = fill_of(("o", L, h))
                        o = b[0:P, 0:T * (DH + 1)].rearrange("p (t e) -> p t e", t=T)
                        then(V.reciprocal(REC[:, h % 2, :], o[:, :, DH]))
                        V.tensor_tensor(O[:, :, h * DH:(h + 1) * DH], o[:, :, 0:DH],
                                        REC[:, h % 2, :].unsqueeze(2).to_broadcast([P, T, DH]), ALU.mult).then_inc(vec_drained, 1)

                    for h in range(H):
                        if h + 2 < H:
                            q_max(h + 2)
                        wait(kexp_done, H * L + h + 1)
                        V.tensor_scalar(KP[:, h, :, :], KP[:, h, :, :], EPS_RF, None, ALU.add).then_inc(kp_ready, 1)
                        for i in range(3):
                            b = fill_of(("qt", L, h, i))
                            n = min(500, 2 * N - 500 * i)
                            V.tensor_scalar(QPT[h % 2][:, 500 * i:500 * i + n], b[:, 0:n], EPS_RF, None, ALU.add).then_inc(vec_drained, 1)
                        b = fill_of(("ctx", L, h))
                        V.tensor_copy(CTX[:, h % 2, :, :], b[:, 0:2 * (DH + 1)].rearrange("p (m e) -> p m e", m=2)).then_inc(vec_drained, 1)
                        if h:
                            take_o(h - 1)
                    take_o(H - 1)
                else:
                    for i in range(T * H + 3):
                        if i < T * H:
                            dt, h = divmod(i, H)
                            if h == 0:
                                wait(pairw_loaded[dt % 2], 16 * (dt // 2 + 1))
                                then(V.tensor_reduce(NEG[dt % 2], PAIRW[dt % 2], AX_X, ALU.max))
                                then(V.tensor_scalar(NEG[dt % 2], NEG[dt % 2], 0.0, MASK, ALU.is_equal, ALU.mult))
                            if i >= 4:
                                wait(act_filled, RA.count(("pt", i - 4, 1)))
                            for c in range(2):
                                n0, n1 = columns(c)
                                b = fill_of(("s", i, c))
                                V.tensor_tensor_reduce(out=TS[i % 4][:, n0:n1], in0=b[0:P, 0:n1 - n0], in1=NEG[dt % 2][:, n0:n1],
                                                       scale=1.0, scalar=-3e38, op0=ALU.add, op1=ALU.max,
                                                       accum_out=pairmax[:, i % 4, c:c + 1]).then_inc(vec_drained, 1)
                            wait(vec_drained, drained[0])
                            V.scalar_tensor_tensor(out=negmax[:, i % 4:i % 4 + 1], in0=pairmax[:, i % 4, 0:1],
                                                   scalar=pairmax[:, i % 4, 1:2], in1=neg1[:, :], op0=ALU.max, op1=ALU.mult)\
                                .then_inc(smax_ready, 1)
                        if 0 <= i - 1 < T * H:
                            j = i - 1
                            dt, h = divmod(j, H)
                            wait(sexp_done, j + 1)
                            V.tensor_tensor_reduce(out=TS[j % 4], in0=TS[j % 4], in1=PAIRW[dt % 2][:, :, h], scale=1.0, scalar=0.0,
                                                   op0=ALU.mult, op1=ALU.add, accum_out=den[:, j % 4:j % 4 + 1]).then_inc(p_ready, 1)
                        if 0 <= i - 3 < T * H:
                            j = i - 3
                            dt, h = divmod(j, H)
                            wait(p_ready, j + 1)
                            then(V.tensor_scalar(rden[:, j % 4:j % 4 + 1], den[:, j % 4:j % 4 + 1], 1e-37, None, ALU.max))
                            then(V.reciprocal(rden[:, j % 4:j % 4 + 1], rden[:, j % 4:j % 4 + 1]))
                            b = fill_of(("agg", j))
                            V.tensor_scalar(O[:, dt, h * DH:(h + 1) * DH], b[0:P, 0:DH], rden[:, j % 4:j % 4 + 1], None, ALU.mult)\
                                .then_inc(vec_drained, 1)
                from_column_form("oT", L)
                dve.wait_ge(vec_step, resid_step)
                for t in range(T):
                    b = fill_of(("x1", L, t))
                    V.tensor_tensor(dst[:, t, :], b[0:P, :], dst[:, t, :], ALU.add).then_inc(vec_drained, 1)
                    wait(vec_drained, drained[0])
                    ins = stats(dst, t)
                ins.then_inc(var_ready, 1)
                normalize(2 * L + 2, dst, Z, z_ready)
                wait(z_ready, 10 * L + 10)
                resid = V.tensor_tensor(dst[:, :, :], dst[:, :, :], ROWB[:, L % 2, 2, :].unsqueeze(1).to_broadcast([P, T, D]), ALU.add)
                resid.then_inc(vec_step, 1)
                steps[0] += 1
                if L == GNN:
                    dve.wait_ge(vec_step, steps[0])
                    then(V.tensor_tensor(dst[:, :, :], dst[:, :, :], MX[:, :, :], ALU.add))
                    wait(x_again, 16)
                    V.tensor_tensor(dst[:, :, :], dst[:, :, :], XAGAIN, ALU.add).then_inc(vec_step, 1)
                    steps[0] += 1
                resid_step = steps[0]
                from_column_form("y2", L)
                if L == 0:
                    wait(prm_in, 32)
                    V.scalar_tensor_tensor(out=PRMT[:, 0:2], in0=PRM[:, 3:5], scalar=-1.0, in1=PRM[:, 3:5], op0=ALU.mult, op1=ALU.min).then_inc(prm_step_d, 1)
                    wait(prm_step_a, 2)
                    then(V.scalar_tensor_tensor(out=PRM[:, 3:5], in0=PRM[:, 3:5], scalar=0.0, in1=PRMT[:, 0:2], op0=ALU.max, op1=ALU.add))
                    then(V.memset(PRM[:, 7:8], 0.0))
                    V.tensor_scalar(PRM[:, 5:7], PRM[:, 3:5], -1.0, None, ALU.mult).then_inc(prm_done, 1)
                if L == 0:
                    wait(edge_max_all, 1)
                    V.tensor_tensor(EA[:, :, :], EA[:, :, :], emaxa[:, :].unsqueeze(1).to_broadcast([P, EB, H]), ALU.subtract)\
                        .then_inc(edge_sub_ready, 1)
                    for g in range(EB // EG):
                        edge_same(g)
                        if g:
                            edge_take(g - 1)
                    edge_take(EB // EG - 1)
                    dve.wait_ge(vec_step, steps[0])
                    then(V.tensor_scalar(before[:, :], before[:, :], 1.0, None, ALU.min))
                    then(V.scalar_tensor_tensor(out=srcf[:, :], in0=key[:, :], scalar=-1.0, in1=spare[:, 0:1].to_broadcast([P, EB]),
                                                op0=ALU.mult, op1=ALU.add))
                    then(V.tensor_tensor(srcf[:, :], srcf[:, :], before[:, :], ALU.mult))
                    then(V.tensor_tensor(srcf[:, :], srcf[:, :], key[:, :], ALU.add))
                    wait(vec_drained, drained[0])
                    V.tensor_copy(idx[:, :], srcf[:, :]).then_inc(idx_ready, 1)
                dve.wait_ge(vec_step, resid_step)
                for t in range(T):
                    b = fill_of(("x2", L, t))
                    V.tensor_tensor(dst[:, t, :], b[0:P, :], dst[:, t, :], ALU.add).then_inc(vec_drained, 1)
                    if L != 1:
                        wait(vec_drained, drained[0])
                        ins = stats(dst, t)
                if L != 1:
                    ins.then_inc(var_ready, 1)
            normalize(2 * LAYERS + 1, XN, Z, z_ready)
            wait(count_ready, 1)
            then(V.tensor_copy(COUNT, COUNT_I))
            V.tensor_scalar(THRESH, COUNT[:, 0:5], float(BLOCK), None, ALU.mult).then_inc(vec_step, 1)
            steps[0] += 1
            then(V.tensor_tensor(UPTO, COUNT[:, 0:NE].unsqueeze(1).to_broadcast([P, NE, NE]),
                                 COUNT[:, 0:NE].unsqueeze(2).to_broadcast([P, NE, NE]), ALU.is_le))
            from_column_form("yf", 0)
            b = fill_of(("gate",))
            wait(ffn_b_loaded, 16 * 4)
            V.tensor_tensor(LOGIT, b[0:P, 0:T * NE].rearrange("p (t e) -> p t e", t=T),
                            GATEB.unsqueeze(1).to_broadcast([P, T, NE]), ALU.add).then_inc(vec_drained, 1)
            wait(vec_drained, drained[0])
            then(V.tensor_reduce(LMAX, LOGIT, AX_X, ALU.max))
            V.tensor_tensor(LOGIT, LOGIT, LMAX.unsqueeze(2).to_broadcast([P, T, NE]), ALU.subtract).then_inc(logits_ready, 1)

            def shared_gate(t):
                s = t % 2
                h0 = fill_of(("sh", t, 0))
                hb = HB[s][0:P]
                V.tensor_tensor(hb[:, 0:NI], h0[0:P, 0:NI], SB1[:, 0:NI], ALU.add).then_inc(vec_drained, 1)
                h1 = fill_of(("sh", t, 1))
                V.tensor_tensor(hb[:, NI:2 * NI], h1[0:P, 0:NI], SB1[:, NI:2 * NI], ALU.add).then_inc(vec_drained, 1)
                wait(vec_drained, drained[0])
                gu = hb.rearrange("p (n c) -> p n c", c=2)
                V.tensor_scalar(GC[s][0:P], gu[:, :, 0], SACT[:, 3:4], SACT[:, 5:6], ALU.min, ALU.max).then_inc(sgate_ready, 1)
                wait(sgate_ready, t + 1)
                then(V.tensor_scalar(UC[s][0:P], gu[:, :, 1], SACT[:, 4:5], SACT[:, 6:7], ALU.min, ALU.max))
                then(V.scalar_tensor_tensor(out=UC[s][0:P], in0=UC[s][0:P], scalar=SACT[:, 2:3], in1=GC[s][0:P], op0=ALU.add, op1=ALU.mult))

            def shared_te(t):
                s = t % 2
                wait(ssig_ready, t + 1)
                if t >= 2:
                    wait(act_filled, RA.count(("st", t - 2)))
                V.scalar_tensor_tensor(out=TE[s][0:P], in0=UC[s][0:P], scalar=SACT[:, 1:2], in1=SIG[s][0:P], op0=ALU.mult, op1=ALU.mult)\
                    .then_inc(ste_ready, 1)

            shared_gate(0)
            wait(gate_exp, 1)
            then(V.tensor_reduce(LSUM, LOGIT, AX_X, ALU.add))
            then(V.reciprocal(LSUM, LSUM))
            then(V.tensor_tensor(LOGIT, LOGIT, LSUM.unsqueeze(2).to_broadcast([P, T, NE]), ALU.mult))
            for t in range(T):
                V.max(TOP[:, t, :], LOGIT[:, t, :]).then_inc(vec_step, 1)
                steps[0] += 1
            dve.wait_ge(vec_step, steps[0])
            for t in range(T):
                V.max_index(TOPI[:, t, :], TOP[:, t, :], LOGIT[:, t, :]).then_inc(vec_step, 1)
                steps[0] += 1
            then(V.tensor_tensor(LSUM, TOP[:, :, 0], TOP[:, :, 1], ALU.add))
            then(V.reciprocal(LSUM, LSUM))
            then(V.tensor_tensor(CW, TOP[:, :, 0:2], LSUM.unsqueeze(2).to_broadcast([P, T, 2]), ALU.mult))
            then(V.tensor_copy(TOPF, TOPI[:, :, 0:2]))
            for t in range(T):
                V.tensor_tensor(PICK[:, t], COUNT[:, 0:NE].unsqueeze(1).to_broadcast([P, 2, NE]),
                                TOPF[:, t].unsqueeze(2).to_broadcast([P, 2, NE]), ALU.is_equal).then_inc(vec_step, 1)
                steps[0] += 1
            dve.wait_ge(vec_step, steps[0])
            V.tensor_tensor(PICKED, PICK[:, :, 0, :], PICK[:, :, 1, :], ALU.add).then_inc(picked_ready, 1)
            b = fill_of(("rank",))
            V.tensor_copy(RANK, b[0:P, 0:(T + 1) * NE].rearrange("p (t e) -> p t e", t=T + 1)).then_inc(vec_drained, 1)
            wait(vec_drained, drained[0])
            c5 = CMP[:, 0:NE * 5].rearrange("p (e j) -> p e j", j=5)
            then(V.tensor_tensor(c5, RANK[:, T, :].unsqueeze(2).to_broadcast([P, NE, 5]), THRESH.unsqueeze(1).to_broadcast([P, NE, 5]), ALU.is_gt))
            then(V.tensor_reduce(NBLK, c5, AX_X, ALU.add))
            c16 = CMP[:, 0:NE * NE].rearrange("p (a b) -> p a b", a=NE)
            then(V.tensor_tensor(c16, NBLK.unsqueeze(1).to_broadcast([P, NE, NE]), UPTO, ALU.mult))
            then(V.tensor_reduce(UPBLK, c16, AX_X, ALU.add))
            then(V.tensor_tensor(BASE, UPBLK, NBLK, ALU.subtract))
            then(V.scalar_tensor_tensor(out=RANK[:, 0:T, :], in0=BASE.unsqueeze(1).to_broadcast([P, T, NE]), scalar=float(BLOCK),
                                        in1=RANK[:, 0:T, :], op0=ALU.mult, op1=ALU.add))
            for c in range(2):
                V.tensor_tensor(PICK[:, :, c, :], PICK[:, :, c, :], RANK[:, 0:T, :], ALU.mult).then_inc(vec_step, 1)
                steps[0] += 1
            dve.wait_ge(vec_step, steps[0])
            then(V.tensor_reduce(SLOTF, PICK.rearrange("p t c e -> p (t c) e"), AX_X, ALU.add))
            then(V.tensor_copy(SLOT, SLOTF))
            cb = CMP[:, 0:BLOCKS * NE].rearrange("p (a b) -> p a b", a=BLOCKS)
            then(V.tensor_tensor(cb, UPBLK.unsqueeze(1).to_broadcast([P, BLOCKS, NE]),
                                 COUNT.unsqueeze(2).to_broadcast([P, BLOCKS, NE]), ALU.is_le))
            then(V.tensor_reduce(BLKF, cb, AX_X, ALU.add))
            V.tensor_scalar(BLKE, BLKF, float(NE - 1), None, ALU.min).then_inc(routed, 1)
            then(V.tensor_tensor(MX[:, :, :], XN[:, :, :], SB2.unsqueeze(1).to_broadcast([P, T, D]), ALU.add))
            shared_te(0)
            for t in range(T):
                if t + 1 < T:
                    shared_gate(t + 1)
                    shared_te(t + 1)
                b = fill_of(("so", t))
                V.tensor_tensor(MX[:, t, :], b[0:P, :], MX[:, t, :], ALU.add).then_inc(vec_drained, 1)

            def step(b, j, s):
                last = isinstance(b, int) and b >= BLOCKS
                if not last:
                    dve.wait_ge(h_filled, b + 1)
                    dve.wait_ge(rows_spread, b + 1)
                    V.tensor_tensor(HB[s][:, 0:NI], H_BANK[s][0][:, 0:NI], EB1[s][:, 0:NI], ALU.add)
                    V.tensor_tensor(HB[s][:, NI:2 * NI], H_BANK[s][1][:, 0:NI], EB1[s][:, NI:2 * NI], ALU.add).then_inc(h_drained, 1)
                    dve.wait_ge(h_drained, b + 1)
                    gu = HB[s].rearrange("p (n c) -> p n c", c=2)
                    V.tensor_scalar(GC[s], gu[:, :, 0], EACT[s][:, 3:4], EACT[s][:, 5:6], ALU.min, ALU.max).then_inc(g_ready, 1)
                    V.tensor_scalar(UC[s], gu[:, :, 1], EACT[s][:, 4:5], EACT[s][:, 6:7], ALU.min, ALU.max).then_inc(u_ready, 1)
                    dve.wait_ge(g_ready, b + 1)
                    dve.wait_ge(u_ready, b + 1)
                    V.scalar_tensor_tensor(out=UC[s], in0=UC[s], scalar=EACT[s][:, 2:3], in1=GC[s], op0=ALU.add, op1=ALU.mult).then_inc(gu_ready, 1)
                if not (isinstance(b, int) and b == 0):
                    q = 1 - s
                    dve.wait_ge(o_filled, b)
                    if not (isinstance(b, int) and b < 3):
                        dve.wait_ge(stored[q], 16 * (j + s - 1))
                    V.tensor_tensor(OG[q], O_BANK[:, :], EB2[q], ALU.add).then_inc(o_drained, 1)
                if not last:
                    dve.wait_ge(sig_ready, b + 1)
                    dve.wait_ge(gu_ready, b + 1)
                    if not (isinstance(b, int) and b < 2):
                        dve.wait_ge(tt_filled, b - 1)
                    V.scalar_tensor_tensor(out=TE[s], in0=UC[s], scalar=EACT[s][:, 1:2], in1=SIG[s], op0=ALU.mult, op1=ALU.mult).then_inc(te_ready, 1)

            run_blocks(dve, step)
            dve.wait_ge(gathered, 16 * 2 * T)
            for t in range(T):
                then(V.scalar_tensor_tensor(out=MX[:, t, :], in0=GOT[:, t, 0, :], scalar=CW[:, t, 0:1], in1=MX[:, t, :], op0=ALU.mult, op1=ALU.add))
                V.scalar_tensor_tensor(out=MX[:, t, :], in0=GOT[:, t, 1, :], scalar=CW[:, t, 1:2], in1=MX[:, t, :], op0=ALU.mult, op1=ALU.add)\
                    .then_inc(y_ready, 1)


_OUTS = [((625, 512), "float32")]


def kernel(**inputs):
    import numpy as _np
    import concourse.bacc as _bacc
    from concourse import mybir as _mybir
    from concourse.bass_utils import run_bass_kernel_spmd as _run

    nc = _bacc.Bacc("TRN2", target_bir_lowering=False, num_devices=1)
    arrays, aps = {}, {}
    for name in inputs:
        a = _np.ascontiguousarray(inputs[name])
        arrays[f"in_{name}_dram"] = a
        aps[name] = nc.dram_tensor(f"in_{name}_dram", a.shape, _mybir.dt.from_np(a.dtype), kind="ExternalInput").ap()
    outs = [nc.dram_tensor(f"out_{i}_dram", shape, _mybir.dt.from_np(_np.dtype(dtype)), kind="ExternalOutput").ap()
            for i, (shape, dtype) in enumerate(_OUTS)]
    gps_layer(nc, aps, *outs)
    r = _run(nc, [arrays], core_ids=[0])
    got = tuple(r.results[0][f"out_{i}_dram"] for i in range(len(_OUTS)))
    return got[0]
```

```python
from contextlib import ExitStack

import concourse.bass as bass
from concourse import mybir

ALU = mybir.AluOpType
ACT = mybir.ActivationFunctionType
F32 = mybir.dt.float32
I32 = mybir.dt.int32
U32 = mybir.dt.uint32
BF16 = mybir.dt.bfloat16
AX_X = mybir.AxisListType.X
RMAX = bass.bass_isa.ReduceOp.max

P, T = 125, 5
N = P * T
D, KD = 512, 4
H, DH = 8, 64
FF, FM = 2048, 16
NF = 256
NE, NI, KI = 16, 384, 3
LAYERS = 3
GNN = 2
EDGES = 10000
EB = EDGES // P
EG = 4
PAIRS = N * N
BLOCK = 128
BLOCKS = (2 * N + NE * (BLOCK - 1)) // BLOCK
CHUNKS = [(0, 3), (3, 5)]
QK_NORM = float(DH) ** -0.25
GNN_SCALE = float(D) ** -0.5
EPS_LN = 1e-5
EPS_RF = 1e-4
MASK = -1e30
WSLOTS = 6
WPER = 12


class Ring:

    def __init__(self, banks, filled, drained):
        self.banks, self.filled, self.drained, self.at = banks, filled, drained, {}

    def add(self, job):
        assert job not in self.at, job
        self.at[job] = len(self.at)
        return self.at[job]

    def bank(self, job):
        return self.banks[self.at[job] % len(self.banks)]

    def count(self, job):
        return self.at[job] + 1


def columns(c):
    t0, t1 = CHUNKS[c]
    return t0 * P, t1 * P


def gps_layer(nc, A, out):
    ctx = ExitStack()
    with ctx:
        def sb(name, shape, dt=F32):
            return ctx.enter_context(nc.sbuf_tensor(name, shape, dt))

        def sem(name):
            return ctx.enter_context(nc.semaphore(name))

        pair_table = nc.dram_tensor("pair_table", (PAIRS + 128, H), F32, kind="Internal").ap()
        slot_in = nc.dram_tensor("slot_in", (BLOCKS * BLOCK, D), F32, kind="Internal").ap()
        slot_out = nc.dram_tensor("slot_out", (BLOCKS * BLOCK, D), F32, kind="Internal").ap()
        act_table = nc.dram_tensor("act_table", (NE + 1, 8), F32, kind="Internal").ap()

        XN = sb("XN", [P, T, D])
        MX = sb("MX", [P, T, D])
        ZB = sb("ZB", [128, T * D])
        Z = ZB[0:P, :].rearrange("p (t d) -> p t d", t=T)
        YT = sb("YT", [128, KD, N])
        QK = sb("QK", [128, 2, KD, N])
        V1 = sb("V1", [P, T, H, DH + 1])
        ARENA = sb("ARENA", [128, 10240])
        W = sb("W", [128, WSLOTS, KD * 512])
        ROWB = sb("ROWB", [P, 2, 3, D])
        EXPB = sb("EXPB", [128, 2560])
        TRB = sb("TRB", [128, 2 * 1250])
        PROJ = sb("PROJ", [128, 2, 2, NF])
        KMA = sb("KMA", [P, H])
        spare_i = sb("spare_i", [P, 1], I32)
        spare = sb("spare", [P, 1])
        CTX = sb("CTX", [128, 2, 2, DH + 1])
        ident = sb("ident", [128, 128])
        lower = sb("lower", [P, P])
        zero = sb("zero", [128, 625])
        halves = sb("halves", [128, KD, H])
        COLS = sb("COLS", [128, 120])
        st = sb("st", [P, T, 6])
        mv = sb("mv", [P, T, 2])
        sd = sb("sd", [P, T])
        rstd = sb("rstd", [P, T])
        eps_ln = sb("eps_ln", [128, 1])
        DG = sb("DG", [P, T, 2, H])
        KM = sb("KM", [P, H])
        KMH = sb("KMH", [H, 1])
        KDIAG = sb("KDIAG", [H, H])
        ones = sb("ones", [H, 128])
        NK = sb("NK", [P, T, H])
        QM = sb("QM", [P, H, T])
        NQ = sb("NQ", [P, H, T])
        REC = sb("REC", [P, 2, T])
        src_i = sb("src_i", [P, EB], I32)
        dst_i = sb("dst_i", [P, EB], I32)
        key = sb("key", [P, EB])
        srcf = sb("srcf", [P, EB])
        EA = sb("EA", [P, EB, H])
        EA2 = sb("EA2", [P, EB, H])
        VC = EA2
        before = sb("before", [P, EB])
        idx = sb("idx", [P, EB], U32)
        emax = sb("emax", [P, H])
        emaxa = sb("emaxa", [P, H])
        pairmax = sb("pairmax", [P, 4, 2])
        negmax = sb("negmax", [P, 4])
        den = sb("den", [P, 4])
        rden = sb("rden", [P, 4])
        neg1 = sb("neg1", [P, 1])

        YTFREE = YT[:, :, :].rearrange("p k n -> p (k n)")
        OCOL = YTFREE[0:DH + 1, 0:2 * N].rearrange("p (s n) -> p s n", s=2)
        DGT = OCOL[0:H, :, :]
        CTXT = YTFREE[0:DH + 1, 2 * N:2 * N + 2 * NF].rearrange("p (s n) -> p s n", s=2)
        PROJR = EXPB[:, 0:512].rearrange("p (l a c d) -> p l a c d", l=2, a=2, c=2)
        VROWS = EXPB[:, 512:640]
        KP = ARENA[0:P, :].rearrange("p (h t m) -> p h t m", h=H, t=T)
        HT = ARENA[:, 0:FM * N].rearrange("p (f n) -> p f n", f=FM)
        SQQ = ZB[:, 0:KD * N].rearrange("p (k n) -> p k n", k=KD)
        SQK = EXPB[:, 0:KD * N].rearrange("p (k n) -> p k n", k=KD)
        QP = EXPB[0:P, :].rearrange("p (c t m) -> p c t m", c=2, t=T)
        QPT = [TRB[:, s * 1250:(s + 1) * 1250] for s in range(2)]
        O = Z
        XAGAIN = QK[0:P].rearrange("p a k n -> p (a k n)")[:, 0:T * D].rearrange("p (t d) -> p t d", t=T)
        QT, KT = QK[:, 0], QK[:, 1]
        PAIRW = [ARENA[0:P, s * 5000:(s + 1) * 5000].rearrange("p (s h) -> p s h", h=H) for s in range(2)]
        QODD = YT
        AGG = ZB[:, 0:KD * N].rearrange("p (k n) -> p k n", k=KD)
        TS = [EXPB[0:P, s * 625:(s + 1) * 625] for s in range(4)]
        PT = [TRB[0:P, s * 625:(s + 1) * 625].rearrange("p (s d) -> p s d", s=T) for s in range(2)]
        NEG = [TRB[0:P, 1250 + s * 625:1250 + (s + 1) * 625] for s in range(2)]
        SAME = [EXPB[0:P, s * 250:(s + 1) * 250].bitcast(BF16).rearrange("p (j q) -> p j q", j=EG) for s in range(2)]
        EAP = EXPB[0:P, 500:500 + 960].bitcast(BF16).rearrange("p (j c h) -> p j c h", j=EB, c=3)
        EAR = EXPB[0:P, 1460:1460 + 640].rearrange("p (j h) -> p j h", j=EB)
        SAMEL = [TRB[0:P, s * 500:(s + 1) * 500].rearrange("p (j q) -> p j q", j=EG) for s in range(2)]

        banks = [ctx.enter_context(nc.psum_tensor(f"bank{i}", [128, 512], F32)) for i in range(8)]

        act_filled, act_drained = sem("act_filled"), sem("act_drained")
        vec_filled, vec_drained = sem("vec_filled"), sem("vec_drained")
        RA = Ring(banks[0:4], act_filled, act_drained)
        RV = Ring(banks[4:8], vec_filled, vec_drained)

        vec_step, act_step, pool_step = sem("vec_step"), sem("act_step"), sem("pool_step")
        x_loaded, rows_loaded, rowb_loaded, rowb_again = sem("x_loaded"), sem("rows_loaded"), sem("rowb_loaded"), sem("rowb_again")
        edges_loaded, attrs_loaded = sem("edges_loaded"), sem("attrs_loaded")
        proj_loaded = sem("proj_loaded")
        consts_ready, zero_ready = sem("consts_ready"), sem("zero_ready")
        table_zeroed, slots_zeroed = sem("table_zeroed"), sem("slots_zeroed")
        w_loaded = [sem(f"w_loaded{i}") for i in range(WSLOTS)]
        var_ready, std_ready, xn_ready, z_ready = sem("var_ready"), sem("std_ready"), sem("xn_ready"), sem("z_ready")
        resid_ready = sem("resid_ready")
        squares_ready = sem("squares_ready")
        kmax_part, kdiag_ready, kbias_ready, qbias_ready = sem("kmax_part"), sem("kdiag_ready"), sem("kbias_ready"), sem("qbias_ready")
        kexp_done, kcol_ready, kp_ready = sem("kexp_done"), sem("kcol_ready"), sem("kp_ready")
        edge_attr_ready, edge_max_part, edge_max_all = sem("edge_attr_ready"), sem("edge_max_part"), sem("edge_max_all")
        edge_sub_ready, edge_exp_ready, edge_parts_ready, idx_ready = sem("edge_sub_ready"), sem("edge_exp_ready"), sem("edge_parts_ready"), sem("idx_ready")
        scattered = sem("scattered")
        pairw_loaded = [sem(f"pairw_loaded{i}") for i in range(2)]
        smax_ready, sexp_done, p_ready = sem("smax_ready"), sem("sexp_done"), sem("p_ready")
        queries_apart, rden_ready, p_scaled, proj_zeroed = sem("queries_apart"), sem("rden_ready"), sem("p_scaled"), sem("proj_zeroed")
        x_again = sem("x_again")

        WFREE = W[:, :, :].rearrange("p s n -> p (s n)")
        SW1 = WFREE[:, 0:KD * 2 * NI].rearrange("p (k n) -> p k n", k=KD)
        GATEW = WFREE[:, 3072:3136].rearrange("p (k e) -> p k e", k=KD)
        SB1 = WFREE[0:P, 3136:3904]
        QKFREE = QK[:, :, :, :].rearrange("p a k n -> p (a k n)")
        SW2 = QKFREE[:, 2560:4096].rearrange("p (k n) -> p k n", k=KI)
        SB2 = QKFREE[0:P, 4096:4608]
        GATEB = QKFREE[0:P, 4608:4624]
        SACT = QKFREE[0:P, 4624:4632]
        EW1 = [ARENA[:, s * 4608:s * 4608 + 3072].rearrange("p (k n) -> p k n", k=KD) for s in range(2)]
        EW2 = [ARENA[:, s * 4608 + 3072:(s + 1) * 4608].rearrange("p (k n) -> p k n", k=KI) for s in range(2)]

        def pair_of(base, size):
            return [WFREE[:, base + s * size:base + (s + 1) * size] for s in range(2)]

        XG, XGT = pair_of(4096, 512), pair_of(5120, 512)
        HB, GC, TE, TET = pair_of(6144, 768), pair_of(7680, 384), pair_of(8448, 384), pair_of(9216, 384)
        UC = pair_of(11520, 384)
        ROW1 = [QKFREE[0:1, s * 1288:(s + 1) * 1288] for s in range(2)]
        ROWS = [WFREE[:, 9984:9984 + 1288], QKFREE[:, 2576:2576 + 1288]]
        EB1, EB2, EACT = [r[:, 0:768] for r in ROWS], [r[:, 768:1280] for r in ROWS], [r[:, 1280:1288] for r in ROWS]
        OG = [EXPB[:, s * 512:(s + 1) * 512] for s in range(2)]
        SIG = [EXPB[:, 1024 + s * 384:1408 + s * 384] for s in range(2)]
        UPPER, ONESP = ROWB[:, 1, 0, 0:P], ROWB[:, 1, 1, 0:P]
        COUNT_I = ROWB[:, 1, 2, 0:BLOCKS].bitcast(I32)
        COUNT = ROWB[:, 1, 2, 32:32 + BLOCKS]
        THRESH = ROWB[:, 1, 2, 64:69]
        UPTO = ROWB[:, 1, 2, 128:384].rearrange("p (a b) -> p a b", a=NE)
        TR = TRB[0:P, :]
        LOGIT = TR[:, 0:80].rearrange("p (t e) -> p t e", t=T)
        LMAX, LSUM = TR[:, 80:85], TR[:, 85:90]
        TOP = TR[:, 96:136].rearrange("p (t e) -> p t e", t=T)
        TOPI = TR[:, 136:176].bitcast(U32).rearrange("p (t e) -> p t e", t=T)
        TOPF = TR[:, 176:186].rearrange("p (t c) -> p t c", t=T)
        CW = TR[:, 186:196].rearrange("p (t c) -> p t c", t=T)
        PICK = TR[:, 256:416].rearrange("p (t c e) -> p t c e", t=T, c=2)
        PICKED = TR[:, 416:496].rearrange("p (t e) -> p t e", t=T)
        RANK = TR[:, 512:608].rearrange("p (t e) -> p t e", t=T + 1)
        NBLK, UPBLK, BASE = TR[:, 608:624], TR[:, 624:640], TR[:, 640:656]
        CMP = TR[:, 1024:1024 + 400]
        SLOTF = TR[:, 656:666]
        SLOT = TR[:, 672:682].bitcast(U32)
        BLKF = TR[:, 704:729]
        BLKE = TR[:, 736:761].bitcast(I32)
        GOT = ARENA[0:P, 0:T * 2 * D].rearrange("p (t c d) -> p t c d", t=T, c=2)
        PRM = sb("PRM", [NE + 1, 8])
        PRMT = sb("PRMT", [NE + 1, 4])

        prm_in, prm_step_a, prm_step_d, prm_done, prm_stored = sem("prm_in"), sem("prm_step_a"), sem("prm_step_d"), sem("prm_done"), sem("prm_stored")
        ffn_w_loaded, ffn_b_loaded, count_ready, tiles_ready = sem("ffn_w_loaded"), sem("ffn_b_loaded"), sem("count_ready"), sem("tiles_ready")
        logits_ready, gate_exp, picked_ready, routed, slots_filled = sem("logits_ready"), sem("gate_exp"), sem("picked_ready"), sem("routed"), sem("slots_filled")
        sgate_ready, ssig_ready, ste_ready = sem("sgate_ready"), sem("ssig_ready"), sem("ste_ready")
        w1_loaded, w2_loaded = [sem(f"w1_loaded{s}") for s in range(2)], [sem(f"w2_loaded{s}") for s in range(2)]
        row_loaded, xg_loaded = [sem(f"row_loaded{s}") for s in range(2)], [sem(f"xg_loaded{s}") for s in range(2)]
        stored = [sem(f"stored{s}") for s in range(2)]
        rows_spread = sem("rows_spread")
        xt_filled, xgt_ready, h_filled, h_drained = sem("xt_filled"), sem("xgt_ready"), sem("h_filled"), sem("h_drained")
        g_ready, u_ready, gu_ready, sig_ready, te_ready, tt_filled, tet_ready = sem("g_ready"), sem("u_ready"), sem("gu_ready"), sem("sig_ready"), sem("te_ready"), sem("tt_filled"), sem("tet_ready")
        o_filled, o_drained, gathered, y_ready, y_stored = sem("o_filled"), sem("o_drained"), sem("gathered"), sem("y_ready"), sem("y_stored")
        XT_BANK, H_BANK, TT_BANK, O_BANK = [banks[0], banks[1]], [banks[2:4], banks[4:6]], banks[6], banks[7]

        def run_blocks(engine, step):
            for b in range(3):
                step(b, b // 2, b % 2)
            with engine.Fori(1, (BLOCKS - 3) // 2) as i:
                step(2 * i + 1, i, 1)
                step(2 * i + 2, i + 1, 0)
            for b in range(2 * ((BLOCKS - 3) // 2) + 1, BLOCKS + 1):
                step(b, b // 2, b % 2)

        chunk_last = {}
        col_at, n = {}, 0
        for group in ("mix", "gnn"):
            layers = 2 if group == "mix" else 1
            for name, k in (("ln1_g", 4), ("ln1_b", 4), ("bq", 4), ("bk", 4), ("ln2_g", 4), ("ln2_b", 4), ("b1", 16)):
                for l in range(layers):
                    col_at[name, l if group == "mix" else GNN] = n
                    n += k
        n_cols = n

        def col(name, L, k):
            c = col_at[name, L] + k
            return COLS[:, c:c + 1]

        def weight(chunk):
            return W[:, chunk % WSLOTS, :].rearrange("p (k n) -> p k n", k=KD)

        def pair_columns(L, t):
            return t * P, (t + 1) * P

        block = ctx.enter_context(nc.Block())

        @block.tensor
        def _(pe):
            seen = {}

            def wait(s, n):
                if seen.get(s.name, 0) < n:
                    pe.wait_ge(s, n)
                    seen[s.name] = n

            def bank_for(ring, job):
                n = ring.add(job)
                if n >= 4:
                    wait(ring.drained, n - 3)
                return ring.bank(job)

            def ready(ring, job):
                wait(ring.drained, ring.count(job))

            def chunk_loaded(c):
                wait(w_loaded[c % WSLOTS], 16 * (c // WSLOTS + 1))

            def transposes(tag, L, src):
                for c, (t0, t1) in enumerate(CHUNKS):
                    for k in range(KD):
                        ring = RV if k % 2 == 0 else RA
                        b = bank_for(ring, (tag, L, c, k))
                        for t in range(t0, t1):
                            ins = pe.transpose(b[:, (t - t0) * P:(t - t0 + 1) * P],
                                               src[:, t, k * 128:(k + 1) * 128], ident[0:P, 0:P])
                        ins.then_inc(ring.filled, 1)

            def column_form_ready(tag, L):
                ready(RV, (tag, L, 1, 2))
                ready(RA, (tag, L, 1, 3))

            def rows_product(ring, job, chunk, t, x=YT):
                b = bank_for(ring, job)
                for k in range(KD):
                    ins = pe.matmul(b[0:P, :], x[:, k, t * P:(t + 1) * P], weight(chunk)[:, k, :],
                                    start=(k == 0), stop=(k == KD - 1))
                ins.then_inc(ring.filled, 1)

            wait(consts_ready, 1)
            wait(rows_loaded, 16 * 14)
            b = bank_for(RV, ("cols",))
            pe.transpose(b[:, 0:n_cols], VROWS[0:n_cols, :], ident[0:n_cols, 0:n_cols]).then_inc(vec_filled, 1)

            wait(proj_loaded, 32)
            b = bank_for(RV, ("proj",))
            for i in range(4):
                ins = pe.transpose(b[:, i * 128:(i + 1) * 128], PROJR[:, i // 2, i % 2].rearrange("p c d -> p (c d)"), ident[:, :])
            ins.then_inc(vec_filled, 1)

            def edge_group(g):
                b = bank_for(RV, ("keys", g))
                wait(edge_exp_ready, 1)
                for j in range(EG):
                    ins = pe.transpose(b[0:P, j * P:(j + 1) * P], key[:, g * EG + j:g * EG + j + 1].to_broadcast([P, P]),
                                       ident[0:P, 0:P])
                ins.then_inc(vec_filled, 1)

            def edge_sums(g):
                b = bank_for(RV, ("sums", g))
                ready(RV, ("keys", g))
                wait(edge_parts_ready, 1)
                for j in range(EG):
                    ins = pe.matmul(b[0:P, j * 3 * H:(j + 1) * 3 * H], SAME[g % 2][:, j, :],
                                    EAP[:, g * EG + j].rearrange("p c h -> p (c h)"), start=True, stop=True)
                ins.then_inc(vec_filled, 1)

            for L in range(LAYERS):
                c0 = WPER * L
                wait(z_ready, 10 * L + 5)
                transposes("y1", L, Z)
                column_form_ready("y1", L)
                chunk_loaded(c0)
                chunk_loaded(c0 + 1)
                for m in range(KD):
                    for c in range(2):
                        n0, n1 = columns(c)
                        for ring, job, ch in ((RV, ("q", L, m, c), c0), (RA, ("k", L, m, c), c0 + 1)):
                            b = bank_for(ring, job)
                            for k in range(KD):
                                ins = pe.matmul(b[:, 0:n1 - n0], weight(ch)[:, k, m * 128:(m + 1) * 128],
                                                YT[:, k, n0:n1], start=(k == 0), stop=(k == KD - 1))
                            ins.then_inc(ring.filled, 1)
                chunk_last[c0] = (RV, ("q", L, KD - 1, 1))
                chunk_last[c0 + 1] = (RA, ("k", L, KD - 1, 1))
                chunk_loaded(c0 + 2)
                for t in range(T):
                    rows_product(RV, ("v", L, t), c0 + 2, t)
                chunk_last[c0 + 2] = (RV, ("v", L, T - 1))

                if L != GNN:
                    ready(RA, ("k", L, KD - 1, 1))
                    ready(RV, ("q", L, KD - 1, 1))

                    def features(tag, x, hp, t):
                        b = bank_for(RA, (tag, L, hp, t))
                        pe.matmul(b[0:P, :], x[:, hp, t * P:(t + 1) * P], PROJ[:, L % 2, :, :].rearrange("p c m -> p (c m)"),
                                  start=True, stop=True).then_inc(act_filled, 1)

                    def context(h):
                        b = bank_for(RV, ("ctxT", L, h))
                        for t in range(T):
                            ins = pe.matmul(b[0:DH + 1, 0:NF], V1[:, t, h, :], KP[:, h, t, :], start=(t == 0), stop=(t == T - 1))
                        ins.then_inc(vec_filled, 1)

                    def context_turned(h):
                        ready(RV, ("ctxT", L, h))
                        b = bank_for(RV, ("ctx", L, h))
                        for mh in range(2):
                            ins = pe.transpose(b[:, mh * (DH + 1):(mh + 1) * (DH + 1)], CTXT[:, h % 2, mh * 128:(mh + 1) * 128],
                                               ident[0:DH + 1, 0:DH + 1])
                        ins.then_inc(vec_filled, 1)

                    def attend(h):
                        ready(RV, ("qt", L, h, 2))
                        ready(RV, ("ctx", L, h))
                        for c in range(2):
                            n0, n1 = columns(c)
                            b = bank_for(RA, ("ocol", L, h, c))
                            for mh in range(2):
                                ins = pe.matmul(b[0:DH + 1, 0:n1 - n0], CTX[:, h % 2, mh, :], QPT[h % 2][:, mh * N + n0:mh * N + n1],
                                                start=(mh == 0), stop=(mh == 1))
                            ins.then_inc(act_filled, 1)

                    def attended_turned(h):
                        ready(RA, ("ocol", L, h, 1))
                        b = bank_for(RV, ("o", L, h))
                        for t in range(T):
                            ins = pe.transpose(b[0:P, t * (DH + 1):(t + 1) * (DH + 1)], OCOL[:, h % 2, t * P:(t + 1) * P],
                                               ident[0:DH + 1, 0:DH + 1])
                        ins.then_inc(vec_filled, 1)

                    for hp in range(H // 2):
                        for t in range(T):
                            features("kd", KT, hp, t)
                    wait(squares_ready, 2 * L + 2)
                    for q in range(2):
                        for c in range(2):
                            n0, n1 = columns(c)
                            b = bank_for(RV, ("dgt", L, q, c))
                            for k in range(KD):
                                ins = pe.matmul(b[0:H, 0:n1 - n0], halves[:, k, :], (SQQ, SQK)[q][:, k, n0:n1],
                                                start=(k == 0), stop=(k == KD - 1))
                            ins.then_inc(vec_filled, 1)
                    for t in range(3):
                        features("qd", QT, 0, t)
                    ready(RV, ("dgt", L, 1, 1))
                    b = bank_for(RV, ("diag", L))
                    for t in range(T):
                        for q in range(2):
                            ins = pe.transpose(b[0:P, (2 * t + q) * H:(2 * t + q + 1) * H], DGT[:, q, t * P:(t + 1) * P], ident[0:H, 0:H])
                    ins.then_inc(vec_filled, 1)
                    for t in range(3, T):
                        features("qd", QT, 0, t)
                    b = bank_for(RV, ("kmax", L))
                    wait(kmax_part, H * L + H)
                    pe.transpose(b[0:H, 0:P], KM[:, :], ident[0:P, 0:P]).then_inc(vec_filled, 1)
                    b = bank_for(RV, ("kmax_all", L))
                    wait(kdiag_ready, L + 1)
                    pe.matmul(b[0:P, 0:H], ones[0:H, 0:P], KDIAG[:, :], start=True, stop=True).then_inc(vec_filled, 1)
                    for h in range(H):
                        if h % 2 == 0:
                            ready(RA, ("qd", L, h // 2, T - 1))
                        for i in range(3):
                            b = bank_for(RV, ("qt", L, h, i))
                            for blk in range(4 * i, min(4 * i + 4, 2 * T)):
                                mh, t = blk // T, blk % T
                                ins = pe.transpose(b[:, (blk - 4 * i) * P:(blk - 4 * i + 1) * P],
                                                   QP[:, h % 2, t, mh * 128:(mh + 1) * 128], ident[0:P, 0:P])
                            ins.then_inc(vec_filled, 1)
                        if h % 2 and h + 1 < H:
                            for t in range(T):
                                features("qd", QT, (h + 1) // 2, t)
                        wait(kp_ready, H * L + h + 1)
                        context(h)
                        if h:
                            attended_turned(h - 1)
                        context_turned(h)
                        attend(h)
                    attended_turned(H - 1)
                    ready(RV, ("o", L, H - 1))
                else:
                    ready(RA, ("k", L, KD - 1, 1))
                    ready(RV, ("v", L, T - 1))
                    wait(queries_apart, 2)

                    def scores(i):
                        dt, h = divmod(i, H)
                        for c in range(2):
                            n0, n1 = columns(c)
                            b = bank_for(RV, ("s", i, c))
                            pe.matmul(b[0:P, 0:n1 - n0], KT[:, h // 2, dt * P:(dt + 1) * P],
                                      (QT, QODD)[h % 2][:, h // 2, n0:n1], start=True, stop=True).then_inc(vec_filled, 1)

                    def probs_turned(i):
                        wait(p_scaled, i + 1)
                        for j in range(2):
                            b = bank_for(RA, ("pt", i, j))
                            for s in range(4 * j, min(4 * j + 4, T)):
                                ins = pe.transpose(b[0:P, (s - 4 * j) * P:(s - 4 * j + 1) * P],
                                                   TS[i % 4][:, s * P:(s + 1) * P], ident[0:P, 0:P])
                            ins.then_inc(act_filled, 1)

                    def gather_messages(i):
                        ready(RA, ("pt", i, 1))
                        b = bank_for(RA, ("agg", i))
                        r0 = DH * (i % 2)
                        for s in range(T):
                            ins = pe.matmul(b[r0:r0 + DH, 0:P], V1[:, s, i % H, 0:DH], PT[i % 2][:, s, :],
                                            start=(s == 0), stop=(s == T - 1))
                        ins.then_inc(act_filled, 1)

                    for i in range(T * H + 4):
                        if i < T * H:
                            scores(i)
                        if 0 <= i - 3 < T * H:
                            probs_turned(i - 3)
                        if 0 <= i - 4 < T * H:
                            gather_messages(i - 4)
                    ready(RA, ("agg", T * H - 1))

                X = YT
                if L != GNN:
                    transposes("oT", L, O)
                    column_form_ready("oT", L)
                else:
                    X = AGG
                chunk_loaded(c0 + 3)
                for t in range(T):
                    rows_product(RV, ("x1", L, t), c0 + 3, t, X)
                chunk_last[c0 + 3] = (RV, ("x1", L, T - 1))

                wait(z_ready, 10 * L + 10)
                transposes("y2", L, Z)
                column_form_ready("y2", L)
                for f in range(FM):
                    ch = c0 + 4 + f // 4
                    chunk_loaded(ch)
                    for c in range(2):
                        n0, n1 = columns(c)
                        b = bank_for(RA, ("h", L, f, c))
                        for k in range(KD):
                            ins = pe.matmul(b[:, 0:n1 - n0], weight(ch)[:, k, (f % 4) * 128:(f % 4 + 1) * 128],
                                            YT[:, k, n0:n1], start=(k == 0), stop=(k == KD - 1))
                        ins.then_inc(act_filled, 1)
                    chunk_last[ch] = (RA, ("h", L, f, 1))
                    if L == 0:
                        for g in range(5 * f // 4, 5 * (f + 1) // 4):
                            edge_group(g)
                            if g:
                                edge_sums(g - 1)
                if L == 0:
                    edge_sums(EB // EG - 1)
                for g in range(4):
                    chunk_loaded(c0 + 8 + g)
                for t in range(T):
                    b = bank_for(RV, ("x2", L, t))
                    ready(RA, ("h", L, FM - 1, 1))
                    for f in range(FM):
                        ins = pe.matmul(b[0:P, :], HT[:, f, t * P:(t + 1) * P], weight(c0 + 8 + f // 4)[:, f % 4, :],
                                        start=(f == 0), stop=(f == FM - 1))
                    ins.then_inc(vec_filled, 1)
                for g in range(4):
                    chunk_last[c0 + 8 + g] = (RV, ("x2", L, T - 1))

            wait(z_ready, 5 * (2 * LAYERS + 1))
            transposes("yf", 0, Z)
            column_form_ready("yf", 0)
            wait(ffn_w_loaded, 16 * 3)
            b = bank_for(RV, ("gate",))
            for t in range(T):
                for k in range(KD):
                    ins = pe.matmul(b[0:P, t * NE:(t + 1) * NE], YT[:, k, t * P:(t + 1) * P], GATEW[:, k, :],
                                    start=(k == 0), stop=(k == KD - 1))
            ins.then_inc(vec_filled, 1)

            def shared_hidden(t):
                for half in range(2):
                    b = bank_for(RV, ("sh", t, half))
                    for k in range(KD):
                        ins = pe.matmul(b[0:P, 0:NI], YT[:, k, t * P:(t + 1) * P], SW1[:, k, half * NI:(half + 1) * NI],
                                        start=(k == 0), stop=(k == KD - 1))
                    ins.then_inc(vec_filled, 1)

            shared_hidden(0)
            b = bank_for(RV, ("rank",))
            wait(picked_ready, 1)
            wait(tiles_ready, 1)
            for t in range(T + 1):
                for u in range(min(t, T)):
                    ins = pe.matmul(b[0:P, t * NE:(t + 1) * NE], ONESP, PICKED[:, u, :], start=(u == 0), stop=(t == T and u == T - 1))
                if t < T:
                    ins = pe.matmul(b[0:P, t * NE:(t + 1) * NE], UPPER, PICKED[:, t, :], start=(t == 0), stop=True)
            ins.then_inc(vec_filled, 1)
            for t in range(T):
                if t + 1 < T:
                    shared_hidden(t + 1)
                wait(ste_ready, t + 1)
                b = bank_for(RA, ("st", t))
                for k in range(KI):
                    ins = pe.transpose(b[:, k * P:(k + 1) * P], TE[t % 2][0:P, k * 128:(k + 1) * 128], ident[0:P, 0:P])
                ins.then_inc(act_filled, 1)
                ready(RA, ("st", t))
                b = bank_for(RV, ("so", t))
                for k in range(KI):
                    ins = pe.matmul(b[0:P, :], TET[t % 2][:, k * 128:k * 128 + P], SW2[:, k, :], start=(k == 0), stop=(k == KI - 1))
                ins.then_inc(vec_filled, 1)
            ready(RV, ("so", T - 1))

            def turn_tokens(b, j, s):
                pe.wait_ge(xg_loaded[s], 16 * (j + 1))
                if not (isinstance(b, int) and b < 2):
                    pe.wait_ge(xgt_ready, b - 1)
                for k in range(KD):
                    ins = pe.transpose(XT_BANK[s][:, k * 128:(k + 1) * 128], XG[s][:, k * 128:(k + 1) * 128], ident[:, :])
                ins.then_inc(xt_filled, 1)

            def hidden(b, j, s):
                pe.wait_ge(w1_loaded[s], 16 * (j + 1))
                pe.wait_ge(xgt_ready, b + 1)
                if not (isinstance(b, int) and b < 2):
                    pe.wait_ge(h_drained, b - 1)
                for half in range(2):
                    for k in range(KD):
                        ins = pe.matmul(H_BANK[s][half][:, 0:NI], XGT[s][:, k * 128:(k + 1) * 128],
                                        EW1[s][:, k, half * NI:(half + 1) * NI], start=(k == 0), stop=(k == KD - 1))
                ins.then_inc(h_filled, 1)

            def output(b, j, s):
                pe.wait_ge(te_ready, b + 1)
                if not (isinstance(b, int) and b < 1):
                    pe.wait_ge(tet_ready, b)
                for k in range(KI):
                    ins = pe.transpose(TT_BANK[:, k * 128:(k + 1) * 128], TE[s][:, k * 128:(k + 1) * 128], ident[:, :])
                ins.then_inc(tt_filled, 1)
                pe.wait_ge(tet_ready, b + 1)
                pe.wait_ge(w2_loaded[s], 16 * (j + 1))
                if not (isinstance(b, int) and b < 1):
                    pe.wait_ge(o_drained, b)
                for k in range(KI):
                    ins = pe.matmul(O_BANK[:, :], TET[s][:, k * 128:(k + 1) * 128], EW2[s][:, k, :], start=(k == 0), stop=(k == KI - 1))
                ins.then_inc(o_filled, 1)

            def step(b, j, s):
                last = isinstance(b, int) and b >= BLOCKS
                if isinstance(b, int) and b == 0:
                    turn_tokens(0, 0, 0)
                if not last:
                    hidden(b, j, s)
                    if not (isinstance(b, int) and b == BLOCKS - 1):
                        turn_tokens(b + 1, j + s, 1 - s)
                if not (isinstance(b, int) and b == 0):
                    output(b - 1, j - 1 + s, 1 - s)

            run_blocks(pe, step)


        @block.sync
        def _(sp):
            x_rows = A["x"].rearrange("(t p) d -> p t d", p=P)
            sp.dma_start(Z, x_rows).then_inc(x_loaded, 16)
            for group, prefix, names in (("mix", "L0_mix_", ("ln1_g", "ln1_b", "bq", "bk", "ln2_g", "ln2_b", "b1")),
                                         ("gnn", "L0_gnn_", ("ln1_g", "ln1_b", "bq", "bk", "ln2_g", "ln2_b", "b1"))):
                for name in names:
                    if group == "mix":
                        v = A[prefix + name].rearrange("l (k p) -> (l k) p", p=128)
                        r0 = col_at[name, 0]
                    elif name in ("bq", "bk"):
                        j = ("bq", "bk").index(name)
                        v = A[prefix + "bqkv"][j * D:(j + 1) * D].rearrange("(k p) -> k p", p=128)
                        r0 = col_at[name, GNN]
                    else:
                        v = A[prefix + name].rearrange("(k p) -> k p", p=128)
                        r0 = col_at[name, GNN]
                    sp.dma_start(VROWS[r0:r0 + v.shape[0], :], v).then_inc(rows_loaded, 16)

            for c in range(2):
                sp.dma_start(PROJR[:, :, :, c, :], A["L0_mix_proj"].rearrange("l (a p) d -> p l a d", p=128)).then_inc(proj_loaded, 16)

            for row0, v in ((0, A["L0_ffn_expert_act"]), (NE, A["L0_ffn_shared_act"].unsqueeze(0))):
                sp.dma_start(PRM[row0:row0 + v.shape[0], 0:5], v).then_inc(prm_in, 16)

            def load_chunk(c):
                L, j = divmod(c, WPER)
                mixed = L != GNN
                if j < 3:
                    src = (A["L0_mix_" + ("Wq", "Wk", "Wv")[j]][L] if mixed
                           else A["L0_gnn_Wqkv"][:, j * D:(j + 1) * D])
                elif j == 3:
                    src = A["L0_mix_Wo"][L] if mixed else A["L0_gnn_Wo"]
                elif j < 8:
                    src = (A["L0_mix_W1"][L] if mixed else A["L0_gnn_W1"])[:, (j - 4) * 512:(j - 3) * 512]
                else:
                    src = (A["L0_mix_W2"][L] if mixed else A["L0_gnn_W2"])[(j - 8) * 512:(j - 7) * 512, :]
                if c >= WSLOTS:
                    ring, job = chunk_last[c - WSLOTS]
                    sp.wait_ge(ring.filled, ring.count(job))
                sp.dma_start(weight(c), src.rearrange("(k p) n -> p k n", p=128)).then_inc(w_loaded[c % WSLOTS], 16)

            for c in range(WPER * LAYERS):
                load_chunk(c)
                if c == WPER + 5:
                    sp.wait_ge(vec_drained, RV.count(("x2", 0, T - 1)))
                    for j, v in enumerate((A["L0_gnn_bqkv"][2 * D:3 * D], A["L0_gnn_bo"], A["L0_gnn_b2"])):
                        sp.dma_start(ROWB[:, 0, j, :], v.partition_broadcast(P)).then_inc(rowb_again, 16)
                if c == WPER * GNN + 8:
                    sp.wait_ge(vec_filled, RV.count(("s", T * H - 1, 1)))
                    sp.dma_start(XAGAIN, x_rows).then_inc(x_again, 16)

            ring, job = chunk_last[WPER * GNN + 7]
            sp.wait_ge(ring.filled, ring.count(job))
            sp.dma_start(SW1, A["L0_ffn_shared_w1"].rearrange("(k p) n -> p k n", p=128)).then_inc(ffn_w_loaded, 16)
            sp.dma_start(GATEW, A["L0_ffn_gate_w"].rearrange("(k p) n -> p k n", p=128)).then_inc(ffn_w_loaded, 16)
            sp.dma_start(SW2, A["L0_ffn_shared_w2"].rearrange("(k p) n -> p k n", p=128)).then_inc(ffn_w_loaded, 16)
            sp.dma_start(SB1, A["L0_ffn_shared_b1"].partition_broadcast(P)).then_inc(ffn_b_loaded, 16)
            sp.dma_start(SB2, A["L0_ffn_shared_b2"].partition_broadcast(P)).then_inc(ffn_b_loaded, 16)
            sp.dma_start(GATEB, A["L0_ffn_gate_b"].partition_broadcast(P)).then_inc(ffn_b_loaded, 16)
            sp.wait_ge(prm_stored, 16)
            sp.dma_start(SACT, act_table[NE].partition_broadcast(P)).then_inc(ffn_b_loaded, 16)

            def step(b, j, s):
                if isinstance(b, int) and b >= BLOCKS:
                    return
                first = isinstance(b, int) and b < 2
                e = sp.value_load(BLKE[0:1, bass.ds(b, 1)], min_val=0, max_val=NE - 1)
                if not first:
                    sp.wait_ge(xt_filled, b - 1)
                sp.dma_start(XG[s], slot_in[bass.ds(b * BLOCK, BLOCK), :]).then_inc(xg_loaded[s], 16)
                if not first:
                    sp.wait_ge(h_filled, b - 1)
                sp.dma_start(EW1[s], A["L0_ffn_expert_w1"][bass.ds(e, 1)].rearrange("o (k p) n -> p (o k) n", p=128)).then_inc(w1_loaded[s], 16)
                if not first:
                    sp.wait_ge(rows_spread, b - 1)
                sp.dma_start(ROW1[s][:, 0:2 * NI], A["L0_ffn_expert_b1"][bass.ds(e, 1)]).then_inc(row_loaded[s], 16)
                sp.dma_start(ROW1[s][:, 2 * NI:2 * NI + D], A["L0_ffn_expert_b2"][bass.ds(e, 1)]).then_inc(row_loaded[s], 16)
                sp.dma_start(ROW1[s][:, 2 * NI + D:], act_table[bass.ds(e, 1)]).then_inc(row_loaded[s], 16)

            sp.wait_ge(routed, 1)
            sp.wait_ge(slots_filled, 16 * 2 * T)
            sp.wait_ge(vec_drained, RV.count(("so", T - 1)))
            run_blocks(sp, step)
            for t in range(T):
                sp.wait_ge(y_ready, t + 1)
                sp.dma_start(out.rearrange("(t p) d -> p t d", p=P)[:, t, :], MX[:, t, :]).then_inc(y_stored, 16)
            sp.wait_ge(y_stored, 16 * T)

        @block.gpsimd
        def _(pool):
            nc.gpsimd.memset(ident[:, :], 0.0).then_inc(pool_step, 1)
            nc.gpsimd.memset(lower[:, :], 1.0).then_inc(pool_step, 1)
            nc.gpsimd.memset(ones[:, :], 1.0).then_inc(pool_step, 1)
            pool.wait_ge(pool_step, 3)
            nc.gpsimd.affine_select(out=ident[:, :], in_=ident[:, :], compare_op=ALU.not_equal, fill=1.0, base=0,
                                    pattern=[[-1, 128]], channel_multiplier=1).then_inc(pool_step, 1)
            nc.gpsimd.affine_select(out=lower[:, :], in_=lower[:, :], compare_op=ALU.is_gt, fill=0.0, base=0,
                                    pattern=[[-1, P]], channel_multiplier=1).then_inc(pool_step, 1)
            pool.wait_ge(pool_step, 5)
            nc.gpsimd.iota(spare_i[:, :], pattern=[[0, 1]], base=PAIRS, channel_multiplier=1).then_inc(pool_step, 1)
            pool.wait_ge(pool_step, 6)
            nc.gpsimd.memset(zero[:, :], 0.0).then_inc(consts_ready, 1)
            pool.wait_ge(consts_ready, 1)
            for L in range(2):
                for j, name in enumerate(("bv", "bo", "b2")):
                    pool.dma_start(ROWB[:, L, j, :], A["L0_mix_" + name][L].partition_broadcast(P)).then_inc(rowb_loaded, 16)
            pool.dma_start(src_i[:, :], A["src"].rearrange("(p j) -> p j", p=P)).then_inc(edges_loaded, 16)
            pool.dma_start(dst_i[:, :], A["dst"].rearrange("(p j) -> p j", p=P)).then_inc(edges_loaded, 16)
            pool.dma_start(EA[:, :, :], A["edge_attr_8"].rearrange("(p j) h -> p j h", p=P)).then_inc(attrs_loaded, 16)
            pool.dma_start(EA2[:, :, :], A["edge_attr_8_n2"].rearrange("(p j) h -> p j h", p=P)).then_inc(attrs_loaded, 16)
            for t in range(T):
                pool.dma_start(pair_table[t * P * N:(t + 1) * P * N, :].rearrange("(p s) h -> p (s h)", p=P)
                               .rearrange("p (r c) -> p r c", r=H),
                               zero[0:P, :].unsqueeze(1).to_broadcast([P, H, N])).then_inc(table_zeroed, 16)
            pool.dma_start(pair_table[PAIRS:PAIRS + 128, :], zero[:, 0:H]).then_inc(table_zeroed, 16)
            for b in range(BLOCKS):
                pool.dma_start(slot_in[b * BLOCK:(b + 1) * BLOCK, :], zero[:, 0:D]).then_inc(slots_zeroed, 16)
            pool.wait_ge(edge_max_part, 1)
            nc.gpsimd.partition_all_reduce(emaxa[:, :], emax[:, :], P, RMAX).then_inc(edge_max_all, 1)
            pool.wait_ge(table_zeroed, 16 * (T + 1))
            pool.wait_ge(idx_ready, 1)
            for j in range(EB):
                pool.indirect_dma_start(out=pair_table[:, :], out_offset=bass.IndirectOffsetOnAxis(ap=idx[:, j:j + 1], axis=0),
                                        in_=VC[:, j, :], in_offset=None, compute_op=ALU.add).then_inc(scattered, 16)
                pool.wait_ge(scattered, 16 * (j + 1))
            def load_pairs(dt):
                if dt == 0:
                    pool.wait_ge(vec_filled, RV.count(("x2", 1, T - 1)))
                pool.dma_start(PAIRW[dt % 2], pair_table[dt * P * N:(dt + 1) * P * N, :].rearrange("(p s) h -> p s h", p=P))\
                    .then_inc(pairw_loaded[dt % 2], 16)

            load_pairs(0)
            load_pairs(1)
            for i in range(T * H):
                pool.wait_ge(rden_ready, i + 1)
                nc.gpsimd.tensor_scalar(TS[i % 4], TS[i % 4], rden[:, i % 4:i % 4 + 1], 1.0, ALU.mult, ALU.mult).then_inc(p_scaled, 1)
                if (i + 1) % H == 0 and (i + 1) // H + 1 < T:
                    load_pairs((i + 1) // H + 1)
            pool.wait_ge(vec_drained, RV.count(("x2", 1, T - 1)))
            nc.gpsimd.iota(COUNT_I, pattern=[[1, BLOCKS]], base=0, channel_multiplier=0).then_inc(count_ready, 1)
            nc.gpsimd.memset(UPPER, 1.0).then_inc(pool_step, 1)
            nc.gpsimd.memset(ONESP, 1.0).then_inc(pool_step, 1)
            pool.wait_ge(pool_step, 8)
            nc.gpsimd.affine_select(out=UPPER, in_=UPPER, compare_op=ALU.is_gt, fill=0.0, base=0,
                                    pattern=[[1, P]], channel_multiplier=-1).then_inc(tiles_ready, 1)
            pool.wait_ge(slots_zeroed, 16 * BLOCKS)
            pool.wait_ge(routed, 1)
            for t in range(T):
                for c in range(2):
                    pool.indirect_dma_start(out=slot_in[:, :], out_offset=bass.IndirectOffsetOnAxis(ap=SLOT[:, 2 * t + c:2 * t + c + 1], axis=0),
                                            in_=Z[:, t, :], in_offset=None).then_inc(slots_filled, 16)

            def step(b, j, s):
                if not (isinstance(b, int) and b >= BLOCKS):
                    pool.wait_ge(row_loaded[s], 48 * (j + 1))
                    if not (isinstance(b, int) and b < 2):
                        pool.wait_ge(o_drained, b - 1)
                    nc.gpsimd.tensor_tensor(zero[0:1, s:s + 1], zero[0:1, 2:3], zero[0:1, 3:4], ALU.add)
                    nc.gpsimd.partition_broadcast(ROWS[s], ROW1[s], 128).then_inc(rows_spread, 1)
                if not (isinstance(b, int) and b < 2):
                    pool.wait_ge(o_drained, b - 1)
                    pool.dma_start(slot_out[bass.ds((b - 2) * BLOCK, BLOCK), :], OG[s]).then_inc(stored[s], 16)

            pool.wait_ge(vec_drained, RV.count(("so", T - 1)))
            run_blocks(pool, step)
            pool.wait_ge(o_drained, BLOCKS)
            pool.dma_start(slot_out[(BLOCKS - 1) * BLOCK:BLOCKS * BLOCK, :], OG[(BLOCKS - 1) % 2]).then_inc(stored[(BLOCKS - 1) % 2], 16)
            pool.wait_ge(stored[0], 16 * ((BLOCKS + 1) // 2))
            pool.wait_ge(stored[1], 16 * (BLOCKS // 2))
            for t in range(T):
                for c in range(2):
                    pool.indirect_dma_start(out=GOT[:, t, c, :], out_offset=None, in_=slot_out[:, :],
                                            in_offset=bass.IndirectOffsetOnAxis(ap=SLOT[:, 2 * t + c:2 * t + c + 1], axis=0)).then_inc(gathered, 16)


        @block.scalar
        def _(act):
            seen = {}
            steps = [0]

            def wait(s, n):
                if seen.get(s.name, 0) < n:
                    act.wait_ge(s, n)
                    seen[s.name] = n

            drained = [0]

            def fill_of(job):
                assert RA.at[job] == drained[0], (job, drained[0])
                drained[0] += 1
                wait(act_filled, RA.count(job))
                return RA.bank(job)

            def std(n):
                wait(var_ready, n + 1)
                nc.scalar.activation(sd[:, :], mv[:, :, 1], ACT.Sqrt, bias=eps_ln[0:P, :]).then_inc(std_ready, 1)

            def from_column_form(tag, L):
                for c in range(2):
                    n0, n1 = columns(c)
                    for k in (1, 3):
                        b = fill_of((tag, L, c, k))
                        if tag == "y1":
                            g, bb = col("ln1_g", L, k), col("ln1_b", L, k)
                        elif tag == "y2":
                            g, bb = col("ln2_g", L, k), col("ln2_b", L, k)
                        else:
                            g, bb = 1.0, 0.0
                        nc.scalar.activation(YT[:, k, n0:n1], b[:, 0:n1 - n0], ACT.Identity, bias=bb, scale=g)\
                            .then_inc(act_drained, 1)

            std(0)
            wait(vec_drained, RV.count(("cols",)))
            for L in range(LAYERS):
                std(2 * L + 1)
                from_column_form("y1", L)
                for m in range(KD):
                    for c in range(2):
                        n0, n1 = columns(c)
                        b = fill_of(("k", L, m, c))
                        wait(kcol_ready, 1)
                        nc.scalar.activation(KT[:, m, n0:n1], b[:, 0:n1 - n0], ACT.Identity, bias=col("bk", L, m),
                                             scale=QK_NORM if L != GNN else 1.0).then_inc(act_drained, 1)
                if L != GNN:
                    wait(act_drained, RA.count(("k", L, KD - 1, 1)))
                    nc.scalar.activation(SQK, KT, ACT.Square).then_inc(squares_ready, 1)
                    wait(vec_drained, RV.count(("q", L, KD - 1, 1)))
                    nc.scalar.activation(SQQ, QT, ACT.Square).then_inc(squares_ready, 1)

                    for hp in range(H // 2):
                        for t in range(T):
                            b = fill_of(("kd", L, hp, t))
                            nc.scalar.copy(KP[:, 2 * hp:2 * hp + 2, t, :], b[0:P, :].rearrange("p (c m) -> p c m", c=2)).then_inc(act_drained, 1)

                    def q_exp(hp):
                        if hp:
                            wait(vec_filled, RV.count(("qt", L, 2 * hp - 1, 2)))
                        for t in range(T):
                            b = fill_of(("qd", L, hp, t))
                            wait(qbias_ready, (H // 2 * L + hp) * T + t + 1)
                            for c in range(2):
                                ins = nc.scalar.activation(QP[:, c, t, :], b[0:P, c * NF:(c + 1) * NF],
                                                           ACT.Exp, bias=NQ[:, 2 * hp + c, t:t + 1])
                            ins.then_inc(act_drained, 1)

                    def k_exp(h):
                        wait(kbias_ready, L + 1)
                        for t in range(T):
                            ins = nc.scalar.activation(KP[:, h, t, :], KP[:, h, t, :], ACT.Exp, bias=NK[:, t, h:h + 1])
                        ins.then_inc(kexp_done, 1)

                    q_exp(0)
                    k_exp(0)
                    k_exp(1)
                    for h in range(H):
                        if h % 2 and h + 1 < H:
                            q_exp((h + 1) // 2)
                            k_exp(h + 1)
                            k_exp(h + 2)
                        for c in range(2):
                            n0, n1 = columns(c)
                            b = fill_of(("ocol", L, h, c))
                            nc.scalar.copy(OCOL[:, h % 2, n0:n1], b[0:DH + 1, 0:n1 - n0]).then_inc(act_drained, 1)
                else:
                    wait(vec_filled, RV.count(("v", L, T - 1)))
                    wait(vec_drained, RV.count(("q", L, KD - 1, 1)))
                    nc.scalar.copy(QODD[64:128, :, :], QT[64:128, :, :]).then_inc(act_step, 1)
                    wait(act_step, 1)
                    nc.scalar.activation(QT[64:128, :, :], KT[64:128, :, :], ACT.Copy, scale=0.0).then_inc(queries_apart, 1)
                    for i in range(T * H + 4):
                        if 0 <= i - 1 < T * H:
                            j = i - 1
                            wait(smax_ready, j + 1)
                            nc.scalar.activation(TS[j % 4], TS[j % 4], ACT.Exp, bias=negmax[:, j % 4:j % 4 + 1])\
                                .then_inc(sexp_done, 1)
                        if 0 <= i - 3 < T * H:
                            j = i - 3
                            for q, (s0, s1) in enumerate(((0, 4), (4, 5))):
                                b = fill_of(("pt", j, q))
                                if j >= 2:
                                    wait(act_filled, RA.count(("agg", j - 2)))
                                nc.scalar.copy(PT[j % 2][:, s0:s1, :], b[0:P, 0:(s1 - s0) * P].rearrange("p (s d) -> p s d", d=P))\
                                    .then_inc(act_drained, 1)
                        if 0 <= i - 4 < T * H:
                            j = i - 4
                            dt, h = divmod(j, H)
                            b = fill_of(("agg", j))
                            r0 = DH * (h % 2)
                            nc.scalar.copy(AGG[r0:r0 + DH, h // 2, dt * P:(dt + 1) * P], b[r0:r0 + DH, 0:P]).then_inc(act_drained, 1)
                if L != GNN:
                    from_column_form("oT", L)
                std(2 * L + 2)
                from_column_form("y2", L)
                for f in range(FM):
                    if L == 0 and f == 0:
                        wait(prm_step_d, 1)
                        nc.scalar.activation(PRMT[:, 2:4], PRMT[:, 0:2], ACT.Exp).then_inc(prm_step_a, 1)
                        wait(prm_step_a, 1)
                        nc.scalar.activation(PRMT[:, 0:2], PRMT[:, 2:4], ACT.Ln, bias=1.0).then_inc(prm_step_a, 1)
                        wait(prm_done, 1)
                        act.dma_start(act_table[:, :], PRM[:, :]).then_inc(prm_stored, 16)
                        wait(edge_sub_ready, 1)
                        nc.scalar.activation(EA[:, :, :], EA[:, :, :], ACT.Exp).then_inc(edge_exp_ready, 1)
                    for c in range(2):
                        n0, n1 = columns(c)
                        b = fill_of(("h", L, f, c))
                        nc.scalar.activation(HT[:, f, n0:n1], b[:, 0:n1 - n0], ACT.Gelu, bias=col("b1", L, f))\
                            .then_inc(act_drained, 1)
            std(2 * LAYERS + 1)
            from_column_form("yf", 0)
            wait(logits_ready, 1)
            nc.scalar.activation(LOGIT, LOGIT, ACT.Exp).then_inc(gate_exp, 1)
            for t in range(T):
                s = t % 2
                wait(sgate_ready, t + 1)
                nc.scalar.activation(SIG[s][0:P], GC[s][0:P], ACT.Sigmoid, scale=SACT[:, 0:1]).then_inc(ssig_ready, 1)
                b = fill_of(("st", t))
                if t >= 2:
                    wait(vec_filled, RV.count(("so", t - 2)))
                nc.scalar.copy(TET[s].rearrange("p (k n) -> p k n", k=KI)[:, :, 0:P], b[:, 0:KI * P].rearrange("p (k n) -> p k n", k=KI))\
                    .then_inc(act_drained, 1)

            def take_tokens(b, s):
                act.wait_ge(xt_filled, b + 1)
                if not (isinstance(b, int) and b < 2):
                    act.wait_ge(h_filled, b - 1)
                nc.scalar.copy(XGT[s], XT_BANK[s][:, :]).then_inc(xgt_ready, 1)

            def step(b, j, s):
                last = isinstance(b, int) and b >= BLOCKS
                if not last:
                    e = act.value_load(BLKE[0:1, bass.ds(b, 1)], min_val=0, max_val=NE - 1)
                    if not (isinstance(b, int) and b < 2):
                        act.wait_ge(o_filled, b - 1)
                    act.dma_start(EW2[s], A["L0_ffn_expert_w2"][bass.ds(e, 1)].rearrange("o (k p) n -> p (o k) n", p=128))\
                        .then_inc(w2_loaded[s], 16)
                if isinstance(b, int) and b == 0:
                    take_tokens(0, 0)
                if not last and not (isinstance(b, int) and b == BLOCKS - 1):
                    take_tokens(b + 1, 1 - s)
                if not (isinstance(b, int) and b == 0):
                    act.wait_ge(tt_filled, b)
                    if not (isinstance(b, int) and b < 3):
                        act.wait_ge(o_filled, b - 2)
                    nc.scalar.copy(TET[1 - s], TT_BANK[:, 0:NI]).then_inc(tet_ready, 1)
                if not last:
                    act.wait_ge(g_ready, b + 1)
                    nc.scalar.activation(SIG[s], GC[s], ACT.Sigmoid, scale=EACT[s][:, 0:1]).then_inc(sig_ready, 1)

            act.wait_ge(routed, 1)
            act.wait_ge(vec_drained, RV.count(("so", T - 1)))
            run_blocks(act, step)


        @block.vector
        def _(dve):
            seen = {}
            steps = [0]
            drained = [0]
            V = nc.vector

            def wait(s, n):
                if seen.get(s.name, 0) < n:
                    dve.wait_ge(s, n)
                    seen[s.name] = n

            def then(ins):
                steps[0] += 1
                ins.then_inc(vec_step, 1)
                dve.wait_ge(vec_step, steps[0])

            def fill_of(job):
                assert RV.at[job] == drained[0], (job, drained[0])
                drained[0] += 1
                wait(vec_filled, RV.count(job))
                return RV.bank(job)

            def stats(src, t):
                then(V.bn_stats(st[:, t, :], src[:, t, :]))
                return V.bn_aggr(mv[:, t, :], st[:, t, :])

            def normalize(n, src, dst, ready):
                wait(std_ready, n + 1)
                then(V.reciprocal(rstd[:, :], sd[:, :]))
                for t in range(T):
                    V.tensor_scalar(dst[:, t, :], src[:, t, :], mv[:, t, 0:1], rstd[:, t:t + 1], ALU.subtract, ALU.mult)\
                        .then_inc(ready, 1)

            def norm(n, src, dst, ready):
                for t in range(T):
                    ins = stats(src, t)
                ins.then_inc(var_ready, 1)
                normalize(n, src, dst, ready)

            def from_column_form(tag, L):
                for c in range(2):
                    n0, n1 = columns(c)
                    for k in (0, 2):
                        b = fill_of((tag, L, c, k))
                        if tag in ("y1", "y2"):
                            name = "ln1" if tag == "y1" else "ln2"
                            V.tensor_scalar(YT[:, k, n0:n1], b[:, 0:n1 - n0], col(name + "_g", L, k), col(name + "_b", L, k),
                                            ALU.mult, ALU.add).then_inc(vec_drained, 1)
                        else:
                            V.tensor_copy(YT[:, k, n0:n1], b[:, 0:n1 - n0]).then_inc(vec_drained, 1)

            V.memset(eps_ln[:, :], EPS_LN).then_inc(vec_step, 1)
            V.memset(neg1[:, :], -1.0).then_inc(vec_step, 1)
            V.memset(PROJ[:, :, :, :], 0.0).then_inc(proj_zeroed, 1)
            V.memset(halves[:, :, :], 0.0).then_inc(vec_step, 1)
            V.memset(V1[:, :, :, DH:DH + 1], 1.0).then_inc(vec_step, 1)
            steps[0] = 4
            dve.wait_ge(vec_step, 4)
            for h in range(H):
                r0 = DH * (h % 2)
                V.memset(halves[r0:r0 + DH, h // 2, h:h + 1], 0.5).then_inc(vec_step, 1)
            steps[0] = 4 + H

            wait(x_loaded, 16)
            norm(0, Z, XN, xn_ready)
            b = fill_of(("cols",))
            V.tensor_copy(COLS[:, 0:n_cols], b[:, 0:n_cols]).then_inc(vec_drained, 1)
            b = fill_of(("proj",))
            wait(proj_zeroed, 1)
            for c in range(2):
                ins = V.tensor_copy(PROJ[64 * c:64 * c + 64, :, c, :], b[64 * c:64 * c + 64, :].rearrange("p (l m) -> p l m", l=2))
            ins.then_inc(vec_drained, 1)
            wait(vec_drained, drained[0])
            c0 = col_at["bk", 0]
            V.tensor_scalar(COLS[:, c0:c0 + 2 * KD], COLS[:, c0:c0 + 2 * KD], QK_NORM, None, ALU.mult).then_inc(kcol_ready, 1)
            wait(xn_ready, T)

            wait(consts_ready, 1)
            then(V.tensor_copy(spare[:, :], spare_i[:, :]))
            def edge_same(g):
                b = fill_of(("keys", g))
                rows = b[0:P, 0:EG * P].rearrange("p (j q) -> p j q", j=EG)
                V.tensor_tensor(SAME[g % 2], rows, key[:, g * EG:(g + 1) * EG].unsqueeze(2).to_broadcast([P, EG, P]),
                                ALU.is_equal).then_inc(vec_drained, 1)
                wait(vec_drained, drained[0])
                then(V.tensor_tensor(SAMEL[g % 2], SAME[g % 2], lower[:, :].unsqueeze(1).to_broadcast([P, EG, P]), ALU.mult))
                V.tensor_reduce(before[:, g * EG:(g + 1) * EG], SAMEL[g % 2], AX_X, ALU.add).then_inc(vec_step, 1)
                steps[0] += 1

            def edge_take(g):
                b = fill_of(("sums", g))
                V.tensor_reduce(VC[:, g * EG:(g + 1) * EG, :], b[0:P, 0:EG * 3 * H].rearrange("p (j c h) -> p j h c", j=EG, c=3),
                                AX_X, ALU.add).then_inc(vec_drained, 1)

            for L in range(LAYERS):
                src = MX if L == 1 else XN
                if L != 1:
                    norm(2 * L + 1, src, Z, z_ready)
                else:
                    normalize(2 * L + 1, src, Z, z_ready)
                wait(z_ready, 10 * L + 5)
                dst = XN if L == GNN else MX
                if L == GNN:
                    wait(rowb_again, 16 * 3)
                else:
                    wait(rowb_loaded, 16 * 6)
                resid = V.tensor_tensor(dst[:, :, :], src[:, :, :], ROWB[:, L % 2, 1, :].unsqueeze(1).to_broadcast([P, T, D]), ALU.add)
                resid.then_inc(vec_step, 1)
                steps[0] += 1
                resid_step = steps[0]
                from_column_form("y1", L)
                for m in range(KD):
                    for c in range(2):
                        n0, n1 = columns(c)
                        b = fill_of(("q", L, m, c))
                        V.tensor_scalar(QT[:, m, n0:n1], b[:, 0:n1 - n0], col("bq", L, m), QK_NORM if L != GNN else GNN_SCALE,
                                        ALU.add, ALU.mult).then_inc(vec_drained, 1)
                for t in range(T):
                    b = fill_of(("v", L, t))
                    V.tensor_tensor(V1[:, t, :, 0:DH], b[0:P, :].rearrange("p (h d) -> p h d", h=H),
                                    ROWB[:, L % 2, 0, :].rearrange("p (h d) -> p h d", h=H), ALU.add).then_inc(vec_drained, 1)
                if L == 0:
                    wait(edges_loaded, 32)
                    V.tensor_copy(key[:, :], dst_i[:, :]).then_inc(vec_step, 1)
                    steps[0] += 1
                    then(V.tensor_copy(srcf[:, :], src_i[:, :]))
                    then(V.scalar_tensor_tensor(out=key[:, :], in0=key[:, :], scalar=float(N), in1=srcf[:, :], op0=ALU.mult, op1=ALU.add))
                    wait(attrs_loaded, 32)
                    then(V.tensor_tensor(EA[:, :, :], EA[:, :, :], EA2[:, :, :], ALU.add))
                    V.tensor_reduce(emax[:, :], EA[:, :, :].rearrange("p j h -> p h j"), AX_X, ALU.max).then_inc(edge_max_part, 1)
                if L != GNN:
                    for h in range(H):
                        wait(act_drained, RA.count(("kd", L, h // 2, T - 1)))
                        V.tensor_reduce(KM[:, h:h + 1], KP[:, h, :, :], mybir.AxisListType.XY, ALU.max).then_inc(kmax_part, 1)

                    for q in range(2):
                        for c in range(2):
                            n0, n1 = columns(c)
                            b = fill_of(("dgt", L, q, c))
                            V.tensor_copy(DGT[:, q, n0:n1], b[0:H, 0:n1 - n0]).then_inc(vec_drained, 1)
                    b = fill_of(("diag", L))
                    V.tensor_copy(DG[:, :, :, :], b[0:P, 0:T * 2 * H].rearrange("p (t q h) -> p t q h", t=T, q=2)).then_inc(vec_drained, 1)

                    def q_max(hp):
                        for t in range(T):
                            job = ("qd", L, hp, t)
                            wait(act_filled, RA.count(job))
                            then(V.tensor_reduce(QM[:, 2 * hp:2 * hp + 2, t], RA.bank(job)[0:P, :].rearrange("p (c m) -> p c m", c=2),
                                                 AX_X, ALU.max))
                            V.scalar_tensor_tensor(out=NQ[:, 2 * hp:2 * hp + 2, t], in0=QM[:, 2 * hp:2 * hp + 2, t], scalar=-1.0,
                                                   in1=DG[:, t, 0, 2 * hp:2 * hp + 2], op0=ALU.mult, op1=ALU.subtract)\
                                .then_inc(qbias_ready, 1)

                    wait(vec_drained, drained[0])
                    q_max(0)
                    b = fill_of(("kmax", L))
                    V.tensor_reduce(KMH[:, :], b[0:H, 0:P], AX_X, ALU.max).then_inc(vec_drained, 1)
                    wait(vec_drained, drained[0])
                    V.tensor_scalar(KDIAG[:, :], ident[0:H, 0:H], KMH[:, 0:1], None, ALU.mult).then_inc(kdiag_ready, 1)
                    b = fill_of(("kmax_all", L))
                    V.tensor_copy(KMA[:, :], b[0:P, 0:H]).then_inc(vec_drained, 1)
                    wait(vec_drained, drained[0])
                    V.scalar_tensor_tensor(out=NK[:, :, :], in0=DG[:, :, 1, :], scalar=-1.0,
                                           in1=KMA[:, :].unsqueeze(1).to_broadcast([P, T, H]),
                                           op0=ALU.mult, op1=ALU.subtract).then_inc(kbias_ready, 1)

                    def take_o(h):
                        b = fill_of(("o", L, h))
                        o = b[0:P, 0:T * (DH + 1)].rearrange("p (t e) -> p t e", t=T)
                        then(V.reciprocal(REC[:, h % 2, :], o[:, :, DH]))
                        V.tensor_tensor(O[:, :, h * DH:(h + 1) * DH], o[:, :, 0:DH],
                                        REC[:, h % 2, :].unsqueeze(2).to_broadcast([P, T, DH]), ALU.mult).then_inc(vec_drained, 1)

                    for h in range(H):
                        for i in range(3):
                            b = fill_of(("qt", L, h, i))
                            n = min(500, 2 * N - 500 * i)
                            V.tensor_scalar(QPT[h % 2][:, 500 * i:500 * i + n], b[:, 0:n], EPS_RF, None, ALU.add).then_inc(vec_drained, 1)
                        if h % 2 and h + 1 < H:
                            q_max((h + 1) // 2)
                        if h == 0:
                            for g in range(2):
                                wait(kexp_done, H * L + g + 1)
                                V.tensor_scalar(KP[:, g, :, :], KP[:, g, :, :], EPS_RF, None, ALU.add).then_inc(kp_ready, 1)
                        b = fill_of(("ctxT", L, h))
                        V.tensor_copy(CTXT[:, h % 2, :], b[0:DH + 1, 0:NF]).then_inc(vec_drained, 1)
                        if h:
                            take_o(h - 1)
                        b = fill_of(("ctx", L, h))
                        V.tensor_copy(CTX[:, h % 2, :, :], b[:, 0:2 * (DH + 1)].rearrange("p (m e) -> p m e", m=2)).then_inc(vec_drained, 1)
                        if h % 2 and h + 1 < H:
                            for g in range(h + 1, h + 3):
                                wait(kexp_done, H * L + g + 1)
                                V.tensor_scalar(KP[:, g, :, :], KP[:, g, :, :], EPS_RF, None, ALU.add).then_inc(kp_ready, 1)
                    take_o(H - 1)
                else:
                    wait(vec_filled, RV.count(("v", L, T - 1)))
                    V.memset(QODD[0:64, :, :], 0.0).then_inc(queries_apart, 1)
                    for i in range(T * H + 2):
                        if i < T * H:
                            dt, h = divmod(i, H)
                            if h == 0:
                                wait(pairw_loaded[dt % 2], 16 * (dt // 2 + 1))
                                then(V.tensor_reduce(NEG[dt % 2], PAIRW[dt % 2], AX_X, ALU.max))
                                then(V.tensor_scalar(NEG[dt % 2], NEG[dt % 2], 0.0, MASK, ALU.is_equal, ALU.mult))
                            if i >= 4:
                                wait(act_filled, RA.count(("pt", i - 4, 1)))
                            for c in range(2):
                                n0, n1 = columns(c)
                                b = fill_of(("s", i, c))
                                V.tensor_tensor_reduce(out=TS[i % 4][:, n0:n1], in0=b[0:P, 0:n1 - n0], in1=NEG[dt % 2][:, n0:n1],
                                                       scale=1.0, scalar=-3e38, op0=ALU.add, op1=ALU.max,
                                                       accum_out=pairmax[:, i % 4, c:c + 1]).then_inc(vec_drained, 1)
                            wait(vec_drained, drained[0])
                            V.scalar_tensor_tensor(out=negmax[:, i % 4:i % 4 + 1], in0=pairmax[:, i % 4, 0:1],
                                                   scalar=pairmax[:, i % 4, 1:2], in1=neg1[:, :], op0=ALU.max, op1=ALU.mult)\
                                .then_inc(smax_ready, 1)
                        if 0 <= i - 1 < T * H:
                            j = i - 1
                            dt, h = divmod(j, H)
                            wait(sexp_done, j + 1)
                            V.tensor_tensor_reduce(out=TS[j % 4], in0=TS[j % 4], in1=PAIRW[dt % 2][:, :, h], scale=1.0, scalar=0.0,
                                                   op0=ALU.mult, op1=ALU.add, accum_out=den[:, j % 4:j % 4 + 1]).then_inc(p_ready, 1)
                            wait(p_ready, j + 1)
                            then(V.tensor_scalar(rden[:, j % 4:j % 4 + 1], den[:, j % 4:j % 4 + 1], 1e-37, None, ALU.max))
                            V.reciprocal(rden[:, j % 4:j % 4 + 1], rden[:, j % 4:j % 4 + 1]).then_inc(rden_ready, 1)
                if L != GNN:
                    from_column_form("oT", L)
                dve.wait_ge(vec_step, resid_step)
                for t in range(T):
                    b = fill_of(("x1", L, t))
                    V.tensor_tensor(dst[:, t, :], b[0:P, :], dst[:, t, :], ALU.add).then_inc(vec_drained, 1)
                    wait(vec_drained, drained[0])
                    ins = stats(dst, t)
                ins.then_inc(var_ready, 1)
                normalize(2 * L + 2, dst, Z, z_ready)
                wait(z_ready, 10 * L + 10)
                resid = V.tensor_tensor(dst[:, :, :], dst[:, :, :], ROWB[:, L % 2, 2, :].unsqueeze(1).to_broadcast([P, T, D]), ALU.add)
                resid.then_inc(vec_step, 1)
                steps[0] += 1
                if L == GNN:
                    dve.wait_ge(vec_step, steps[0])
                    then(V.tensor_tensor(dst[:, :, :], dst[:, :, :], MX[:, :, :], ALU.add))
                    wait(x_again, 16)
                    V.tensor_tensor(dst[:, :, :], dst[:, :, :], XAGAIN, ALU.add).then_inc(vec_step, 1)
                    steps[0] += 1
                resid_step = steps[0]
                from_column_form("y2", L)
                if L == 0:
                    wait(prm_in, 32)
                    V.scalar_tensor_tensor(out=PRMT[:, 0:2], in0=PRM[:, 3:5], scalar=-1.0, in1=PRM[:, 3:5], op0=ALU.mult, op1=ALU.min).then_inc(prm_step_d, 1)
                    wait(prm_step_a, 2)
                    then(V.scalar_tensor_tensor(out=PRM[:, 3:5], in0=PRM[:, 3:5], scalar=0.0, in1=PRMT[:, 0:2], op0=ALU.max, op1=ALU.add))
                    then(V.memset(PRM[:, 7:8], 0.0))
                    V.tensor_scalar(PRM[:, 5:7], PRM[:, 3:5], -1.0, None, ALU.mult).then_inc(prm_done, 1)
                if L == 0:
                    wait(edge_max_all, 1)
                    V.tensor_tensor(EA[:, :, :], EA[:, :, :], emaxa[:, :].unsqueeze(1).to_broadcast([P, EB, H]), ALU.subtract)\
                        .then_inc(edge_sub_ready, 1)
                    wait(edge_exp_ready, 1)
                    then(V.tensor_copy(EAP[:, :, 0, :], EA[:, :, :]))
                    then(V.tensor_tensor(EAR, EA[:, :, :], EAP[:, :, 0, :], ALU.subtract))
                    then(V.tensor_copy(EAP[:, :, 1, :], EAR))
                    V.tensor_tensor(EAP[:, :, 2, :], EAR, EAP[:, :, 1, :], ALU.subtract).then_inc(edge_parts_ready, 1)
                    for g in range(EB // EG):
                        edge_same(g)
                        if g:
                            edge_take(g - 1)
                    edge_take(EB // EG - 1)
                    dve.wait_ge(vec_step, steps[0])
                    then(V.tensor_scalar(before[:, :], before[:, :], 1.0, None, ALU.min))
                    then(V.scalar_tensor_tensor(out=srcf[:, :], in0=key[:, :], scalar=-1.0, in1=spare[:, 0:1].to_broadcast([P, EB]),
                                                op0=ALU.mult, op1=ALU.add))
                    then(V.tensor_tensor(srcf[:, :], srcf[:, :], before[:, :], ALU.mult))
                    then(V.tensor_tensor(srcf[:, :], srcf[:, :], key[:, :], ALU.add))
                    wait(vec_drained, drained[0])
                    V.tensor_copy(idx[:, :], srcf[:, :]).then_inc(idx_ready, 1)
                dve.wait_ge(vec_step, resid_step)
                for t in range(T):
                    b = fill_of(("x2", L, t))
                    V.tensor_tensor(dst[:, t, :], b[0:P, :], dst[:, t, :], ALU.add).then_inc(vec_drained, 1)
                    if L != 1:
                        wait(vec_drained, drained[0])
                        ins = stats(dst, t)
                if L != 1:
                    ins.then_inc(var_ready, 1)
            normalize(2 * LAYERS + 1, XN, Z, z_ready)
            wait(count_ready, 1)
            then(V.tensor_copy(COUNT, COUNT_I))
            V.tensor_scalar(THRESH, COUNT[:, 0:5], float(BLOCK), None, ALU.mult).then_inc(vec_step, 1)
            steps[0] += 1
            then(V.tensor_tensor(UPTO, COUNT[:, 0:NE].unsqueeze(1).to_broadcast([P, NE, NE]),
                                 COUNT[:, 0:NE].unsqueeze(2).to_broadcast([P, NE, NE]), ALU.is_le))
            from_column_form("yf", 0)
            b = fill_of(("gate",))
            wait(ffn_b_loaded, 16 * 4)
            V.tensor_tensor(LOGIT, b[0:P, 0:T * NE].rearrange("p (t e) -> p t e", t=T),
                            GATEB.unsqueeze(1).to_broadcast([P, T, NE]), ALU.add).then_inc(vec_drained, 1)
            wait(vec_drained, drained[0])
            then(V.tensor_reduce(LMAX, LOGIT, AX_X, ALU.max))
            V.tensor_tensor(LOGIT, LOGIT, LMAX.unsqueeze(2).to_broadcast([P, T, NE]), ALU.subtract).then_inc(logits_ready, 1)

            def shared_gate(t):
                s = t % 2
                h0 = fill_of(("sh", t, 0))
                hb = HB[s][0:P]
                V.tensor_tensor(hb[:, 0:NI], h0[0:P, 0:NI], SB1[:, 0:NI], ALU.add).then_inc(vec_drained, 1)
                h1 = fill_of(("sh", t, 1))
                V.tensor_tensor(hb[:, NI:2 * NI], h1[0:P, 0:NI], SB1[:, NI:2 * NI], ALU.add).then_inc(vec_drained, 1)
                wait(vec_drained, drained[0])
                gu = hb.rearrange("p (n c) -> p n c", c=2)
                V.tensor_scalar(GC[s][0:P], gu[:, :, 0], SACT[:, 3:4], SACT[:, 5:6], ALU.min, ALU.max).then_inc(sgate_ready, 1)
                wait(sgate_ready, t + 1)
                then(V.tensor_scalar(UC[s][0:P], gu[:, :, 1], SACT[:, 4:5], SACT[:, 6:7], ALU.min, ALU.max))
                then(V.scalar_tensor_tensor(out=UC[s][0:P], in0=UC[s][0:P], scalar=SACT[:, 2:3], in1=GC[s][0:P], op0=ALU.add, op1=ALU.mult))

            def shared_te(t):
                s = t % 2
                wait(ssig_ready, t + 1)
                if t >= 2:
                    wait(act_filled, RA.count(("st", t - 2)))
                V.scalar_tensor_tensor(out=TE[s][0:P], in0=UC[s][0:P], scalar=SACT[:, 1:2], in1=SIG[s][0:P], op0=ALU.mult, op1=ALU.mult)\
                    .then_inc(ste_ready, 1)

            shared_gate(0)
            wait(gate_exp, 1)
            then(V.tensor_reduce(LSUM, LOGIT, AX_X, ALU.add))
            then(V.reciprocal(LSUM, LSUM))
            then(V.tensor_tensor(LOGIT, LOGIT, LSUM.unsqueeze(2).to_broadcast([P, T, NE]), ALU.mult))
            for t in range(T):
                V.max(TOP[:, t, :], LOGIT[:, t, :]).then_inc(vec_step, 1)
                steps[0] += 1
            dve.wait_ge(vec_step, steps[0])
            for t in range(T):
                V.max_index(TOPI[:, t, :], TOP[:, t, :], LOGIT[:, t, :]).then_inc(vec_step, 1)
                steps[0] += 1
            then(V.tensor_tensor(LSUM, TOP[:, :, 0], TOP[:, :, 1], ALU.add))
            then(V.reciprocal(LSUM, LSUM))
            then(V.tensor_tensor(CW, TOP[:, :, 0:2], LSUM.unsqueeze(2).to_broadcast([P, T, 2]), ALU.mult))
            then(V.tensor_copy(TOPF, TOPI[:, :, 0:2]))
            for t in range(T):
                V.tensor_tensor(PICK[:, t], COUNT[:, 0:NE].unsqueeze(1).to_broadcast([P, 2, NE]),
                                TOPF[:, t].unsqueeze(2).to_broadcast([P, 2, NE]), ALU.is_equal).then_inc(vec_step, 1)
                steps[0] += 1
            dve.wait_ge(vec_step, steps[0])
            V.tensor_tensor(PICKED, PICK[:, :, 0, :], PICK[:, :, 1, :], ALU.add).then_inc(picked_ready, 1)
            b = fill_of(("rank",))
            V.tensor_copy(RANK, b[0:P, 0:(T + 1) * NE].rearrange("p (t e) -> p t e", t=T + 1)).then_inc(vec_drained, 1)
            wait(vec_drained, drained[0])
            c5 = CMP[:, 0:NE * 5].rearrange("p (e j) -> p e j", j=5)
            then(V.tensor_tensor(c5, RANK[:, T, :].unsqueeze(2).to_broadcast([P, NE, 5]), THRESH.unsqueeze(1).to_broadcast([P, NE, 5]), ALU.is_gt))
            then(V.tensor_reduce(NBLK, c5, AX_X, ALU.add))
            c16 = CMP[:, 0:NE * NE].rearrange("p (a b) -> p a b", a=NE)
            then(V.tensor_tensor(c16, NBLK.unsqueeze(1).to_broadcast([P, NE, NE]), UPTO, ALU.mult))
            then(V.tensor_reduce(UPBLK, c16, AX_X, ALU.add))
            then(V.tensor_tensor(BASE, UPBLK, NBLK, ALU.subtract))
            then(V.scalar_tensor_tensor(out=RANK[:, 0:T, :], in0=BASE.unsqueeze(1).to_broadcast([P, T, NE]), scalar=float(BLOCK),
                                        in1=RANK[:, 0:T, :], op0=ALU.mult, op1=ALU.add))
            for c in range(2):
                V.tensor_tensor(PICK[:, :, c, :], PICK[:, :, c, :], RANK[:, 0:T, :], ALU.mult).then_inc(vec_step, 1)
                steps[0] += 1
            dve.wait_ge(vec_step, steps[0])
            then(V.tensor_reduce(SLOTF, PICK.rearrange("p t c e -> p (t c) e"), AX_X, ALU.add))
            then(V.tensor_copy(SLOT, SLOTF))
            cb = CMP[:, 0:BLOCKS * NE].rearrange("p (a b) -> p a b", a=BLOCKS)
            then(V.tensor_tensor(cb, UPBLK.unsqueeze(1).to_broadcast([P, BLOCKS, NE]),
                                 COUNT.unsqueeze(2).to_broadcast([P, BLOCKS, NE]), ALU.is_le))
            then(V.tensor_reduce(BLKF, cb, AX_X, ALU.add))
            V.tensor_scalar(BLKE, BLKF, float(NE - 1), None, ALU.min).then_inc(routed, 1)
            then(V.tensor_tensor(MX[:, :, :], XN[:, :, :], SB2.unsqueeze(1).to_broadcast([P, T, D]), ALU.add))
            shared_te(0)
            for t in range(T):
                if t + 1 < T:
                    shared_gate(t + 1)
                    shared_te(t + 1)
                b = fill_of(("so", t))
                V.tensor_tensor(MX[:, t, :], b[0:P, :], MX[:, t, :], ALU.add).then_inc(vec_drained, 1)

            def step(b, j, s):
                last = isinstance(b, int) and b >= BLOCKS
                if not last:
                    dve.wait_ge(h_filled, b + 1)
                    dve.wait_ge(rows_spread, b + 1)
                    V.tensor_tensor(HB[s][:, 0:NI], H_BANK[s][0][:, 0:NI], EB1[s][:, 0:NI], ALU.add)
                    V.tensor_tensor(HB[s][:, NI:2 * NI], H_BANK[s][1][:, 0:NI], EB1[s][:, NI:2 * NI], ALU.add).then_inc(h_drained, 1)
                    dve.wait_ge(h_drained, b + 1)
                    gu = HB[s].rearrange("p (n c) -> p n c", c=2)
                    V.tensor_scalar(GC[s], gu[:, :, 0], EACT[s][:, 3:4], EACT[s][:, 5:6], ALU.min, ALU.max).then_inc(g_ready, 1)
                    V.tensor_scalar(UC[s], gu[:, :, 1], EACT[s][:, 4:5], EACT[s][:, 6:7], ALU.min, ALU.max).then_inc(u_ready, 1)
                    dve.wait_ge(g_ready, b + 1)
                    dve.wait_ge(u_ready, b + 1)
                    V.scalar_tensor_tensor(out=UC[s], in0=UC[s], scalar=EACT[s][:, 2:3], in1=GC[s], op0=ALU.add, op1=ALU.mult).then_inc(gu_ready, 1)
                if not (isinstance(b, int) and b == 0):
                    q = 1 - s
                    dve.wait_ge(o_filled, b)
                    if not (isinstance(b, int) and b < 3):
                        dve.wait_ge(stored[q], 16 * (j + s - 1))
                    V.tensor_tensor(OG[q], O_BANK[:, :], EB2[q], ALU.add).then_inc(o_drained, 1)
                if not last:
                    dve.wait_ge(sig_ready, b + 1)
                    dve.wait_ge(gu_ready, b + 1)
                    if not (isinstance(b, int) and b < 2):
                        dve.wait_ge(tt_filled, b - 1)
                    V.scalar_tensor_tensor(out=TE[s], in0=UC[s], scalar=EACT[s][:, 1:2], in1=SIG[s], op0=ALU.mult, op1=ALU.mult).then_inc(te_ready, 1)

            run_blocks(dve, step)
            dve.wait_ge(gathered, 16 * 2 * T)
            for t in range(T):
                then(V.scalar_tensor_tensor(out=MX[:, t, :], in0=GOT[:, t, 0, :], scalar=CW[:, t, 0:1], in1=MX[:, t, :], op0=ALU.mult, op1=ALU.add))
                V.scalar_tensor_tensor(out=MX[:, t, :], in0=GOT[:, t, 1, :], scalar=CW[:, t, 1:2], in1=MX[:, t, :], op0=ALU.mult, op1=ALU.add)\
                    .then_inc(y_ready, 1)


_OUTS = [((625, 512), "float32")]


def kernel(**inputs):
    import numpy as _np
    import concourse.bacc as _bacc
    from concourse import mybir as _mybir
    from concourse.bass_utils import run_bass_kernel_spmd as _run

    nc = _bacc.Bacc("TRN2", target_bir_lowering=False, num_devices=1)
    arrays, aps = {}, {}
    for name in inputs:
        a = _np.ascontiguousarray(inputs[name])
        arrays[f"in_{name}_dram"] = a
        aps[name] = nc.dram_tensor(f"in_{name}_dram", a.shape, _mybir.dt.from_np(a.dtype), kind="ExternalInput").ap()
    outs = [nc.dram_tensor(f"out_{i}_dram", shape, _mybir.dt.from_np(_np.dtype(dtype)), kind="ExternalOutput").ap()
            for i, (shape, dtype) in enumerate(_OUTS)]
    gps_layer(nc, aps, *outs)
    r = _run(nc, [arrays], core_ids=[0])
    got = tuple(r.results[0][f"out_{i}_dram"] for i in range(len(_OUTS)))
    return got[0]
```

```python
from contextlib import ExitStack

import concourse.bass as bass
from concourse import mybir

ALU = mybir.AluOpType
ACT = mybir.ActivationFunctionType
F32 = mybir.dt.float32
F32R = mybir.dt.float32r
I32 = mybir.dt.int32
U32 = mybir.dt.uint32
BF16 = mybir.dt.bfloat16
AX_X = mybir.AxisListType.X
RMAX = bass.bass_isa.ReduceOp.max

P, T = 125, 5
N = P * T
D, KD = 512, 4
H, DH = 8, 64
FF, FM = 2048, 16
NF = 256
NE, NI, KI = 16, 384, 3
LAYERS = 3
GNN = 2
EDGES = 10000
EB = EDGES // P
EG = 4
PAIRS = N * N
BLOCK = 128
BLOCKS = (2 * N + NE * (BLOCK - 1)) // BLOCK
CHUNKS = [(0, 3), (3, 5)]
FORMS = [(0, 2), (2, 3), (3, 5)]
SPANS = [(0, N // 2 + 2, 0), (N // 2 + 1, N // 2, 1)]
QK_NORM = float(DH) ** -0.25
GNN_SCALE = float(D) ** -0.5
EPS_LN = 1e-5
EPS_RF = 1e-4
MASK = -1e30
WSLOTS = 3
WPER = 12
NTS = 6


class Ring:

    def __init__(self, banks, filled, drained):
        self.banks, self.filled, self.drained, self.at = banks, filled, drained, {}

    def add(self, job):
        assert job not in self.at, job
        self.at[job] = len(self.at)
        return self.at[job]

    def bank(self, job):
        return self.banks[self.at[job] % len(self.banks)]

    def count(self, job):
        return self.at[job] + 1


def columns(c):
    t0, t1 = CHUNKS[c]
    return t0 * P, t1 * P


def gps_layer(nc, A, out):
    ctx = ExitStack()
    with ctx:
        def sb(name, shape, dt=F32):
            return ctx.enter_context(nc.sbuf_tensor(name, shape, dt))

        offset = {}

        def placed(name, shape):
            offset[name] = -(-nc.sbuf_base // 32) * 32
            return ctx.enter_context(nc.sbuf_tensor(name, shape, F32))

        def also(name, shape, at, skip=0):
            return nc.alloc_sbuf_tensor_at(name, shape, F32R, offset=offset[at] + 4 * skip)

        def sem(name):
            return ctx.enter_context(nc.semaphore(name))

        pair_table = nc.dram_tensor("pair_table", (PAIRS + 128, H), F32, kind="Internal").ap()
        slot_in = nc.dram_tensor("slot_in", (BLOCKS * BLOCK, D), F32, kind="Internal").ap()
        slot_out = nc.dram_tensor("slot_out", (BLOCKS * BLOCK, D), F32, kind="Internal").ap()
        act_table = nc.dram_tensor("act_table", (NE + 1, 8), F32, kind="Internal").ap()

        XN = sb("XN", [P, T, D])
        MX = sb("MX", [P, T, D])
        ZB = placed("ZB", [128, T * D])
        Z = ZB[0:P, :].rearrange("p (t d) -> p t d", t=T)
        YT = placed("YT", [128, KD, N])
        QK = sb("QK", [128, 2, KD, N])
        V1 = sb("V1", [P, T, H, DH + 1])
        ARENA = placed("ARENA", [128, 10240])
        W = placed("W", [128, 2 * WSLOTS, KD * 512])
        ROWB = sb("ROWB", [P, 2, 3, D])
        EXPB = sb("EXPB", [128, 2560])
        TRB = placed("TRB", [128, 2 * 1250])
        PROJ = sb("PROJ", [128, 2, 2, NF])
        KMA = sb("KMA", [P, H])
        spare_i = sb("spare_i", [P, 1], I32)
        spare = sb("spare", [P, 1])
        CTX = sb("CTX", [128, 2, 2, DH + 1])
        ident = sb("ident", [128, 128])
        lower = sb("lower", [P, P])
        zero = sb("zero", [128, 625])
        halves = sb("halves", [128, KD, H])
        COLS = sb("COLS", [128, 120])
        st = sb("st", [P, T, 6])
        mv = sb("mv", [P, T, 2])
        sd = sb("sd", [P, T])
        rstd = sb("rstd", [P, T])
        mv_x = sb("mv_x", [P, T, 2])
        rstd_x = sb("rstd_x", [P, T])
        eps_ln = sb("eps_ln", [128, 1])
        DG = sb("DG", [P, T, 2, H])
        KM = sb("KM", [P, H])
        KMH = sb("KMH", [H, 1])
        KDIAG = sb("KDIAG", [H, H])
        ones = sb("ones", [H, 128])
        NK = sb("NK", [P, T, H])
        QM = sb("QM", [P, H, T])
        NQ = sb("NQ", [P, H, T])
        REC = sb("REC", [P, 2, T])
        src_i = sb("src_i", [P, EB], I32)
        dst_i = sb("dst_i", [P, EB], I32)
        key = sb("key", [P, EB])
        srcf = sb("srcf", [P, EB])
        EA = sb("EA", [P, EB, H])
        EA2 = sb("EA2", [P, EB, H])
        VC = EA2
        before = sb("before", [P, EB])
        idx = sb("idx", [P, EB], U32)
        emax = sb("emax", [P, H])
        emaxa = sb("emaxa", [P, H])
        pairmax = sb("pairmax", [P, NTS, 2])
        negmax = sb("negmax", [P, NTS])
        den = sb("den", [P, NTS])
        rden = sb("rden", [P, NTS])
        neg1 = sb("neg1", [P, 1])

        WLOW = also("WLOW", [128, WSLOTS, KD, 512], "W")
        WHIGH = also("WHIGH", [128, WSLOTS, KD, 512], "W", WSLOTS * KD * 512)
        YLOW, YHIGH = also("YLOW", [128, KD, N], "YT"), also("YHIGH", [128, KD, N], "TRB")
        AGGLOW, AGGHIGH = also("AGGLOW", [128, KD, N], "ZB"), also("AGGHIGH", [128, KD, N], "YT")
        HTLOW, HTHIGH = also("HTLOW", [128, 8, N], "ARENA"), also("HTHIGH", [128, 8, N], "ARENA", 8 * N)

        YTFREE = YT[:, :, :].rearrange("p k n -> p (k n)")
        OCOL = YTFREE[0:DH + 1, 0:2 * N].rearrange("p (s n) -> p s n", s=2)
        DGT = OCOL[0:H, :, :]
        CTXT = YTFREE[0:DH + 1, 2 * N:2 * N + 2 * NF].rearrange("p (s n) -> p s n", s=2)
        PROJR = EXPB[:, 0:512].rearrange("p (l a c d) -> p l a c d", l=2, a=2, c=2)
        VROWS = EXPB[:, 512:640]
        KP = ARENA[0:P, :].rearrange("p (h t m) -> p h t m", h=H, t=T)
        HT = ARENA[:, 0:8 * N].rearrange("p (f n) -> p f n", f=8)
        SQQ = ZB[:, 0:KD * N].rearrange("p (k n) -> p k n", k=KD)
        SQK = EXPB[:, 0:KD * N].rearrange("p (k n) -> p k n", k=KD)
        QP = EXPB[0:P, :].rearrange("p (c t m) -> p c t m", c=2, t=T)
        QPT = [TRB[:, s * 1250:(s + 1) * 1250] for s in range(2)]
        O = Z
        ZG = EXPB[0:P, :].rearrange("p (t d) -> p t d", t=T)
        XAGAIN = QK[0:P].rearrange("p a k n -> p (a k n)")[:, 0:T * D].rearrange("p (t d) -> p t d", t=T)
        QT, KT = QK[:, 0], QK[:, 1]
        PAIRW = [ARENA[0:P, s * 5000:(s + 1) * 5000].rearrange("p (s h) -> p s h", h=H) for s in range(2)]
        QODD = EXPB[:, 0:KD * N].rearrange("p (k n) -> p k n", k=KD)
        AGG = ZB[:, 0:KD * N].rearrange("p (k n) -> p k n", k=KD)
        TS = [YTFREE[0:P, s * N:(s + 1) * N] for s in range(4)]
        TS += [ROWB[:, 1].rearrange("p j d -> p (j d)")[:, s * N:(s + 1) * N] for s in range(2)]
        PT = [TRB[0:P, s * 625:(s + 1) * 625].rearrange("p (s d) -> p s d", s=T) for s in range(2)]
        NEG0 = zero[0:P, :]
        NEG = [TRB[0:P, 1250 + s * 625:1250 + (s + 1) * 625] for s in range(2)]
        SAME = [EXPB[0:P, s * 250:(s + 1) * 250].bitcast(BF16).rearrange("p (j q) -> p j q", j=EG) for s in range(2)]
        EAP = EXPB[0:P, 500:500 + 960].bitcast(BF16).rearrange("p (j c h) -> p j c h", j=EB, c=3)
        EAR = EXPB[0:P, 1460:1460 + 640].rearrange("p (j h) -> p j h", j=EB)
        SAMEL = [QK[0:P].rearrange("p a k n -> p (a k n)")[:, T * D + s * 500:T * D + (s + 1) * 500]
                 .rearrange("p (j q) -> p j q", j=EG) for s in range(2)]

        banks = [ctx.enter_context(nc.psum_tensor(f"bank{i}", [128, 512], F32)) for i in range(8)]

        act_filled, act_drained = sem("act_filled"), sem("act_drained")
        vec_filled, vec_drained = sem("vec_filled"), sem("vec_drained")
        RA = Ring(banks[0:4], act_filled, act_drained)
        RV = Ring(banks[4:8], vec_filled, vec_drained)

        vec_step, act_step, pool_step = sem("vec_step"), sem("act_step"), sem("pool_step")
        x_loaded, rows_loaded, rowb_loaded, rowb_again = sem("x_loaded"), sem("rows_loaded"), sem("rowb_loaded"), sem("rowb_again")
        edges_loaded, attrs_loaded = sem("edges_loaded"), sem("attrs_loaded")
        proj_loaded = sem("proj_loaded")
        consts_ready, zero_ready = sem("consts_ready"), sem("zero_ready")
        table_zeroed, slots_zeroed = sem("table_zeroed"), sem("slots_zeroed")
        w_loaded = [sem(f"w_loaded{i}") for i in range(WSLOTS)]
        var_ready, std_ready, xn_ready, z_ready = sem("var_ready"), sem("std_ready"), sem("xn_ready"), sem("z_ready")
        resid_ready = sem("resid_ready")
        squares_ready = sem("squares_ready")
        kmax_part, kdiag_ready, kbias_ready, qbias_ready = sem("kmax_part"), sem("kdiag_ready"), sem("kbias_ready"), sem("qbias_ready")
        kexp_done, kcol_ready, kp_ready = sem("kexp_done"), sem("kcol_ready"), sem("kp_ready")
        edge_attr_ready, edge_max_part, edge_max_all = sem("edge_attr_ready"), sem("edge_max_part"), sem("edge_max_all")
        edge_sub_ready, edge_exp_ready, edge_parts_ready, idx_ready = sem("edge_sub_ready"), sem("edge_exp_ready"), sem("edge_parts_ready"), sem("idx_ready")
        scattered = sem("scattered")
        pairw_loaded = [sem(f"pairw_loaded{i}") for i in range(2)]
        smax_ready, sexp_done, p_ready = sem("smax_ready"), sem("sexp_done"), sem("p_ready")
        w_high, w_low, col_high, col_low = sem("w_high"), sem("w_low"), sem("col_high"), sem("col_low")
        hid_high, hid_low, agg_high, agg_low = sem("hid_high"), sem("hid_low"), sem("agg_high"), sem("agg_low")
        queries_apart, den_ready, rden_ready, p_scaled, proj_zeroed = sem("queries_apart"), sem("den_ready"), sem("rden_ready"), sem("p_scaled"), sem("proj_zeroed")
        x_again = sem("x_again")

        WFREE = W[:, :, :].rearrange("p s n -> p (s n)")
        SW1 = WFREE[:, 0:KD * 2 * NI].rearrange("p (k n) -> p k n", k=KD)
        SB1 = WFREE[0:P, 3136:3904]
        QKFREE = QK[:, :, :, :].rearrange("p a k n -> p (a k n)")
        SW2 = QKFREE[:, 2560:4096].rearrange("p (k n) -> p k n", k=KI)
        SB2 = QKFREE[0:P, 4096:4608]
        GATEB = QKFREE[0:P, 4608:4624]
        SACT = QKFREE[0:P, 4624:4632]
        GATEW = QKFREE[:, 4632:4696].rearrange("p (k e) -> p k e", k=KD)
        EW1 = ARENA[:, 0:2 * 3072].rearrange("p (s k n) -> p s k n", s=2, k=KD)
        EW2 = ARENA[:, 2 * 3072:2 * 4608].rearrange("p (s k n) -> p s k n", s=2, k=KI)

        def pair_of(base, size):
            return [WFREE[:, base + s * size:base + (s + 1) * size] for s in range(2)]

        XG, XGT = pair_of(4096, 512), pair_of(5120, 512)
        HB, GC, TE, TET = pair_of(6144, 768), pair_of(7680, 384), pair_of(8448, 384), pair_of(9216, 384)
        UC = pair_of(11520, 384)
        ROW1 = [QKFREE[0:1, s * 1288:(s + 1) * 1288] for s in range(2)]
        ROWS = [WFREE[:, 9984:9984 + 1288], QKFREE[:, 2576:2576 + 1288]]
        EB1, EB2, EACT = [r[:, 0:768] for r in ROWS], [r[:, 768:1280] for r in ROWS], [r[:, 1280:1288] for r in ROWS]
        OG = [EXPB[:, s * 512:(s + 1) * 512] for s in range(2)]
        SIG = [EXPB[:, 1024 + s * 384:1408 + s * 384] for s in range(2)]
        UPPER, ONESP = ROWB[:, 1, 0, 0:P], ROWB[:, 1, 1, 0:P]
        COUNT_I = ROWB[:, 1, 2, 0:BLOCKS].bitcast(I32)
        COUNT = ROWB[:, 1, 2, 32:32 + BLOCKS]
        THRESH = ROWB[:, 1, 2, 64:69]
        UPTO = ROWB[:, 1, 2, 128:384].rearrange("p (a b) -> p a b", a=NE)
        TR = TRB[0:P, :]
        LOGIT = TR[:, 0:80].rearrange("p (t e) -> p t e", t=T)
        LOGITT = EXPB[0:NE, 0:N]
        LMAX, LSUM = TR[:, 80:85], TR[:, 85:90]
        TOP = TR[:, 96:136].rearrange("p (t e) -> p t e", t=T)
        TOPI = TR[:, 136:176].bitcast(U32).rearrange("p (t e) -> p t e", t=T)
        TOPF = TR[:, 176:186].rearrange("p (t c) -> p t c", t=T)
        CW = TR[:, 186:196].rearrange("p (t c) -> p t c", t=T)
        PICK = TR[:, 256:416].rearrange("p (t c e) -> p t c e", t=T, c=2)
        PICKED = TR[:, 416:496].rearrange("p (t e) -> p t e", t=T)
        RANK = TR[:, 512:608].rearrange("p (t e) -> p t e", t=T + 1)
        NBLK, UPBLK, BASE = TR[:, 608:624], TR[:, 624:640], TR[:, 640:656]
        CMP = TR[:, 1024:1024 + 400]
        SLOTF = TR[:, 656:666]
        SLOT = TR[:, 672:682].bitcast(U32)
        BLKF = TR[:, 704:729]
        BLKE = TR[:, 736:761].bitcast(I32)
        BLKS = TR[:, 768:793].bitcast(I32)
        BLKW = [TR[:, 800 + 32 * q:800 + 32 * q + BLOCKS].bitcast(I32) for q in range(2)]
        EVENS, EVENF = TR[:, 864:872], TR[:, 896:921]
        ODDF = TR[:, 928:953]
        PAST = TR[:, 960:976].bitcast(I32)
        GOT = ARENA[0:P, 0:T * 2 * D].rearrange("p (t c d) -> p t c d", t=T, c=2)
        PRM = sb("PRM", [NE + 1, 8])
        PRMT = sb("PRMT", [NE + 1, 4])

        prm_in, prm_step_a, prm_step_d, prm_done, prm_stored = sem("prm_in"), sem("prm_step_a"), sem("prm_step_d"), sem("prm_done"), sem("prm_stored")
        ffn_w_loaded, gate_loaded, count_ready, tiles_ready = sem("ffn_w_loaded"), sem("gate_loaded"), sem("count_ready"), sem("tiles_ready")
        logits_ready, gate_exp, picked_ready, routed, slots_filled = sem("logits_ready"), sem("gate_exp"), sem("picked_ready"), sem("routed"), sem("slots_filled")
        sgate_ready, ssig_ready, ste_ready = sem("sgate_ready"), sem("ssig_ready"), sem("ste_ready")
        w1_loaded = [[sem(f"w1_half{half}_loaded{s}") for half in range(2)] for s in range(2)]
        w2_loaded = [sem(f"w2_loaded{s}") for s in range(2)]
        half_filled = sem("half_filled")
        w1_there = [sem(f"w1_half{half}_there") for half in range(2)]
        row_loaded, xg_loaded = [sem(f"row_loaded{s}") for s in range(2)], [sem(f"xg_loaded{s}") for s in range(2)]
        stored = [sem(f"stored{s}") for s in range(2)]
        rows_spread = sem("rows_spread")
        xt_filled, xgt_ready, h_filled, h_drained = sem("xt_filled"), sem("xgt_ready"), sem("h_filled"), sem("h_drained")
        g_ready, u_ready, gu_ready, sig_ready, te_ready, tt_filled, tet_ready = sem("g_ready"), sem("u_ready"), sem("gu_ready"), sem("sig_ready"), sem("te_ready"), sem("tt_filled"), sem("tet_ready")
        gathered = [sem(f"gathered{t}") for t in range(T)]
        o_filled, o_drained, y_ready, y_stored = sem("o_filled"), sem("o_drained"), sem("y_ready"), sem("y_stored")
        XT_BANK, H_BANK, TT_BANK, O_BANK = [banks[0], banks[1]], [banks[2:4], banks[4:6]], banks[6], banks[7]

        def run_blocks(engine, step):
            for b in range(3):
                step(b, b // 2, b % 2)
            with engine.Fori(1, (BLOCKS - 3) // 2) as i:
                step(2 * i + 1, i, 1)
                step(2 * i + 2, i + 1, 0)
            for b in range(2 * ((BLOCKS - 3) // 2) + 1, BLOCKS + 1):
                step(b, b // 2, b % 2)

        chunk_last = {}
        col_at, n = {}, 0
        for group in ("mix", "gnn"):
            layers = 2 if group == "mix" else 1
            for name, k in (("ln1_g", 4), ("ln1_b", 4), ("bq", 4), ("bk", 4), ("ln2_g", 4), ("ln2_b", 4), ("b1", 16)):
                for l in range(layers):
                    col_at[name, l if group == "mix" else GNN] = n
                    n += k
        n_cols = n

        def col(name, L, k):
            c = col_at[name, L] + k
            return COLS[:, c:c + 1]

        def weight(chunk):
            return W[:, chunk % WSLOTS, :].rearrange("p (k n) -> p k n", k=KD)

        def high_low(x_high, x_low, y_high, y_low):
            return ((x_high, y_high), (x_high, y_low), (x_low, y_high))

        def col_form(tag, L):
            return 3 * L + (("y1", "y2") if L == GNN else ("y1", "oT", "y2")).index(tag)

        Z_ORDER = [("y1", 0), ("y2", 0), ("y1", 1), ("y2", 1), ("y1", 2), ("y2", 2), ("yf", 0)]
        NORM_OF = {("y1", 0): 1, ("y2", 0): 2, ("y1", 1): 3, ("y2", 1): 4, ("y2", 2): 5, ("yf", 0): 6}

        def z_of(tag, L):
            return ZG if (tag, L) == ("y2", GNN) else Z

        def z_count(tag, L, tiles):
            return T * Z_ORDER.index((tag, L)) + tiles

        def moments(n):
            return (mv_x, rstd_x) if n == 1 else (mv, rstd)

        W1_AT, W2_AT = (4, 5, 7, 9), (6, 8, 10, 11)

        block = ctx.enter_context(nc.Block())

        @block.tensor
        def _(pe):
            seen = {}

            def wait(s, n):
                if seen.get(s.name, 0) < n:
                    pe.wait_ge(s, n)
                    seen[s.name] = n

            def bank_for(ring, job):
                n = ring.add(job)
                if n >= 4:
                    wait(ring.drained, n - 3)
                return ring.bank(job)

            def ready(ring, job):
                wait(ring.drained, ring.count(job))

            def chunk_ready(c):
                wait(w_low, c + 1)

            def transposes(tag, L, src, c):
                t0, t1 = FORMS[c]
                if tag != "oT":
                    wait(z_ready, z_count(tag, L, t1))
                for k in range(KD):
                    ring = RV if k % 2 == 0 else RA
                    b = bank_for(ring, (tag, L, c, k))
                    for t in range(t0, t1):
                        ins = pe.transpose(b[:, (t - t0) * P:(t - t0 + 1) * P],
                                           src[:, t, k * 128:(k + 1) * 128], ident[0:P, 0:P])
                    ins.then_inc(ring.filled, 1)

            def column_form_ready(tag, L, c):
                wait(col_low, 3 * col_form(tag, L) + 2 + c)

            def rows_product(job, chunk, t, high=YHIGH, low=YLOW):
                b = bank_for(RV, job)
                w = chunk % WSLOTS
                for k in range(KD):
                    for i, (X, Wp) in enumerate(high_low(high, low, WHIGH, WLOW)):
                        ins = pe.matmul(b[0:P, :], X[:, k, t * P:(t + 1) * P], Wp[:, w, k, :],
                                        start=(k == 0 and i == 0), stop=(k == KD - 1 and i == 2))
                ins.then_inc(RV.filled, 1)

            def columns_product(ring, job, chunk, m, c):
                b = bank_for(ring, job)
                n0, n, _ = SPANS[c]
                w = chunk % WSLOTS
                for k in range(KD):
                    for i, (Wp, X) in enumerate(high_low(WHIGH, WLOW, YHIGH, YLOW)):
                        ins = pe.matmul(b[:, 0:n], Wp[:, w, k, m * 128:(m + 1) * 128], X[:, k, n0:n0 + n],
                                        start=(k == 0 and i == 0), stop=(k == KD - 1 and i == 2))
                ins.then_inc(ring.filled, 1)

            wait(consts_ready, 1)
            wait(rows_loaded, 16 * 14)
            b = bank_for(RV, ("cols",))
            pe.transpose(b[:, 0:n_cols], VROWS[0:n_cols, :], ident[0:n_cols, 0:n_cols]).then_inc(vec_filled, 1)

            def edge_group(g):
                b = bank_for(RV, ("keys", g))
                wait(edge_exp_ready, 1)
                for j in range(EG):
                    ins = pe.transpose(b[0:P, j * P:(j + 1) * P], key[:, g * EG + j:g * EG + j + 1].to_broadcast([P, P]),
                                       ident[0:P, 0:P])
                ins.then_inc(vec_filled, 1)

            def edge_sums(g):
                b = bank_for(RV, ("sums", g))
                ready(RV, ("keys", g))
                wait(edge_parts_ready, 1)
                for j in range(EG):
                    ins = pe.matmul(b[0:P, j * 3 * H:(j + 1) * 3 * H], SAME[g % 2][:, j, :],
                                    EAP[:, g * EG + j].rearrange("p c h -> p (c h)"), start=True, stop=True)
                ins.then_inc(vec_filled, 1)

            transposes("y1", 0, Z, 0)
            transposes("y1", 0, Z, 1)
            for L in range(LAYERS):
                c0 = WPER * L
                chunk_ready(c0)
                column_form_ready("y1", L, 0)
                for m in range(KD):
                    columns_product(RV, ("q", L, m, 0), c0, m, 0)
                    if m == 1:
                        transposes("y1", L, Z, 2)
                column_form_ready("y1", L, 1)
                for m in range(KD):
                    columns_product(RV, ("q", L, m, 1), c0, m, 1)
                chunk_last[c0] = (RV, ("q", L, KD - 1, 1))
                if L == 0:
                    wait(proj_loaded, 32)
                    b = bank_for(RV, ("proj",))
                    for i in range(4):
                        ins = pe.transpose(b[:, i * 128:(i + 1) * 128], PROJR[:, i // 2, i % 2].rearrange("p c d -> p (c d)"), ident[:, :])
                    ins.then_inc(vec_filled, 1)
                chunk_ready(c0 + 1)
                for m in range(KD):
                    for c in range(2):
                        columns_product(RA, ("k", L, m, c), c0 + 1, m, c)
                chunk_last[c0 + 1] = (RA, ("k", L, KD - 1, 1))
                chunk_ready(c0 + 2)
                for t in range(T):
                    rows_product(("v", L, t), c0 + 2, t)
                chunk_last[c0 + 2] = (RV, ("v", L, T - 1))

                if L != GNN:
                    ready(RA, ("k", L, KD - 1, 1))
                    ready(RV, ("q", L, KD - 1, 1))

                    def features(tag, x, hp, t):
                        b = bank_for(RA, (tag, L, hp, t))
                        pe.matmul(b[0:P, :], x[:, hp, t * P:(t + 1) * P], PROJ[:, L % 2, :, :].rearrange("p c m -> p (c m)"),
                                  start=True, stop=True).then_inc(act_filled, 1)

                    def context(h):
                        b = bank_for(RV, ("ctxT", L, h))
                        for t in range(T):
                            ins = pe.matmul(b[0:DH + 1, 0:NF], V1[:, t, h, :], KP[:, h, t, :], start=(t == 0), stop=(t == T - 1))
                        ins.then_inc(vec_filled, 1)

                    def context_turned(h):
                        ready(RV, ("ctxT", L, h))
                        b = bank_for(RV, ("ctx", L, h))
                        for mh in range(2):
                            ins = pe.transpose(b[:, mh * (DH + 1):(mh + 1) * (DH + 1)], CTXT[:, h % 2, mh * 128:(mh + 1) * 128],
                                               ident[0:DH + 1, 0:DH + 1])
                        ins.then_inc(vec_filled, 1)

                    def attend(h):
                        ready(RV, ("qt", L, h, 2))
                        ready(RV, ("ctx", L, h))
                        for c in range(2):
                            n0, n1 = columns(c)
                            b = bank_for(RA, ("ocol", L, h, c))
                            for mh in range(2):
                                ins = pe.matmul(b[0:DH + 1, 0:n1 - n0], CTX[:, h % 2, mh, :], QPT[h % 2][:, mh * N + n0:mh * N + n1],
                                                start=(mh == 0), stop=(mh == 1))
                            ins.then_inc(act_filled, 1)

                    def attended_turned(h):
                        ready(RA, ("ocol", L, h, 1))
                        b = bank_for(RV, ("o", L, h))
                        for t in range(T):
                            ins = pe.transpose(b[0:P, t * (DH + 1):(t + 1) * (DH + 1)], OCOL[:, h % 2, t * P:(t + 1) * P],
                                               ident[0:DH + 1, 0:DH + 1])
                        ins.then_inc(vec_filled, 1)

                    ready(RV, ("proj",))
                    for hp in range(H // 2):
                        for t in range(T):
                            features("kd", KT, hp, t)
                    wait(squares_ready, 2 * L + 2)
                    for q in range(2):
                        for c in range(2):
                            n0, n1 = columns(c)
                            b = bank_for(RV, ("dgt", L, q, c))
                            for k in range(KD):
                                ins = pe.matmul(b[0:H, 0:n1 - n0], halves[:, k, :], (SQQ, SQK)[q][:, k, n0:n1],
                                                start=(k == 0), stop=(k == KD - 1))
                            ins.then_inc(vec_filled, 1)
                    b = bank_for(RV, ("kmax", L))
                    wait(kmax_part, H * L + H)
                    pe.transpose(b[0:H, 0:P], KM[:, :], ident[0:P, 0:P]).then_inc(vec_filled, 1)
                    for t in range(2):
                        features("qd", QT, 0, t)
                    b = bank_for(RV, ("kmax_all", L))
                    wait(kdiag_ready, L + 1)
                    pe.matmul(b[0:P, 0:H], ones[0:H, 0:P], KDIAG[:, :], start=True, stop=True).then_inc(vec_filled, 1)
                    ready(RV, ("dgt", L, 1, 1))
                    b = bank_for(RV, ("diag", L))
                    for t in range(T):
                        for q in range(2):
                            ins = pe.transpose(b[0:P, (2 * t + q) * H:(2 * t + q + 1) * H], DGT[:, q, t * P:(t + 1) * P], ident[0:H, 0:H])
                    ins.then_inc(vec_filled, 1)
                    for t in range(2, T):
                        features("qd", QT, 0, t)

                    def queries_turned(h, i):
                        if h % 2 == 0:
                            ready(RA, ("qd", L, h // 2, T - 1))
                        b = bank_for(RV, ("qt", L, h, i))
                        for blk in range(4 * i, min(4 * i + 4, 2 * T)):
                            mh, t = blk // T, blk % T
                            ins = pe.transpose(b[:, (blk - 4 * i) * P:(blk - 4 * i + 1) * P],
                                               QP[:, h % 2, t, mh * 128:(mh + 1) * 128], ident[0:P, 0:P])
                        ins.then_inc(vec_filled, 1)

                    for i in range(3):
                        queries_turned(0, i)
                    for h in range(H):
                        wait(kp_ready, H * L + h + 1)
                        context(h)
                        if h:
                            attended_turned(h - 1)
                        if h + 1 < H:
                            queries_turned(h + 1, 0)
                        context_turned(h)
                        if h + 1 < H:
                            queries_turned(h + 1, 1)
                            queries_turned(h + 1, 2)
                        attend(h)
                        if h % 2 == 0 and h + 2 < H:
                            for t in range(T):
                                features("qd", QT, h // 2 + 1, t)
                    attended_turned(H - 1)
                    ready(RV, ("o", L, H - 1))
                else:
                    ready(RA, ("k", L, KD - 1, 1))
                    ready(RV, ("v", L, T - 1))
                    wait(queries_apart, 2)

                    def scores(i):
                        dt, h = divmod(i, H)
                        for c in range(2):
                            n0, n1 = columns(c)
                            b = bank_for(RV, ("s", i, c))
                            pe.matmul(b[0:P, 0:n1 - n0], KT[:, h // 2, dt * P:(dt + 1) * P],
                                      (QT, QODD)[h % 2][:, h // 2, n0:n1], start=True, stop=True).then_inc(vec_filled, 1)

                    def probs_turned(i):
                        wait(p_scaled, i + 1)
                        for j in range(2):
                            b = bank_for(RA, ("pt", i, j))
                            for s in range(4 * j, min(4 * j + 4, T)):
                                ins = pe.transpose(b[0:P, (s - 4 * j) * P:(s - 4 * j + 1) * P],
                                                   TS[i % NTS][:, s * P:(s + 1) * P], ident[0:P, 0:P])
                            ins.then_inc(act_filled, 1)

                    def gather_messages(i):
                        ready(RA, ("pt", i, 1))
                        b = bank_for(RA, ("agg", i))
                        r0 = DH * (i % 2)
                        for s in range(T):
                            ins = pe.matmul(b[r0:r0 + DH, 0:P], V1[:, s, i % H, 0:DH], PT[i % 2][:, s, :],
                                            start=(s == 0), stop=(s == T - 1))
                        ins.then_inc(act_filled, 1)

                    for i in range(T * H + 6):
                        if i < T * H:
                            scores(i)
                        if 0 <= i - 5 < T * H:
                            probs_turned(i - 5)
                        if 0 <= i - 6 < T * H:
                            gather_messages(i - 6)
                    ready(RA, ("agg", T * H - 1))

                chunk_ready(c0 + 3)
                if L != GNN:
                    transposes("oT", L, O, 0)
                    transposes("oT", L, O, 1)
                    transposes("oT", L, O, 2)
                for t in range(T):
                    if t >= T - 2:
                        transposes("y2", L, z_of("y2", L), t - (T - 2))
                    if L != GNN:
                        column_form_ready("oT", L, 0 if t < CHUNKS[0][1] else 1)
                        rows_product(("x1", L, t), c0 + 3, t)
                    else:
                        wait(agg_low, 1 if t < T - 1 else 2)
                        rows_product(("x1", L, t), c0 + 3, t, AGGHIGH, AGGLOW)
                chunk_last[c0 + 3] = (RV, ("x1", L, T - 1))

                def mlp_in(g):
                    ch = c0 + W1_AT[g]
                    chunk_ready(ch)
                    column_form_ready("y2", L, 0)
                    if g == 0:
                        for f in range(4):
                            columns_product(RA, ("h", L, f, 0), ch, f, 0)
                            if f == 1:
                                transposes("y2", L, z_of("y2", L), 2)
                    column_form_ready("y2", L, 1)
                    for f in range(4 * g, 4 * g + 4):
                        for c in range(2) if g else (1,):
                            columns_product(RA, ("h", L, f, c), ch, f % 4, c)
                        if L == 0:
                            for e in range(5 * f // 4, 5 * (f + 1) // 4):
                                edge_group(e)
                                if e:
                                    edge_sums(e - 1)
                    if L == 0 and g == 3:
                        edge_sums(EB // EG - 1)
                    chunk_last[ch] = (RA, ("h", L, 4 * g + 3, 1))

                def mlp_out(g):
                    ch = c0 + W2_AT[g]
                    chunk_ready(ch)
                    for t in range(T):
                        if g == 3 and t >= T - 2:
                            transposes(*(("y1", L + 1) if L + 1 < LAYERS else ("yf", 0)), Z, t - (T - 2))
                        b = bank_for(RV, ("x2", L, g, t))
                        wait(hid_low, FM * L + 4 * g + 4)
                        for f in range(4 * g, 4 * g + 4):
                            for i, (X, Wp) in enumerate(high_low(HTHIGH, HTLOW, WHIGH, WLOW)):
                                ins = pe.matmul(b[0:P, :], X[:, f % 8, t * P:(t + 1) * P], Wp[:, ch % WSLOTS, f % 4, :],
                                                start=(f % 4 == 0 and i == 0), stop=(f % 4 == 3 and i == 2))
                        ins.then_inc(vec_filled, 1)
                    chunk_last[ch] = (RV, ("x2", L, g, T - 1))

                mlp_in(0)
                for g in range(1, 4):
                    mlp_in(g)
                    mlp_out(g - 1)
                mlp_out(3)

            transposes("yf", 0, Z, 2)
            ready(RV, ("yf", 0, 2, 2))
            ready(RA, ("yf", 0, 2, 3))
            wait(gate_loaded, 16 * 5)
            for c in range(2):
                n0, n1 = columns(c)
                b = bank_for(RV, ("gateT", c))
                for k in range(KD):
                    ins = pe.matmul(b[0:NE, 0:n1 - n0], GATEW[:, k, :], YT[:, k, n0:n1], start=(k == 0), stop=(k == KD - 1))
                ins.then_inc(vec_filled, 1)

            def shared_hidden(t):
                for half in range(2):
                    b = bank_for(RV, ("sh", t, half))
                    for k in range(KD):
                        ins = pe.matmul(b[0:P, 0:NI], YT[:, k, t * P:(t + 1) * P], SW1[:, k, half * NI:(half + 1) * NI],
                                        start=(k == 0), stop=(k == KD - 1))
                    ins.then_inc(vec_filled, 1)

            ready(RV, ("gateT", 1))
            b = bank_for(RV, ("gate",))
            for t in range(T):
                ins = pe.transpose(b[0:P, t * NE:(t + 1) * NE], LOGITT[:, t * P:(t + 1) * P], ident[0:NE, 0:NE])
            ins.then_inc(vec_filled, 1)
            wait(ffn_w_loaded, 16 * 2)
            shared_hidden(0)
            shared_hidden(1)
            b = bank_for(RV, ("rank",))
            wait(picked_ready, 1)
            wait(tiles_ready, 1)
            for t in range(T + 1):
                for u in range(min(t, T)):
                    ins = pe.matmul(b[0:P, t * NE:(t + 1) * NE], ONESP, PICKED[:, u, :], start=(u == 0), stop=(t == T and u == T - 1))
                if t < T:
                    ins = pe.matmul(b[0:P, t * NE:(t + 1) * NE], UPPER, PICKED[:, t, :], start=(t == 0), stop=True)
            ins.then_inc(vec_filled, 1)
            for t in range(T):
                if t and t + 1 < T:
                    shared_hidden(t + 1)
                wait(ste_ready, t + 1)
                b = bank_for(RA, ("st", t))
                for k in range(KI):
                    ins = pe.transpose(b[:, k * P:(k + 1) * P], TE[t % 2][0:P, k * 128:(k + 1) * 128], ident[0:P, 0:P])
                ins.then_inc(act_filled, 1)
                ready(RA, ("st", t))
                b = bank_for(RV, ("so", t))
                for k in range(KI):
                    ins = pe.matmul(b[0:P, :], TET[t % 2][:, k * 128:k * 128 + P], SW2[:, k, :], start=(k == 0), stop=(k == KI - 1))
                ins.then_inc(vec_filled, 1)
            ready(RV, ("so", T - 1))

            def turn_tokens(b, j, s):
                pe.wait_ge(xg_loaded[s], 16 * (j + 1))
                if not (isinstance(b, int) and b < 2):
                    pe.wait_ge(xgt_ready, b - 1)
                for k in range(KD):
                    ins = pe.transpose(XT_BANK[s][:, k * 128:(k + 1) * 128], XG[s][:, k * 128:(k + 1) * 128], ident[:, :])
                ins.then_inc(xt_filled, 1)

            def side_of(b):
                return pe.value_load(BLKS[0:1, bass.ds(b, 1)], min_val=0, max_val=1)

            def hidden(b, j, s):
                side = side_of(b)
                pe.wait_ge(xgt_ready, b + 1)
                if not (isinstance(b, int) and b < 2):
                    pe.wait_ge(h_drained, b - 1)
                for half in range(2):
                    pe.wait_ge(w1_there[half], b + 1)
                    for k in range(KD):
                        ins = pe.matmul(H_BANK[s][half][:, 0:NI], XGT[s][:, k * 128:(k + 1) * 128],
                                        EW1[:, bass.ds(side, 1), k, half * NI:(half + 1) * NI], start=(k == 0), stop=(k == KD - 1))
                    ins.then_inc((half_filled, h_filled)[half], 1)

            def turn_hidden(b, j, s):
                pe.wait_ge(te_ready, b + 1)
                if not (isinstance(b, int) and b < 1):
                    pe.wait_ge(tet_ready, b)
                for k in range(KI):
                    ins = pe.transpose(TT_BANK[:, k * 128:(k + 1) * 128], TE[s][:, k * 128:(k + 1) * 128], ident[:, :])
                ins.then_inc(tt_filled, 1)

            def output(b, j, s):
                pe.wait_ge(tet_ready, b + 1)
                pe.wait_ge(w2_loaded[s], 16 * (j + 1))
                if not (isinstance(b, int) and b < 1):
                    pe.wait_ge(o_drained, b)
                for k in range(KI):
                    ins = pe.matmul(O_BANK[:, :], TET[s][:, k * 128:(k + 1) * 128], EW2[:, s, k, :], start=(k == 0), stop=(k == KI - 1))
                ins.then_inc(o_filled, 1)

            def step(b, j, s):
                last = isinstance(b, int) and b >= BLOCKS
                if isinstance(b, int) and b == 0:
                    turn_tokens(0, 0, 0)
                if not last:
                    hidden(b, j, s)
                if not (isinstance(b, int) and b == 0):
                    turn_hidden(b - 1, j - 1 + s, 1 - s)
                if not last and not (isinstance(b, int) and b == BLOCKS - 1):
                    turn_tokens(b + 1, j + s, 1 - s)
                if not (isinstance(b, int) and b == 0):
                    output(b - 1, j - 1 + s, 1 - s)

            pe.wait_ge(routed, 2)
            run_blocks(pe, step)


        @block.sync
        def _(sp):
            x_rows = A["x"].rearrange("(t p) d -> p t d", p=P)
            sp.dma_start(Z, x_rows).then_inc(x_loaded, 16)
            for group, prefix, names in (("mix", "L0_mix_", ("ln1_g", "ln1_b", "bq", "bk", "ln2_g", "ln2_b", "b1")),
                                         ("gnn", "L0_gnn_", ("ln1_g", "ln1_b", "bq", "bk", "ln2_g", "ln2_b", "b1"))):
                for name in names:
                    if group == "mix":
                        v = A[prefix + name].rearrange("l (k p) -> (l k) p", p=128)
                        r0 = col_at[name, 0]
                    elif name in ("bq", "bk"):
                        j = ("bq", "bk").index(name)
                        v = A[prefix + "bqkv"][j * D:(j + 1) * D].rearrange("(k p) -> k p", p=128)
                        r0 = col_at[name, GNN]
                    else:
                        v = A[prefix + name].rearrange("(k p) -> k p", p=128)
                        r0 = col_at[name, GNN]
                    sp.dma_start(VROWS[r0:r0 + v.shape[0], :], v).then_inc(rows_loaded, 16)

            for c in range(2):
                sp.dma_start(PROJR[:, :, :, c, :], A["L0_mix_proj"].rearrange("l (a p) d -> p l a d", p=128)).then_inc(proj_loaded, 16)

            for row0, v in ((0, A["L0_ffn_expert_act"]), (NE, A["L0_ffn_shared_act"].unsqueeze(0))):
                sp.dma_start(PRM[row0:row0 + v.shape[0], 0:5], v).then_inc(prm_in, 16)

            def load_chunk(c):
                L, j = divmod(c, WPER)
                mixed = L != GNN
                if j < 3:
                    src = (A["L0_mix_" + ("Wq", "Wk", "Wv")[j]][L] if mixed
                           else A["L0_gnn_Wqkv"][:, j * D:(j + 1) * D])
                elif j == 3:
                    src = A["L0_mix_Wo"][L] if mixed else A["L0_gnn_Wo"]
                elif j in W1_AT:
                    g = W1_AT.index(j)
                    src = (A["L0_mix_W1"][L] if mixed else A["L0_gnn_W1"])[:, g * 512:(g + 1) * 512]
                else:
                    g = W2_AT.index(j)
                    src = (A["L0_mix_W2"][L] if mixed else A["L0_gnn_W2"])[g * 512:(g + 1) * 512, :]
                if c >= WSLOTS:
                    ring, job = chunk_last[c - WSLOTS]
                    sp.wait_ge(ring.filled, ring.count(job))
                sp.dma_start(weight(c), src.rearrange("(k p) n -> p k n", p=128)).then_inc(w_loaded[c % WSLOTS], 16)

            for c in range(WPER * LAYERS):
                load_chunk(c)
                if c == WPER + 2:
                    sp.wait_ge(vec_drained, RV.count(("x2", 0, 3, T - 1)))
                    for j, v in enumerate((A["L0_gnn_bqkv"][2 * D:3 * D], A["L0_gnn_bo"], A["L0_gnn_b2"])):
                        sp.dma_start(ROWB[:, 0, j, :], v.partition_broadcast(P)).then_inc(rowb_again, 16)
                if c == WPER * GNN + 5:
                    sp.wait_ge(vec_filled, RV.count(("s", T * H - 1, 1)))
                    sp.dma_start(XAGAIN, x_rows).then_inc(x_again, 16)
                    sp.dma_start(GATEW, A["L0_ffn_gate_w"].rearrange("(k p) n -> p k n", p=128)).then_inc(gate_loaded, 16)
                    sp.dma_start(GATEB, A["L0_ffn_gate_b"].partition_broadcast(P)).then_inc(gate_loaded, 16)
                    sp.dma_start(SW2, A["L0_ffn_shared_w2"].rearrange("(k p) n -> p k n", p=128)).then_inc(gate_loaded, 16)
                    sp.dma_start(SB2, A["L0_ffn_shared_b2"].partition_broadcast(P)).then_inc(gate_loaded, 16)
                    sp.wait_ge(prm_stored, 16)
                    sp.dma_start(SACT, act_table[NE].partition_broadcast(P)).then_inc(gate_loaded, 16)

            ring, job = chunk_last[WPER * GNN + 10]
            sp.wait_ge(ring.filled, ring.count(job))
            sp.dma_start(SW1, A["L0_ffn_shared_w1"].rearrange("(k p) n -> p k n", p=128)).then_inc(ffn_w_loaded, 16)
            sp.dma_start(SB1, A["L0_ffn_shared_b1"].partition_broadcast(P)).then_inc(ffn_w_loaded, 16)

            def load_w1(e, side, before=0, past=None):
                for half in range(2):
                    if past is not None:
                        sp.wait_ge(w1_loaded[side][half], 16 * before)
                        sp.wait_ge((half_filled, h_filled)[half], past)
                    sp.dma_start(EW1[:, side, :, half * NI:(half + 1) * NI],
                                 A["L0_ffn_expert_w1"][bass.ds(e, 1), :, half * NI:(half + 1) * NI].rearrange("o (k p) n -> p (o k) n", p=128))\
                        .then_inc(w1_loaded[side][half], 16)

            def past_of(e):
                return sp.value_load(PAST[0:1, bass.ds(e, 1)], min_val=1, max_val=BLOCKS + 1)

            sp.wait_ge(vec_filled, RV.count(("x2", GNN, 3, T - 1)))
            load_w1(0, 0)
            load_w1(1, 1)
            sp.wait_ge(routed, 2)
            with sp.Fori(1, NE // 2) as i:
                for side in range(2):
                    load_w1(2 * i + side, side, i, past_of(2 * i + (side - 2)))
            for t in range(T):
                sp.wait_ge(y_ready, t + 1)
                sp.dma_start(out.rearrange("(t p) d -> p t d", p=P)[:, t, :], MX[:, t, :]).then_inc(y_stored, 16)
            sp.wait_ge(y_stored, 16 * T)

        @block.gpsimd
        def _(pool):
            nc.gpsimd.memset(ident[:, :], 0.0).then_inc(pool_step, 1)
            nc.gpsimd.memset(lower[:, :], 1.0).then_inc(pool_step, 1)
            nc.gpsimd.memset(ones[:, :], 1.0).then_inc(pool_step, 1)
            pool.wait_ge(pool_step, 3)
            nc.gpsimd.affine_select(out=ident[:, :], in_=ident[:, :], compare_op=ALU.not_equal, fill=1.0, base=0,
                                    pattern=[[-1, 128]], channel_multiplier=1).then_inc(pool_step, 1)
            nc.gpsimd.affine_select(out=lower[:, :], in_=lower[:, :], compare_op=ALU.is_gt, fill=0.0, base=0,
                                    pattern=[[-1, P]], channel_multiplier=1).then_inc(pool_step, 1)
            pool.wait_ge(pool_step, 5)
            nc.gpsimd.iota(spare_i[:, :], pattern=[[0, 1]], base=PAIRS, channel_multiplier=1).then_inc(pool_step, 1)
            pool.wait_ge(pool_step, 6)
            nc.gpsimd.memset(zero[:, :], 0.0).then_inc(consts_ready, 1)
            pool.wait_ge(consts_ready, 1)
            pool.wait_ge(w_high, 1)
            nc.gpsimd.tensor_tensor(WLOW[:, 0, :, :], weight(0), WHIGH[:, 0, :, :].bitcast(F32), ALU.subtract).then_inc(w_low, 1)
            pool.wait_ge(w_loaded[1], 16)
            for L in range(2):
                for j, name in enumerate(("bv", "bo", "b2")):
                    pool.dma_start(ROWB[:, L, j, :], A["L0_mix_" + name][L].partition_broadcast(P)).then_inc(rowb_loaded, 16)
            pool.dma_start(src_i[:, :], A["src"].rearrange("(p j) -> p j", p=P)).then_inc(edges_loaded, 16)
            pool.dma_start(dst_i[:, :], A["dst"].rearrange("(p j) -> p j", p=P)).then_inc(edges_loaded, 16)
            pool.dma_start(EA[:, :, :], A["edge_attr_8"].rearrange("(p j) h -> p j h", p=P)).then_inc(attrs_loaded, 16)
            pool.dma_start(EA2[:, :, :], A["edge_attr_8_n2"].rearrange("(p j) h -> p j h", p=P)).then_inc(attrs_loaded, 16)
            pool.wait_ge(w_loaded[2], 16)
            for t in range(T):
                pool.dma_start(pair_table[t * P * N:(t + 1) * P * N, :].rearrange("(p s) h -> p (s h)", p=P)
                               .rearrange("p (r c) -> p r c", r=H),
                               zero[0:P, :].unsqueeze(1).to_broadcast([P, H, N])).then_inc(table_zeroed, 16)
            pool.dma_start(pair_table[PAIRS:PAIRS + 128, :], zero[:, 0:H]).then_inc(table_zeroed, 16)
            for b in range(BLOCKS):
                pool.dma_start(slot_in[b * BLOCK:(b + 1) * BLOCK, :], zero[:, 0:D]).then_inc(slots_zeroed, 16)
            pool.wait_ge(edge_max_part, 1)
            nc.gpsimd.partition_all_reduce(emaxa[:, :], emax[:, :], P, RMAX).then_inc(edge_max_all, 1)
            pool.wait_ge(table_zeroed, 16 * (T + 1))
            pool.wait_ge(idx_ready, 1)
            for j in range(EB):
                pool.indirect_dma_start(out=pair_table[:, :], out_offset=bass.IndirectOffsetOnAxis(ap=idx[:, j:j + 1], axis=0),
                                        in_=VC[:, j, :], in_offset=None, compute_op=ALU.add).then_inc(scattered, 16)
                pool.wait_ge(scattered, 16 * (j + 1))

            def load_pairs(dt):
                if dt == 0:
                    pool.wait_ge(vec_filled, RV.count(("x2", 1, 3, T - 1)))
                pool.dma_start(PAIRW[dt % 2], pair_table[dt * P * N:(dt + 1) * P * N, :].rearrange("(p s) h -> p s h", p=P))\
                    .then_inc(pairw_loaded[dt % 2], 16)

            load_pairs(0)
            load_pairs(1)
            nc.gpsimd.memset(QODD[0:DH, :, :], 0.0).then_inc(queries_apart, 1)
            nc.gpsimd.memset(QT[DH:2 * DH, :, :], 0.0).then_inc(queries_apart, 1)
            for i in range(T * H):
                pool.wait_ge(rden_ready, i + 1)
                nc.gpsimd.tensor_scalar(TS[i % NTS], TS[i % NTS], rden[:, i % NTS:i % NTS + 1], 1.0, ALU.mult, ALU.mult).then_inc(p_scaled, 1)
                if (i + 1) % H == 0 and (i + 1) // H + 1 < T:
                    load_pairs((i + 1) // H + 1)
            pool.wait_ge(act_filled, RA.count(("pt", T * H - 1, 1)))
            nc.gpsimd.iota(COUNT_I, pattern=[[1, BLOCKS]], base=0, channel_multiplier=0).then_inc(count_ready, 1)
            nc.gpsimd.memset(UPPER, 1.0).then_inc(pool_step, 1)
            nc.gpsimd.memset(ONESP, 1.0).then_inc(pool_step, 1)
            pool.wait_ge(pool_step, 8)
            nc.gpsimd.affine_select(out=UPPER, in_=UPPER, compare_op=ALU.is_gt, fill=0.0, base=0,
                                    pattern=[[1, P]], channel_multiplier=-1).then_inc(tiles_ready, 1)
            pool.wait_ge(slots_zeroed, 16 * BLOCKS)
            pool.wait_ge(routed, 1)
            for t in range(T):
                for c in range(2):
                    pool.indirect_dma_start(out=slot_in[:, :], out_offset=bass.IndirectOffsetOnAxis(ap=SLOT[:, 2 * t + c:2 * t + c + 1], axis=0),
                                            in_=Z[:, t, :], in_offset=None).then_inc(slots_filled, 16)

            def counts(b):
                return [pool.value_load(BLKW[q][0:1, bass.ds(b, 1)], min_val=16, max_val=16 * NE // 2) for q in range(2)]

            def tell(i, there):
                nc.gpsimd.tensor_tensor(zero[0:1, i:i + 1], zero[0:1, 2:3], zero[0:1, 3:4], ALU.add).then_inc(there, 1)

            def step(b, j, s):
                if not (isinstance(b, int) and b >= BLOCKS):
                    loaded = counts(b)
                    for half in range(2):
                        for q in range(2):
                            pool.wait_ge(w1_loaded[q][half], loaded[q])
                        if not (isinstance(b, int) and b < 2):
                            pool.wait_ge(w1_there[half], b - 1)
                        tell(4 + 2 * half + s, w1_there[half])
                    pool.wait_ge(row_loaded[s], 48 * (j + 1))
                    if not (isinstance(b, int) and b < 2):
                        pool.wait_ge(o_drained, b - 1)
                    nc.gpsimd.tensor_tensor(zero[0:1, s:s + 1], zero[0:1, 2:3], zero[0:1, 3:4], ALU.add)
                    if isinstance(b, int) and b == 1:
                        pool.wait_ge(vec_drained, RV.count(("so", T - 1)))
                    nc.gpsimd.partition_broadcast(ROWS[s], ROW1[s], 128).then_inc(rows_spread, 1)
                if not (isinstance(b, int) and b < 2):
                    pool.wait_ge(o_drained, b - 1)
                    pool.dma_start(slot_out[bass.ds((b - 2) * BLOCK, BLOCK), :], OG[s]).then_inc(stored[s], 16)

            pool.wait_ge(routed, 2)
            run_blocks(pool, step)
            pool.wait_ge(o_drained, BLOCKS)
            pool.dma_start(slot_out[(BLOCKS - 1) * BLOCK:BLOCKS * BLOCK, :], OG[(BLOCKS - 1) % 2]).then_inc(stored[(BLOCKS - 1) % 2], 16)
            pool.wait_ge(stored[0], 16 * ((BLOCKS + 1) // 2))
            pool.wait_ge(stored[1], 16 * (BLOCKS // 2))
            for t in range(T):
                for c in range(2):
                    pool.indirect_dma_start(out=GOT[:, t, c, :], out_offset=None, in_=slot_out[:, :],
                                            in_offset=bass.IndirectOffsetOnAxis(ap=SLOT[:, 2 * t + c:2 * t + c + 1], axis=0)).then_inc(gathered[t], 16)


        @block.scalar
        def _(act):
            seen = {}
            steps = [0]

            def wait(s, n):
                if seen.get(s.name, 0) < n:
                    act.wait_ge(s, n)
                    seen[s.name] = n

            drained = [0]

            def fill_of(job):
                assert RA.at[job] == drained[0], (job, drained[0])
                drained[0] += 1
                wait(act_filled, RA.count(job))
                return RA.bank(job)

            def std(n, t):
                wait(var_ready, T * n + t + 1)
                nc.scalar.activation(sd[:, t:t + 1], moments(n)[0][:, t, 1:2], ACT.Sqrt, bias=eps_ln[0:P, :]).then_inc(std_ready, 1)

            def high_part(c):
                wait(w_loaded[c % WSLOTS], 16 * (c // WSLOTS + 1))
                nc.scalar.copy(WHIGH[:, c % WSLOTS, :, :], weight(c)).then_inc(w_high, 1)

            def from_column_form(tag, L, c):
                n0, n1 = FORMS[c][0] * P, FORMS[c][1] * P
                for k in (1, 3):
                    b = fill_of((tag, L, c, k))
                    if tag == "y1":
                        g, bb = col("ln1_g", L, k), col("ln1_b", L, k)
                    elif tag == "y2":
                        g, bb = col("ln2_g", L, k), col("ln2_b", L, k)
                    else:
                        g, bb = 1.0, 0.0
                    ins = nc.scalar.activation(YT[:, k, n0:n1], b[:, 0:n1 - n0], ACT.Identity, bias=bb, scale=g)
                    if tag != "yf":
                        ins = nc.scalar.activation(YHIGH[:, k, n0:n1], b[:, 0:n1 - n0], ACT.Identity, bias=bb, scale=g)
                    ins.then_inc(act_drained, 1)
                if tag != "yf":
                    wait(vec_drained, RV.count((tag, L, c, 2)))
                    nc.scalar.copy(YHIGH[:, 0::2, n0:n1], YT[:, 0::2, n0:n1]).then_inc(col_high, 1)

            def begin_form(tag, L):
                for t in range(T - 2):
                    std(NORM_OF[tag, L], t)
                for c in range(2):
                    from_column_form(tag, L, c)
                for t in range(T - 2, T):
                    std(NORM_OF[tag, L], t)

            for t in range(T):
                std(0, t)
            high_part(0)
            wait(vec_drained, RV.count(("cols",)))
            for L in range(LAYERS):
                if L == 0:
                    for t in range(T):
                        std(NORM_OF["y1", L], t)
                if L == 1:
                    begin_form("y1", L)
                else:
                    from_column_form("y1", L, 0)
                    from_column_form("y1", L, 1)
                from_column_form("y1", L, 2)
                for c in range(WPER * L + 1, WPER * L + 3):
                    high_part(c)
                for m in range(KD):
                    for c in range(2):
                        n0, n, skip = SPANS[c]
                        b = fill_of(("k", L, m, c))
                        wait(kcol_ready, 1)
                        nc.scalar.activation(KT[:, m, n0 + skip:n0 + n], b[:, skip:n], ACT.Identity, bias=col("bk", L, m),
                                             scale=QK_NORM if L != GNN else 1.0).then_inc(act_drained, 1)
                if L == GNN:
                    high_part(WPER * L + 3)
                if L != GNN:
                    wait(act_drained, RA.count(("k", L, KD - 1, 1)))
                    nc.scalar.activation(SQK, KT, ACT.Square).then_inc(squares_ready, 1)
                    wait(vec_drained, RV.count(("q", L, KD - 1, 1)))
                    nc.scalar.activation(SQQ, QT, ACT.Square).then_inc(squares_ready, 1)

                    for hp in range(H // 2):
                        for t in range(T):
                            b = fill_of(("kd", L, hp, t))
                            nc.scalar.copy(KP[:, 2 * hp:2 * hp + 2, t, :], b[0:P, :].rearrange("p (c m) -> p c m", c=2)).then_inc(act_drained, 1)

                    high_part(WPER * L + 3)
                    high_part(WPER * L + 4)

                    def q_exp(hp):
                        if hp:
                            wait(vec_filled, RV.count(("qt", L, 2 * hp - 1, 2)))
                        for t in range(T):
                            b = fill_of(("qd", L, hp, t))
                            wait(qbias_ready, (H // 2 * L + hp) * T + t + 1)
                            for c in range(2):
                                ins = nc.scalar.activation(QP[:, c, t, :], b[0:P, c * NF:(c + 1) * NF],
                                                           ACT.Exp, bias=NQ[:, 2 * hp + c, t:t + 1])
                            ins.then_inc(act_drained, 1)

                    def k_exp(h):
                        wait(kbias_ready, L + 1)
                        for t in range(T):
                            ins = nc.scalar.activation(KP[:, h, t, :], KP[:, h, t, :], ACT.Exp, bias=NK[:, t, h:h + 1])
                        ins.then_inc(kexp_done, 1)

                    q_exp(0)
                    k_exp(0)
                    k_exp(1)
                    for h in range(H):
                        for c in range(2):
                            n0, n1 = columns(c)
                            b = fill_of(("ocol", L, h, c))
                            nc.scalar.copy(OCOL[:, h % 2, n0:n1], b[0:DH + 1, 0:n1 - n0]).then_inc(act_drained, 1)
                        if h % 2 == 0 and h + 2 < H:
                            q_exp(h // 2 + 1)
                            k_exp(h + 2)
                            k_exp(h + 3)
                        if h == 1:
                            high_part(WPER * L + 5)
                        if L == 0 and h == 3:
                            wait(edge_sub_ready, 1)
                            nc.scalar.activation(EA[:, :, :], EA[:, :, :], ACT.Exp).then_inc(edge_exp_ready, 1)
                else:
                    for i in range(T * H + 6):
                        if 0 <= i - 1 < T * H:
                            j = i - 1
                            wait(smax_ready, j + 1)
                            nc.scalar.activation(TS[j % NTS], TS[j % NTS], ACT.Exp, bias=negmax[:, j % NTS:j % NTS + 1])\
                                .then_inc(sexp_done, 1)
                        if 0 <= i - 5 < T * H:
                            j = i - 5
                            for q, (s0, s1) in enumerate(((0, 4), (4, 5))):
                                b = fill_of(("pt", j, q))
                                if j >= 2:
                                    wait(act_filled, RA.count(("agg", j - 2)))
                                nc.scalar.copy(PT[j % 2][:, s0:s1, :], b[0:P, 0:(s1 - s0) * P].rearrange("p (s d) -> p s d", d=P))\
                                    .then_inc(act_drained, 1)
                        if 0 <= i - 6 < T * H:
                            j = i - 6
                            dt, h = divmod(j, H)
                            b = fill_of(("agg", j))
                            r0 = DH * (h % 2)
                            nc.scalar.copy(AGG[r0:r0 + DH, h // 2, dt * P:(dt + 1) * P], b[r0:r0 + DH, 0:P]).then_inc(act_drained, 1)
                        if i in (2, 10):
                            high_part(WPER * L + (4 if i == 2 else 5))
                        for j, t0, t1 in ((T * H - 2, 0, T - 1), (T * H - 1, T - 1, T)):
                            if i - 6 == j:
                                wait(act_filled, RA.count(("pt", T * H - 1, 1)))
                                wait(act_drained, RA.count(("agg", T * H - 1 if t1 == T else (T - 1) * H - 1)))
                                nc.scalar.copy(AGGHIGH[:, :, t0 * P:t1 * P], AGG[:, :, t0 * P:t1 * P]).then_inc(agg_high, 1)
                if L != GNN:
                    for c in range(3):
                        from_column_form("oT", L, c)
                begin_form("y2", L)

                def take_hidden(f, c):
                    n0, n, skip = SPANS[c]
                    b = fill_of(("h", L, f, c))
                    nc.scalar.activation(HT[:, f % 8, n0 + skip:n0 + n], b[:, skip:n], ACT.Gelu, bias=col("b1", L, f))\
                        .then_inc(act_drained, 1)

                for f in range(4):
                    take_hidden(f, 0)
                    if f == 1:
                        from_column_form("y2", L, 2)
                for f in range(FM):
                    if L == 0 and f == 0:
                        wait(prm_step_d, 1)
                        nc.scalar.activation(PRMT[:, 2:4], PRMT[:, 0:2], ACT.Exp).then_inc(prm_step_a, 1)
                        wait(prm_step_a, 1)
                        nc.scalar.activation(PRMT[:, 0:2], PRMT[:, 2:4], ACT.Ln, bias=1.0).then_inc(prm_step_a, 1)
                        wait(prm_done, 1)
                        act.dma_start(act_table[:, :], PRM[:, :]).then_inc(prm_stored, 16)
                    for c in {2: (6,), 8: (7, 8), 10: (9,), 12: (10,), 14: (11,)}.get(f, ()):
                        high_part(WPER * L + c)
                    if f >= 4:
                        take_hidden(f, 0)
                    take_hidden(f, 1)
                    wait(act_drained, drained[0])
                    nc.scalar.copy(HTHIGH[:, f % 8, :], HT[:, f % 8, :]).then_inc(hid_high, 1)
                if L + 1 < LAYERS:
                    high_part(WPER * (L + 1))
            begin_form("yf", 0)
            from_column_form("yf", 0, 2)
            wait(logits_ready, 1)
            nc.scalar.activation(LOGIT, LOGIT, ACT.Exp).then_inc(gate_exp, 1)
            def load_w2(b, s):
                e = act.value_load(BLKE[0:1, bass.ds(b, 1)], min_val=0, max_val=NE - 1)
                if not (isinstance(b, int) and b < 2):
                    act.wait_ge(o_filled, b - 1)
                act.dma_start(EW2[:, s], A["L0_ffn_expert_w2"][bass.ds(e, 1)].rearrange("o (k p) n -> p (o k) n", p=128))\
                    .then_inc(w2_loaded[s], 16)

            def load_tokens(b, s):
                e = act.value_load(BLKE[0:1, bass.ds(b, 1)], min_val=0, max_val=NE - 1)
                if not (isinstance(b, int) and b < 2):
                    act.wait_ge(xt_filled, b - 1)
                act.dma_start(XG[s], slot_in[bass.ds(b * BLOCK, BLOCK), :]).then_inc(xg_loaded[s], 16)
                if not (isinstance(b, int) and b < 2):
                    act.wait_ge(rows_spread, b - 1)
                act.dma_start(ROW1[s][:, 0:2 * NI], A["L0_ffn_expert_b1"][bass.ds(e, 1)]).then_inc(row_loaded[s], 16)
                act.dma_start(ROW1[s][:, 2 * NI:2 * NI + D], A["L0_ffn_expert_b2"][bass.ds(e, 1)]).then_inc(row_loaded[s], 16)
                act.dma_start(ROW1[s][:, 2 * NI + D:], act_table[bass.ds(e, 1)]).then_inc(row_loaded[s], 16)

            for t in range(T):
                s = t % 2
                if t == T - 1:
                    act.wait_ge(routed, 1)
                    act.wait_ge(slots_filled, 16 * 2 * T)
                    act.wait_ge(prm_stored, 16)
                    load_tokens(0, 0)
                wait(sgate_ready, t + 1)
                nc.scalar.activation(SIG[s][0:P], GC[s][0:P], ACT.Sigmoid, scale=SACT[:, 0:1]).then_inc(ssig_ready, 1)
                b = fill_of(("st", t))
                if t >= 2:
                    wait(vec_filled, RV.count(("so", t - 2)))
                nc.scalar.copy(TET[s].rearrange("p (k n) -> p k n", k=KI)[:, :, 0:P], b[:, 0:KI * P].rearrange("p (k n) -> p k n", k=KI))\
                    .then_inc(act_drained, 1)

            def take_tokens(b, s):
                act.wait_ge(xt_filled, b + 1)
                if not (isinstance(b, int) and b < 2):
                    act.wait_ge(h_filled, b)
                nc.scalar.copy(XGT[s], XT_BANK[s][:, :]).then_inc(xgt_ready, 1)

            def step(b, j, s):
                last = isinstance(b, int) and b >= BLOCKS
                if isinstance(b, int) and b == 0:
                    take_tokens(0, 0)
                if not last:
                    load_w2(b, s)
                if not (isinstance(b, int) and b == 0):
                    act.wait_ge(tt_filled, b)
                    if not (isinstance(b, int) and b < 3):
                        act.wait_ge(o_filled, b - 2)
                    nc.scalar.copy(TET[1 - s], TT_BANK[:, 0:NI]).then_inc(tet_ready, 1)
                if not last and not (isinstance(b, int) and b == BLOCKS - 1):
                    take_tokens(b + 1, 1 - s)
                if not last:
                    act.wait_ge(g_ready, b + 1)
                    nc.scalar.activation(SIG[s], GC[s], ACT.Sigmoid, scale=EACT[s][:, 0:1]).then_inc(sig_ready, 1)
                if not (isinstance(b, int) and b + 2 >= BLOCKS):
                    load_tokens(b + 2, s)

            act.wait_ge(vec_drained, RV.count(("so", T - 1)))
            load_tokens(1, 1)
            run_blocks(act, step)


        @block.vector
        def _(dve):
            seen = {}
            steps = [0]
            drained = [0]
            V = nc.vector

            def wait(s, n):
                if seen.get(s.name, 0) < n:
                    dve.wait_ge(s, n)
                    seen[s.name] = n

            def then(ins):
                steps[0] += 1
                ins.then_inc(vec_step, 1)
                dve.wait_ge(vec_step, steps[0])

            def fill_of(job):
                assert RV.at[job] == drained[0], (job, drained[0])
                drained[0] += 1
                wait(vec_filled, RV.count(job))
                return RV.bank(job)

            def stats(n, src, t):
                then(V.bn_stats(st[:, t, :], src[:, t, :]))
                V.bn_aggr(moments(n)[0][:, t, :], st[:, t, :]).then_inc(var_ready, 1)

            def normalize(n, src, dst, t, ready):
                m, r = moments(n)
                wait(std_ready, T * n + t + 1)
                then(V.reciprocal(r[:, t:t + 1], sd[:, t:t + 1]))
                V.tensor_scalar(dst[:, t, :], src[:, t, :], m[:, t, 0:1], r[:, t:t + 1], ALU.subtract, ALU.mult).then_inc(ready, 1)

            def from_column_form(tag, L, c):
                n0, n1 = FORMS[c][0] * P, FORMS[c][1] * P
                for k in (0, 2):
                    b = fill_of((tag, L, c, k))
                    if tag in ("y1", "y2"):
                        name = "ln1" if tag == "y1" else "ln2"
                        V.tensor_scalar(YT[:, k, n0:n1], b[:, 0:n1 - n0], col(name + "_g", L, k), col(name + "_b", L, k),
                                        ALU.mult, ALU.add).then_inc(vec_drained, 1)
                    else:
                        V.tensor_copy(YT[:, k, n0:n1], b[:, 0:n1 - n0]).then_inc(vec_drained, 1)

            def low_columns(tag, L, c):
                n0, n1 = FORMS[c][0] * P, FORMS[c][1] * P
                wait(col_high, 3 * col_form(tag, L) + c + 1)
                V.tensor_tensor(YLOW[:, :, n0:n1], YT[:, :, n0:n1], YHIGH[:, :, n0:n1].bitcast(F32), ALU.subtract)\
                    .then_inc(col_low, 1)

            def low_part(c):
                wait(w_high, c + 1)
                V.tensor_tensor(WLOW[:, c % WSLOTS, :, :], weight(c), WHIGH[:, c % WSLOTS, :, :].bitcast(F32), ALU.subtract)\
                    .then_inc(w_low, 1)

            V.memset(eps_ln[:, :], EPS_LN).then_inc(vec_step, 1)
            V.memset(neg1[:, :], -1.0).then_inc(vec_step, 1)
            V.memset(PROJ[:, :, :, :], 0.0).then_inc(proj_zeroed, 1)
            V.memset(halves[:, :, :], 0.0).then_inc(vec_step, 1)
            V.memset(V1[:, :, :, DH:DH + 1], 1.0).then_inc(vec_step, 1)
            steps[0] = 4
            dve.wait_ge(vec_step, 4)
            for h in range(H):
                r0 = DH * (h % 2)
                V.memset(halves[r0:r0 + DH, h // 2, h:h + 1], 0.5).then_inc(vec_step, 1)
            steps[0] = 4 + H

            wait(x_loaded, 16)
            for t in range(T):
                stats(0, Z, t)
            for t in range(T):
                normalize(0, Z, XN, t, xn_ready)
            b = fill_of(("cols",))
            V.tensor_copy(COLS[:, 0:n_cols], b[:, 0:n_cols]).then_inc(vec_drained, 1)
            wait(vec_drained, drained[0])
            c0 = col_at["bk", 0]
            V.tensor_scalar(COLS[:, c0:c0 + 2 * KD], COLS[:, c0:c0 + 2 * KD], QK_NORM, None, ALU.mult).then_inc(kcol_ready, 1)
            for t in range(T):
                wait(xn_ready, t + 1)
                stats(1, XN, t)
            for t in range(T):
                normalize(1, XN, Z, t, z_ready)
            for c in range(2):
                from_column_form("y1", 0, c)
                low_columns("y1", 0, c)

            wait(consts_ready, 1)
            then(V.tensor_copy(spare[:, :], spare_i[:, :]))
            def edge_same(g):
                b = fill_of(("keys", g))
                rows = b[0:P, 0:EG * P].rearrange("p (j q) -> p j q", j=EG)
                V.tensor_tensor(SAME[g % 2], rows, key[:, g * EG:(g + 1) * EG].unsqueeze(2).to_broadcast([P, EG, P]),
                                ALU.is_equal).then_inc(vec_drained, 1)
                wait(vec_drained, drained[0])
                then(V.tensor_tensor(SAMEL[g % 2], SAME[g % 2], lower[:, :].unsqueeze(1).to_broadcast([P, EG, P]), ALU.mult))
                V.tensor_reduce(before[:, g * EG:(g + 1) * EG], SAMEL[g % 2], AX_X, ALU.add).then_inc(vec_step, 1)
                steps[0] += 1

            def edge_take(g):
                b = fill_of(("sums", g))
                V.tensor_reduce(VC[:, g * EG:(g + 1) * EG, :], b[0:P, 0:EG * 3 * H].rearrange("p (j c h) -> p j h c", j=EG, c=3),
                                AX_X, ALU.add).then_inc(vec_drained, 1)

            for L in range(LAYERS):
                src = MX if L == 1 else XN
                dst = XN if L == GNN else MX
                if L == 0:
                    wait(w_low, 1)

                def take_q(m, c):
                    n0, n, skip = SPANS[c]
                    b = fill_of(("q", L, m, c))
                    for dst_q, r0, r1 in (((QT, 0, 2 * DH),) if L != GNN else ((QT, 0, DH), (QODD, DH, 2 * DH))):
                        ins = V.tensor_scalar(dst_q[r0:r1, m, n0 + skip:n0 + n], b[r0:r1, skip:n], col("bq", L, m)[r0:r1],
                                              QK_NORM if L != GNN else GNN_SCALE, ALU.add, ALU.mult)
                    ins.then_inc(vec_drained, 1)

                for m in range(KD):
                    take_q(m, 0)
                    if m == 1:
                        from_column_form("y1", L, 2)
                        low_columns("y1", L, 2)
                low_part(WPER * L + 1)
                for m in range(KD):
                    take_q(m, 1)
                if L == 0:
                    b = fill_of(("proj",))
                    wait(proj_zeroed, 1)
                    for c in range(2):
                        ins = V.tensor_copy(PROJ[64 * c:64 * c + 64, :, c, :], b[64 * c:64 * c + 64, :].rearrange("p (l m) -> p l m", l=2))
                    ins.then_inc(vec_drained, 1)
                wait(z_ready, z_count("y1", L, T))
                if L == GNN:
                    wait(rowb_again, 16 * 3)
                else:
                    wait(rowb_loaded, 16 * 6)
                resid = V.tensor_tensor(dst[:, :, :], src[:, :, :], ROWB[:, L % 2, 1, :].unsqueeze(1).to_broadcast([P, T, D]), ALU.add)
                resid.then_inc(vec_step, 1)
                steps[0] += 1
                resid_step = steps[0]
                low_part(WPER * L + 2)
                def find_pairs(dt, neg):
                    wait(pairw_loaded[dt % 2], 16 * (dt // 2 + 1))
                    then(V.tensor_reduce(neg, PAIRW[dt % 2], AX_X, ALU.max))
                    then(V.tensor_scalar(neg, neg, 0.0, MASK, ALU.is_equal, ALU.mult))

                if L == GNN:
                    wait(slots_zeroed, 16 * BLOCKS)
                    find_pairs(0, NEG0)
                for t in range(T):
                    b = fill_of(("v", L, t))
                    V.tensor_tensor(V1[:, t, :, 0:DH], b[0:P, :].rearrange("p (h d) -> p h d", h=H),
                                    ROWB[:, L % 2, 0, :].rearrange("p (h d) -> p h d", h=H), ALU.add).then_inc(vec_drained, 1)
                if L == 0:
                    wait(edges_loaded, 32)
                    V.tensor_copy(key[:, :], dst_i[:, :]).then_inc(vec_step, 1)
                    steps[0] += 1
                    then(V.tensor_copy(srcf[:, :], src_i[:, :]))
                    then(V.scalar_tensor_tensor(out=key[:, :], in0=key[:, :], scalar=float(N), in1=srcf[:, :], op0=ALU.mult, op1=ALU.add))
                    wait(attrs_loaded, 32)
                    then(V.tensor_tensor(EA[:, :, :], EA[:, :, :], EA2[:, :, :], ALU.add))
                    V.tensor_reduce(emax[:, :], EA[:, :, :].rearrange("p j h -> p h j"), AX_X, ALU.max).then_inc(edge_max_part, 1)
                if L != GNN:
                    for h in range(H):
                        wait(act_drained, RA.count(("kd", L, h // 2, T - 1)))
                        V.tensor_reduce(KM[:, h:h + 1], KP[:, h, :, :], mybir.AxisListType.XY, ALU.max).then_inc(kmax_part, 1)

                    for q in range(2):
                        for c in range(2):
                            n0, n1 = columns(c)
                            b = fill_of(("dgt", L, q, c))
                            V.tensor_copy(DGT[:, q, n0:n1], b[0:H, 0:n1 - n0]).then_inc(vec_drained, 1)
                    def q_max(hp):
                        for t in range(T):
                            job = ("qd", L, hp, t)
                            wait(act_filled, RA.count(job))
                            then(V.tensor_reduce(QM[:, 2 * hp:2 * hp + 2, t], RA.bank(job)[0:P, :].rearrange("p (c m) -> p c m", c=2),
                                                 AX_X, ALU.max))
                            V.scalar_tensor_tensor(out=NQ[:, 2 * hp:2 * hp + 2, t], in0=QM[:, 2 * hp:2 * hp + 2, t], scalar=-1.0,
                                                   in1=DG[:, t, 0, 2 * hp:2 * hp + 2], op0=ALU.mult, op1=ALU.subtract)\
                                .then_inc(qbias_ready, 1)

                    b = fill_of(("kmax", L))
                    V.tensor_reduce(KMH[:, :], b[0:H, 0:P], AX_X, ALU.max).then_inc(vec_drained, 1)
                    wait(vec_drained, drained[0])
                    V.tensor_scalar(KDIAG[:, :], ident[0:H, 0:H], KMH[:, 0:1], None, ALU.mult).then_inc(kdiag_ready, 1)
                    b = fill_of(("kmax_all", L))
                    V.tensor_copy(KMA[:, :], b[0:P, 0:H]).then_inc(vec_drained, 1)
                    b = fill_of(("diag", L))
                    V.tensor_copy(DG[:, :, :, :], b[0:P, 0:T * 2 * H].rearrange("p (t q h) -> p t q h", t=T, q=2)).then_inc(vec_drained, 1)
                    wait(vec_drained, drained[0])
                    V.scalar_tensor_tensor(out=NK[:, :, :], in0=DG[:, :, 1, :], scalar=-1.0,
                                           in1=KMA[:, :].unsqueeze(1).to_broadcast([P, T, H]),
                                           op0=ALU.mult, op1=ALU.subtract).then_inc(kbias_ready, 1)
                    q_max(0)

                    def take_o(h):
                        b = fill_of(("o", L, h))
                        o = b[0:P, 0:T * (DH + 1)].rearrange("p (t e) -> p t e", t=T)
                        then(V.reciprocal(REC[:, h % 2, :], o[:, :, DH]))
                        V.tensor_tensor(O[:, :, h * DH:(h + 1) * DH], o[:, :, 0:DH],
                                        REC[:, h % 2, :].unsqueeze(2).to_broadcast([P, T, DH]), ALU.mult).then_inc(vec_drained, 1)

                    low_part(WPER * L + 3)

                    def take_queries(h, i):
                        b = fill_of(("qt", L, h, i))
                        n = min(500, 2 * N - 500 * i)
                        V.tensor_scalar(QPT[h % 2][:, 500 * i:500 * i + n], b[:, 0:n], EPS_RF, None, ALU.add).then_inc(vec_drained, 1)

                    def key_features(h):
                        wait(kexp_done, H * L + h + 1)
                        V.tensor_scalar(KP[:, h, :, :], KP[:, h, :, :], EPS_RF, None, ALU.add).then_inc(kp_ready, 1)

                    for i in range(3):
                        take_queries(0, i)
                    for h in range(2):
                        key_features(h)
                    for h in range(H):
                        b = fill_of(("ctxT", L, h))
                        V.tensor_copy(CTXT[:, h % 2, :], b[0:DH + 1, 0:NF]).then_inc(vec_drained, 1)
                        if h:
                            take_o(h - 1)
                        if h + 1 < H:
                            take_queries(h + 1, 0)
                        b = fill_of(("ctx", L, h))
                        V.tensor_copy(CTX[:, h % 2, :, :], b[:, 0:2 * (DH + 1)].rearrange("p (m e) -> p m e", m=2)).then_inc(vec_drained, 1)
                        if h + 1 < H:
                            take_queries(h + 1, 1)
                            take_queries(h + 1, 2)
                        if h % 2 == 0 and h + 2 < H:
                            q_max(h // 2 + 1)
                        if h % 2 and h + 1 < H:
                            key_features(h + 1)
                            key_features(h + 2)
                        if L == 0 and h == 1:
                            wait(edge_max_all, 1)
                            V.tensor_tensor(EA[:, :, :], EA[:, :, :], emaxa[:, :].unsqueeze(1).to_broadcast([P, EB, H]), ALU.subtract)\
                                .then_inc(edge_sub_ready, 1)
                        if h in (3, 5):
                            low_part(WPER * L + (4 if h == 3 else 5))
                    take_o(H - 1)
                else:
                    for i in range(T * H + 3):
                        def mask_and_max(c):
                            n0, n1 = columns(c)
                            b = fill_of(("s", i, c))
                            V.tensor_tensor_reduce(out=TS[i % NTS][:, n0:n1], in0=b[0:P, 0:n1 - n0], in1=(NEG[dt % 2] if dt else NEG0)[:, n0:n1],
                                                   scale=1.0, scalar=-3e38, op0=ALU.add, op1=ALU.max,
                                                   accum_out=pairmax[:, i % NTS, c:c + 1]).then_inc(vec_drained, 1)

                        if 0 <= i - 3 < T * H:
                            j = i - 3
                            wait(p_ready, j + 1)
                            V.tensor_scalar(rden[:, j % NTS:j % NTS + 1], den[:, j % NTS:j % NTS + 1], 1e-37, None, ALU.max)\
                                .then_inc(den_ready, 1)
                        if i < T * H:
                            dt, h = divmod(i, H)
                            if i >= NTS:
                                wait(act_filled, RA.count(("pt", i - NTS, 1)))
                            if h:
                                mask_and_max(0)
                        if 0 <= i - 3 < T * H:
                            wait(den_ready, j + 1)
                            V.reciprocal(rden[:, j % NTS:j % NTS + 1], rden[:, j % NTS:j % NTS + 1]).then_inc(rden_ready, 1)
                        if i < T * H and h:
                            mask_and_max(1)
                        if 0 <= i - 2 < T * H:
                            j = i - 2
                            wait(sexp_done, j + 1)
                            V.tensor_tensor_reduce(out=TS[j % NTS], in0=TS[j % NTS], in1=PAIRW[(j // H) % 2][:, :, j % H], scale=1.0, scalar=0.0,
                                                   op0=ALU.mult, op1=ALU.add, accum_out=den[:, j % NTS:j % NTS + 1]).then_inc(p_ready, 1)
                        if i < T * H:
                            if h == 0:
                                if dt:
                                    find_pairs(dt, NEG[dt % 2])
                                mask_and_max(0)
                                mask_and_max(1)
                            wait(vec_drained, drained[0])
                            V.scalar_tensor_tensor(out=negmax[:, i % NTS:i % NTS + 1], in0=pairmax[:, i % NTS, 0:1],
                                                   scalar=pairmax[:, i % NTS, 1:2], in1=neg1[:, :], op0=ALU.max, op1=ALU.mult)\
                                .then_inc(smax_ready, 1)
                        if i in (1, 4, 12):
                            low_part(WPER * L + {1: 3, 4: 4, 12: 5}[i])
                    for j, t0, t1 in ((0, 0, T - 1), (1, T - 1, T)):
                        wait(agg_high, j + 1)
                        V.tensor_tensor(AGGLOW[:, :, t0 * P:t1 * P], AGG[:, :, t0 * P:t1 * P], AGGHIGH[:, :, t0 * P:t1 * P].bitcast(F32),
                                        ALU.subtract).then_inc(agg_low, 1)
                if L != GNN:
                    for c in range(3):
                        from_column_form("oT", L, c)
                        low_columns("oT", L, c)
                dve.wait_ge(vec_step, resid_step)
                if L == 0:
                    wait(edge_exp_ready, 1)
                    then(V.tensor_copy(EAP[:, :, 0, :], EA[:, :, :]))
                    then(V.tensor_tensor(EAR, EA[:, :, :], EAP[:, :, 0, :], ALU.subtract))
                    then(V.tensor_copy(EAP[:, :, 1, :], EAR))
                    V.tensor_tensor(EAP[:, :, 2, :], EAR, EAP[:, :, 1, :], ALU.subtract).then_inc(edge_parts_ready, 1)
                n = NORM_OF["y2", L]
                for t in range(T):
                    if t == T - 2:
                        from_column_form("y2", L, 0)
                        low_columns("y2", L, 0)
                    b = fill_of(("x1", L, t))
                    V.tensor_tensor(dst[:, t, :], b[0:P, :], dst[:, t, :], ALU.add).then_inc(vec_drained, 1)
                    wait(vec_drained, drained[0])
                    if t == T - 2:
                        from_column_form("y2", L, 1)
                        low_columns("y2", L, 1)
                    stats(n, dst, t)
                    normalize(n, dst, z_of("y2", L), t, z_ready)
                from_column_form("y2", L, 2)
                low_columns("y2", L, 2)
                wait(z_ready, z_count("y2", L, T))
                resid = V.tensor_tensor(dst[:, :, :], dst[:, :, :], ROWB[:, L % 2, 2, :].unsqueeze(1).to_broadcast([P, T, D]), ALU.add)
                resid.then_inc(vec_step, 1)
                steps[0] += 1
                if L == GNN:
                    dve.wait_ge(vec_step, steps[0])
                    then(V.tensor_tensor(dst[:, :, :], dst[:, :, :], MX[:, :, :], ALU.add))
                    wait(x_again, 16)
                    V.tensor_tensor(dst[:, :, :], dst[:, :, :], XAGAIN, ALU.add).then_inc(vec_step, 1)
                    steps[0] += 1
                resid_step = steps[0]
                if L == 0:
                    wait(prm_in, 32)
                    V.scalar_tensor_tensor(out=PRMT[:, 0:2], in0=PRM[:, 3:5], scalar=-1.0, in1=PRM[:, 3:5], op0=ALU.mult, op1=ALU.min).then_inc(prm_step_d, 1)
                    wait(prm_step_a, 2)
                    then(V.scalar_tensor_tensor(out=PRM[:, 3:5], in0=PRM[:, 3:5], scalar=0.0, in1=PRMT[:, 0:2], op0=ALU.max, op1=ALU.add))
                    then(V.memset(PRM[:, 7:8], 0.0))
                    V.tensor_scalar(PRM[:, 5:7], PRM[:, 3:5], -1.0, None, ALU.mult).then_inc(prm_done, 1)

                def scatter_rows():
                    dve.wait_ge(vec_step, steps[0])
                    then(V.tensor_scalar(before[:, :], before[:, :], 1.0, None, ALU.min))
                    then(V.scalar_tensor_tensor(out=srcf[:, :], in0=key[:, :], scalar=-1.0, in1=spare[:, 0:1].to_broadcast([P, EB]),
                                                op0=ALU.mult, op1=ALU.add))
                    then(V.tensor_tensor(srcf[:, :], srcf[:, :], before[:, :], ALU.mult))
                    then(V.tensor_tensor(srcf[:, :], srcf[:, :], key[:, :], ALU.add))
                    wait(vec_drained, drained[0])
                    V.tensor_copy(idx[:, :], srcf[:, :]).then_inc(idx_ready, 1)

                def take_x2(g):
                    following = ("y1", L + 1) if L + 1 < LAYERS else ("yf", 0)

                    def next_columns(c):
                        from_column_form(*following, c)
                        if following[0] == "y1":
                            low_columns(*following, c)

                    for t in range(T):
                        if g == 3 and t == T - 2:
                            next_columns(0)
                        b = fill_of(("x2", L, g, t))
                        if g:
                            wait(vec_drained, RV.count(("x2", L, g - 1, t)))
                        else:
                            dve.wait_ge(vec_step, resid_step)
                        V.tensor_tensor(dst[:, t, :], b[0:P, :], dst[:, t, :], ALU.add).then_inc(vec_drained, 1)
                        if g == 3 and t == T - 2:
                            wait(vec_drained, drained[0])
                            next_columns(1)
                        if g == 3 and L != 1:
                            wait(vec_drained, drained[0])
                            stats(NORM_OF[following], dst, t)
                            normalize(NORM_OF[following], dst, Z, t, z_ready)

                for f in range(FM):
                    if f in (8, 12):
                        take_x2(f // 4 - 2)
                    for c in {2: (6,), 8: (8,), 10: (9,), 12: (10,), 14: (11,)}.get(f, ()):
                        low_part(WPER * L + c)
                    if L == 0:
                        for g in range(5 * f // 4, 5 * (f + 1) // 4):
                            edge_same(g)
                            if g:
                                edge_take(g - 1)
                        if f == FM - 1:
                            edge_take(EB // EG - 1)
                            scatter_rows()
                    wait(hid_high, FM * L + f + 1)
                    V.tensor_tensor(HTLOW[:, f % 8, :], HT[:, f % 8, :], HTHIGH[:, f % 8, :].bitcast(F32), ALU.subtract).then_inc(hid_low, 1)
                    if f == 7:
                        low_part(WPER * L + 7)
                    if f == 9 and L == 1:
                        for t in range(T):
                            V.tensor_scalar(Z[:, t, :], XN[:, t, :], mv_x[:, t, 0:1], rstd_x[:, t:t + 1], ALU.subtract, ALU.mult)\
                                .then_inc(z_ready, 1)
                take_x2(2)
                if L + 1 < LAYERS:
                    low_part(WPER * (L + 1))
                take_x2(3)
            wait(count_ready, 1)
            then(V.tensor_copy(COUNT, COUNT_I))
            V.tensor_scalar(THRESH, COUNT[:, 0:5], float(BLOCK), None, ALU.mult).then_inc(vec_step, 1)
            steps[0] += 1
            then(V.tensor_tensor(UPTO, COUNT[:, 0:NE].unsqueeze(1).to_broadcast([P, NE, NE]),
                                 COUNT[:, 0:NE].unsqueeze(2).to_broadcast([P, NE, NE]), ALU.is_le))
            from_column_form("yf", 0, 2)
            for c in range(2):
                n0, n1 = columns(c)
                b = fill_of(("gateT", c))
                V.tensor_copy(LOGITT[:, n0:n1], b[0:NE, 0:n1 - n0]).then_inc(vec_drained, 1)
            b = fill_of(("gate",))
            wait(gate_loaded, 16 * 5)
            V.tensor_tensor(LOGIT, b[0:P, 0:T * NE].rearrange("p (t e) -> p t e", t=T),
                            GATEB.unsqueeze(1).to_broadcast([P, T, NE]), ALU.add).then_inc(vec_drained, 1)
            wait(vec_drained, drained[0])
            then(V.tensor_reduce(LMAX, LOGIT, AX_X, ALU.max))
            V.tensor_tensor(LOGIT, LOGIT, LMAX.unsqueeze(2).to_broadcast([P, T, NE]), ALU.subtract).then_inc(logits_ready, 1)

            def shared_gate(t):
                s = t % 2
                h0 = fill_of(("sh", t, 0))
                hb = HB[s][0:P]
                V.tensor_tensor(hb[:, 0:NI], h0[0:P, 0:NI], SB1[:, 0:NI], ALU.add).then_inc(vec_drained, 1)
                h1 = fill_of(("sh", t, 1))
                V.tensor_tensor(hb[:, NI:2 * NI], h1[0:P, 0:NI], SB1[:, NI:2 * NI], ALU.add).then_inc(vec_drained, 1)
                wait(vec_drained, drained[0])
                gu = hb.rearrange("p (n c) -> p n c", c=2)
                V.tensor_scalar(GC[s][0:P], gu[:, :, 0], SACT[:, 3:4], SACT[:, 5:6], ALU.min, ALU.max).then_inc(sgate_ready, 1)
                wait(sgate_ready, t + 1)
                then(V.tensor_scalar(UC[s][0:P], gu[:, :, 1], SACT[:, 4:5], SACT[:, 6:7], ALU.min, ALU.max))
                then(V.scalar_tensor_tensor(out=UC[s][0:P], in0=UC[s][0:P], scalar=SACT[:, 2:3], in1=GC[s][0:P], op0=ALU.add, op1=ALU.mult))

            def shared_te(t):
                s = t % 2
                wait(ssig_ready, t + 1)
                if t >= 2:
                    wait(act_filled, RA.count(("st", t - 2)))
                V.scalar_tensor_tensor(out=TE[s][0:P], in0=UC[s][0:P], scalar=SACT[:, 1:2], in1=SIG[s][0:P], op0=ALU.mult, op1=ALU.mult)\
                    .then_inc(ste_ready, 1)

            wait(ffn_w_loaded, 16 * 2)
            shared_gate(0)
            wait(gate_exp, 1)
            then(V.tensor_reduce(LSUM, LOGIT, AX_X, ALU.add))
            then(V.reciprocal(LSUM, LSUM))
            then(V.tensor_tensor(LOGIT, LOGIT, LSUM.unsqueeze(2).to_broadcast([P, T, NE]), ALU.mult))
            for t in range(T):
                V.max(TOP[:, t, :], LOGIT[:, t, :]).then_inc(vec_step, 1)
                steps[0] += 1
            dve.wait_ge(vec_step, steps[0])
            for t in range(T):
                V.max_index(TOPI[:, t, :], TOP[:, t, :], LOGIT[:, t, :]).then_inc(vec_step, 1)
                steps[0] += 1
            then(V.tensor_tensor(LSUM, TOP[:, :, 0], TOP[:, :, 1], ALU.add))
            then(V.reciprocal(LSUM, LSUM))
            then(V.tensor_tensor(CW, TOP[:, :, 0:2], LSUM.unsqueeze(2).to_broadcast([P, T, 2]), ALU.mult))
            then(V.tensor_copy(TOPF, TOPI[:, :, 0:2]))
            for t in range(T):
                V.tensor_tensor(PICK[:, t], COUNT[:, 0:NE].unsqueeze(1).to_broadcast([P, 2, NE]),
                                TOPF[:, t].unsqueeze(2).to_broadcast([P, 2, NE]), ALU.is_equal).then_inc(vec_step, 1)
                steps[0] += 1
            dve.wait_ge(vec_step, steps[0])
            V.tensor_tensor(PICKED, PICK[:, :, 0, :], PICK[:, :, 1, :], ALU.add).then_inc(picked_ready, 1)
            shared_gate(1)
            shared_te(0)
            b = fill_of(("rank",))
            V.tensor_copy(RANK, b[0:P, 0:(T + 1) * NE].rearrange("p (t e) -> p t e", t=T + 1)).then_inc(vec_drained, 1)
            wait(vec_drained, drained[0])
            c5 = CMP[:, 0:NE * 5].rearrange("p (e j) -> p e j", j=5)
            then(V.tensor_tensor(c5, RANK[:, T, :].unsqueeze(2).to_broadcast([P, NE, 5]), THRESH.unsqueeze(1).to_broadcast([P, NE, 5]), ALU.is_gt))
            then(V.tensor_reduce(NBLK, c5, AX_X, ALU.add))
            c16 = CMP[:, 0:NE * NE].rearrange("p (a b) -> p a b", a=NE)
            then(V.tensor_tensor(c16, NBLK.unsqueeze(1).to_broadcast([P, NE, NE]), UPTO, ALU.mult))
            then(V.tensor_reduce(UPBLK, c16, AX_X, ALU.add))
            then(V.tensor_tensor(BASE, UPBLK, NBLK, ALU.subtract))
            then(V.scalar_tensor_tensor(out=RANK[:, 0:T, :], in0=BASE.unsqueeze(1).to_broadcast([P, T, NE]), scalar=float(BLOCK),
                                        in1=RANK[:, 0:T, :], op0=ALU.mult, op1=ALU.add))
            for c in range(2):
                V.tensor_tensor(PICK[:, :, c, :], PICK[:, :, c, :], RANK[:, 0:T, :], ALU.mult).then_inc(vec_step, 1)
                steps[0] += 1
            dve.wait_ge(vec_step, steps[0])
            then(V.tensor_reduce(SLOTF, PICK.rearrange("p t c e -> p (t c) e"), AX_X, ALU.add))
            then(V.tensor_copy(SLOT, SLOTF))
            cb = CMP[:, 0:BLOCKS * NE].rearrange("p (a b) -> p a b", a=BLOCKS)
            then(V.tensor_tensor(cb, UPBLK.unsqueeze(1).to_broadcast([P, BLOCKS, NE]),
                                 COUNT.unsqueeze(2).to_broadcast([P, BLOCKS, NE]), ALU.is_le))
            then(V.tensor_reduce(BLKF, cb, AX_X, ALU.add))
            then(V.tensor_scalar(BLKF, BLKF, float(NE - 1), None, ALU.min))
            V.tensor_copy(BLKE, BLKF).then_inc(routed, 1)

            def block_tables():
                then(V.tensor_scalar(EVENS, COUNT[:, 0:NE // 2], 2.0, None, ALU.mult))
                ce = CMP[:, 0:BLOCKS * NE // 2].rearrange("p (a b) -> p a b", a=BLOCKS)
                then(V.tensor_tensor(ce, EVENS.unsqueeze(1).to_broadcast([P, BLOCKS, NE // 2]),
                                     BLKF.unsqueeze(2).to_broadcast([P, BLOCKS, NE // 2]), ALU.is_le))
                then(V.tensor_reduce(EVENF, ce, AX_X, ALU.add))
                then(V.tensor_scalar(BLKW[0], EVENF, 16.0, None, ALU.mult))
                then(V.scalar_tensor_tensor(out=ODDF, in0=BLKF, scalar=1.0, in1=EVENF, op0=ALU.add, op1=ALU.subtract))
                then(V.tensor_scalar(BLKW[1], ODDF, 1.0, 16.0, ALU.max, ALU.mult))
                then(V.scalar_tensor_tensor(out=ODDF, in0=ODDF, scalar=1.0, in1=EVENF, op0=ALU.add, op1=ALU.subtract))
                then(V.tensor_copy(BLKS, ODDF))
                for i, filled in enumerate((half_filled, h_filled)):
                    V.memset(TR[:, 980 + i:981 + i], 0.0).then_inc(filled, 1)
                V.tensor_scalar(PAST, UPBLK, 1.0, None, ALU.add).then_inc(routed, 1)

            then(V.tensor_tensor(MX[:, :, :], XN[:, :, :], SB2.unsqueeze(1).to_broadcast([P, T, D]), ALU.add))
            for t in range(T):
                if t and t + 1 < T:
                    shared_gate(t + 1)
                if t + 1 < T:
                    shared_te(t + 1)
                if t == 1:
                    block_tables()
                b = fill_of(("so", t))
                V.tensor_tensor(MX[:, t, :], b[0:P, :], MX[:, t, :], ALU.add).then_inc(vec_drained, 1)

            def step(b, j, s):
                last = isinstance(b, int) and b >= BLOCKS
                if not last:
                    dve.wait_ge(h_filled, b + 2)
                    dve.wait_ge(rows_spread, b + 1)
                    V.tensor_tensor(HB[s][:, 0:NI], H_BANK[s][0][:, 0:NI], EB1[s][:, 0:NI], ALU.add)
                    V.tensor_tensor(HB[s][:, NI:2 * NI], H_BANK[s][1][:, 0:NI], EB1[s][:, NI:2 * NI], ALU.add).then_inc(h_drained, 1)
                    dve.wait_ge(h_drained, b + 1)
                    gu = HB[s].rearrange("p (n c) -> p n c", c=2)
                    V.tensor_scalar(GC[s], gu[:, :, 0], EACT[s][:, 3:4], EACT[s][:, 5:6], ALU.min, ALU.max).then_inc(g_ready, 1)
                    V.tensor_scalar(UC[s], gu[:, :, 1], EACT[s][:, 4:5], EACT[s][:, 6:7], ALU.min, ALU.max).then_inc(u_ready, 1)
                    dve.wait_ge(g_ready, b + 1)
                    dve.wait_ge(u_ready, b + 1)
                    V.scalar_tensor_tensor(out=UC[s], in0=UC[s], scalar=EACT[s][:, 2:3], in1=GC[s], op0=ALU.add, op1=ALU.mult).then_inc(gu_ready, 1)
                if not (isinstance(b, int) and b == 0):
                    q = 1 - s
                    dve.wait_ge(o_filled, b)
                    if not (isinstance(b, int) and b < 3):
                        dve.wait_ge(stored[q], 16 * (j + s - 1))
                    V.tensor_tensor(OG[q], O_BANK[:, :], EB2[q], ALU.add).then_inc(o_drained, 1)
                if not last:
                    dve.wait_ge(sig_ready, b + 1)
                    dve.wait_ge(gu_ready, b + 1)
                    if not (isinstance(b, int) and b < 2):
                        dve.wait_ge(tt_filled, b - 1)
                    V.scalar_tensor_tensor(out=TE[s], in0=UC[s], scalar=EACT[s][:, 1:2], in1=SIG[s], op0=ALU.mult, op1=ALU.mult).then_inc(te_ready, 1)

            run_blocks(dve, step)
            for t in range(T):
                dve.wait_ge(gathered[t], 16 * 2)
                then(V.scalar_tensor_tensor(out=MX[:, t, :], in0=GOT[:, t, 0, :], scalar=CW[:, t, 0:1], in1=MX[:, t, :], op0=ALU.mult, op1=ALU.add))
                V.scalar_tensor_tensor(out=MX[:, t, :], in0=GOT[:, t, 1, :], scalar=CW[:, t, 1:2], in1=MX[:, t, :], op0=ALU.mult, op1=ALU.add)\
                    .then_inc(y_ready, 1)


_OUTS = [((625, 512), "float32")]


def kernel(**inputs):
    import numpy as _np
    import concourse.bacc as _bacc
    from concourse import mybir as _mybir
    from concourse.bass_utils import run_bass_kernel_spmd as _run

    nc = _bacc.Bacc("TRN2", target_bir_lowering=False, num_devices=1)
    arrays, aps = {}, {}
    for name in inputs:
        a = _np.ascontiguousarray(inputs[name])
        arrays[f"in_{name}_dram"] = a
        aps[name] = nc.dram_tensor(f"in_{name}_dram", a.shape, _mybir.dt.from_np(a.dtype), kind="ExternalInput").ap()
    outs = [nc.dram_tensor(f"out_{i}_dram", shape, _mybir.dt.from_np(_np.dtype(dtype)), kind="ExternalOutput").ap()
            for i, (shape, dtype) in enumerate(_OUTS)]
    gps_layer(nc, aps, *outs)
    r = _run(nc, [arrays], core_ids=[0])
    got = tuple(r.results[0][f"out_{i}_dram"] for i in range(len(_OUTS)))
    return got[0]
```
